# Optimizing a Trainium2 kernel written in Bass

```python
import numpy as np
import jax
import jax.numpy as jnp

def _softmax(x, axis=-1):
    return jax.nn.softmax(x, axis=axis)

def _gelu(x):
    return jax.nn.gelu(x, approximate=True)

def _silu(x):
    return jax.nn.silu(x)

def _sigmoid(x):
    return jax.nn.sigmoid(x)

def _layernorm(x, axis=-1, eps=1e-05):
    m = jnp.mean(x, axis=axis, keepdims=True)
    v = jnp.var(x, axis=axis, keepdims=True)
    return (x - m) / jnp.sqrt(v + eps)

def _scatter_add(tgt, idx, src, axis=0):
    return tgt.at[idx].add(src)

def _segment_sum(src, seg, n):
    return jax.ops.segment_sum(src, seg, n)
kernel_name = 'mk_decoder_preln_d2_seqx_r8_149ebb'

def setup_inputs(seed: int=0):
    np.random.seed(seed)
    _w = jnp.asarray

    def _rec_inputs():
        import jax
        import jax.numpy as jnp
        _rk = jax.random.key(seed)
        x = 7.22e-05 + 1 * jax.random.normal(jax.random.fold_in(_rk, 1), (16, 128, 256), jnp.float32)
        _lenS = 128 - jax.random.randint(jax.random.fold_in(_rk, 7), (16,), 0, max(1, 128 // 4) + 1, jnp.int32)
        _lenS2 = 128 - jax.random.randint(jax.random.fold_in(_rk, 8), (16,), 0, max(1, 128 // 4) + 1, jnp.int32)
        _ctx_512P = jax.random.normal(jax.random.fold_in(_rk, 11), (16, 16, 64), jnp.float32)
        _ctx_512c = jax.random.dirichlet(jax.random.fold_in(_rk, 511), 0.3 * jnp.ones((16,), jnp.float32), (16, 128))
        _ctx_512t = jnp.einsum('bsk,bkd->bsd', _ctx_512c, _ctx_512P)
        _ctx_512t = _ctx_512t * jax.lax.rsqrt(jnp.mean(jnp.square(_ctx_512t)) + 1e-12) * 0.953939
        ctx_512 = -0.000514642 + 1.00011 * (_ctx_512t + 0.3 * jax.random.normal(jax.random.fold_in(_rk, 611), (16, 128, 64), jnp.float32))
        return (x, ctx_512)
    x, ctx_512 = _rec_inputs()

    def _L0_attn_setup():
        import jax, jax.numpy as jnp
        import numpy as np
        import math
        H = 256
        B = 4
        T = 256
        LAYER_ID = 0
        N_LAYERS = 24

        def _init_params(key):
            ratio_0_to_1 = LAYER_ID / (N_LAYERS - 1)
            ratio_1_to_0 = 1.0 - LAYER_ID / N_LAYERS
            d = jnp.arange(H, dtype=jnp.float32) / max(H - 1, 1)
            tmk = jnp.power(d, ratio_1_to_0).reshape(1, 1, H)
            tmv = jnp.clip(jnp.power(d, ratio_1_to_0) + 0.3 * ratio_0_to_1, 0.0, 1.0).reshape(1, 1, H)
            tmr = jnp.power(d, 0.5 * ratio_1_to_0).reshape(1, 1, H)
            frac = jnp.arange(H, dtype=jnp.float32) / max(H - 1, 1)
            time_decay = -5.0 + 8.0 * jnp.power(frac, 0.7 + 1.3 * ratio_0_to_1)
            zigzag = ((jnp.arange(H) + 1) % 3 - 1).astype(jnp.float32) * 0.5
            time_first = jnp.full((H,), math.log(0.3), dtype=jnp.float32) + zigzag
            ks = jax.random.split(key, 4)
            lim = math.sqrt(6.0 / (H + H))
            Wk = jax.random.uniform(ks[0], (H, H), jnp.float32, -lim, lim)
            Wv = jax.random.uniform(ks[1], (H, H), jnp.float32, -lim, lim)
            Wr = jax.random.uniform(ks[2], (H, H), jnp.float32, -lim, lim)
            Wo = jax.random.normal(ks[3], (H, H), jnp.float32) * (0.02 / math.sqrt(N_LAYERS))
            z = jnp.zeros((H,), jnp.float32)
            return dict(Wk=Wk, bk=z, Wv=Wv, bv=z, Wr=Wr, br=z, Wo=Wo, bo=z, tmk=tmk, tmv=tmv, tmr=tmr, time_decay=time_decay, time_first=time_first)

        def _wkv_scan(k, v, time_decay, time_first):
            decay = -jnp.exp(time_decay)
            bonus = time_first
            b, t, h = k.shape
            aa0 = jnp.zeros((b, h), jnp.float32)
            bb0 = jnp.zeros((b, h), jnp.float32)
            pp0 = jnp.full((b, h), -1e+30, jnp.float32)

            def step(carry, kv):
                aa, bb, pp = carry
                kt, vt = kv
                ww = bonus + kt
                p = jnp.maximum(pp, ww)
                e1 = jnp.exp(pp - p)
                e2 = jnp.exp(ww - p)
                out = (e1 * aa + e2 * vt) / (e1 * bb + e2)
                ww2 = pp + decay
                p2 = jnp.maximum(ww2, kt)
                e1 = jnp.exp(ww2 - p2)
                e2 = jnp.exp(kt - p2)
                return ((e1 * aa + e2 * vt, e1 * bb + e2, p2), out)
            kT = jnp.swapaxes(k, 0, 1)
            vT = jnp.swapaxes(v, 0, 1)
            _, outs = jax.lax.scan(step, (aa0, bb0, pp0), (kT, vT))
            return jnp.swapaxes(outs, 0, 1)
        key = jax.random.key(seed)
        kx, kp = jax.random.split(key)
        inp = {'x': jax.random.normal(kx, (B, T, H), jnp.float32)}
        inp.update(_init_params(kp))
        return inp
    _L0_attn_all = _L0_attn_setup()
    _L0_attn_in = {k: v for k, v in _L0_attn_all.items() if k in ('Wk', 'bk', 'Wv', 'bv', 'Wr', 'br', 'Wo', 'bo', 'tmk', 'tmv', 'tmr', 'time_decay', 'time_first')}
    del _L0_attn_all

    def _L0_xattn_setup():
        import jax, jax.numpy as jnp
        import numpy as np
        import math
        NUM_Q_HEADS = 32
        NUM_KV_HEADS = 8
        key = jax.random.key(seed)
        k1, k2, k3 = jax.random.split(key, 3)
        B, S, E = (2, 256, 256)
        kv_E = NUM_KV_HEADS * (E // NUM_Q_HEADS)
        q = jax.random.normal(k1, (B, S, E), dtype=jnp.float32)
        k = jax.random.normal(k2, (B, S, kv_E), dtype=jnp.float32)
        v = jax.random.normal(k3, (B, S, kv_E), dtype=jnp.float32)
        return {'q': q, 'k': k, 'v': v}
    _L0_xattn_all = _L0_xattn_setup()
    _L0_xattn_in = {k: v for k, v in _L0_xattn_all.items() if k in ()}
    del _L0_xattn_all

    def _L0_ffn_setup():
        import jax, jax.numpy as jnp
        import numpy as np
        H = 256
        I = 1024
        MI = 128
        E = 8
        K = 2
        B, S = (2, 128)
        EPS = 1e-06
        ROOT = H ** (-0.5)

        def _rms(x, w=None, eps=EPS):
            ms = jnp.mean(x * x, axis=-1, keepdims=True) + eps
            y = x * jax.lax.rsqrt(ms)
            return y * w if w is not None else y

        def _gelu_tanh(x):
            return jax.nn.gelu(x, approximate=True)
        key = jax.random.key(seed)
        ks = jax.random.split(key, 10)
        s = 0.02
        return {'hidden_states': jax.random.normal(ks[0], (B, S, H), jnp.float32), 'rn_pre1': jnp.ones((H,), jnp.float32), 'rn_pre2': jnp.ones((H,), jnp.float32), 'rn_post1': jnp.ones((H,), jnp.float32), 'rn_post2': jnp.ones((H,), jnp.float32), 'rn_post': jnp.ones((H,), jnp.float32), 'w_gate': jax.random.normal(ks[1], (H, I), jnp.float32) * s, 'w_up': jax.random.normal(ks[2], (H, I), jnp.float32) * s, 'w_down': jax.random.normal(ks[3], (I, H), jnp.float32) * s, 'router_w': jax.random.normal(ks[4], (H, E), jnp.float32) * s, 'router_scale': jnp.ones((H,), jnp.float32), 'per_expert_scale': jnp.ones((E,), jnp.float32), 'we_gate': jax.random.normal(ks[5], (E, H, MI), jnp.float32) * s, 'we_up': jax.random.normal(ks[6], (E, H, MI), jnp.float32) * s, 'we_down': jax.random.normal(ks[7], (E, MI, H), jnp.float32) * s}
    _L0_ffn_all = _L0_ffn_setup()
    _L0_ffn_in = {k: v for k, v in _L0_ffn_all.items() if k in ('rn_pre1', 'rn_pre2', 'rn_post1', 'rn_post2', 'rn_post', 'w_gate', 'w_up', 'w_down', 'router_w', 'router_scale', 'per_expert_scale', 'we_gate', 'we_up', 'we_down')}
    del _L0_ffn_all

    def _L1_attn_setup():
        import jax, jax.numpy as jnp
        import numpy as np
        HEADS, KV_HEADS, HEAD_DIM = (16, 4, 128)
        WINDOW, ROPE_THETA, EPS = (64, 10000.0, 1e-06)

        def _rms_norm(x, w):
            xf = x.astype(jnp.float32)
            y = xf * jax.lax.rsqrt(jnp.mean(xf * xf, axis=-1, keepdims=True) + EPS)
            return (y * (1.0 + w.astype(jnp.float32))).astype(x.dtype)

        def _rope_cos_sin(T, dtype):
            inv_freq = 1.0 / ROPE_THETA ** (jnp.arange(0, HEAD_DIM, 2, dtype=jnp.float32) / HEAD_DIM)
            pos = jnp.arange(T, dtype=jnp.float32)
            freqs = pos[:, None] * inv_freq[None, :]
            emb = jnp.concatenate([freqs, freqs], axis=-1)
            return (emb.astype(dtype), emb)

        def _rotate_half(x):
            x1, x2 = jnp.split(x, 2, axis=-1)
            return jnp.concatenate([-x2, x1], axis=-1)
        key = jax.random.key(seed)
        ks = jax.random.split(key, 7)
        B, T, D = (2, 256, 256)
        s = lambda k, shape, fan: jax.random.normal(k, shape, jnp.float32) * fan ** (-0.5)
        return {'x': jax.random.normal(ks[0], (B, T, D), jnp.float32), 'Wq': s(ks[1], (HEADS * HEAD_DIM, D), D), 'Wk': s(ks[2], (KV_HEADS * HEAD_DIM, D), D), 'Wv': s(ks[3], (KV_HEADS * HEAD_DIM, D), D), 'Wo': s(ks[4], (D, HEADS * HEAD_DIM), HEADS * HEAD_DIM), 'qn_w': jax.random.normal(ks[5], (HEAD_DIM,), jnp.float32) * 0.02, 'kn_w': jax.random.normal(ks[6], (HEAD_DIM,), jnp.float32) * 0.02}
    _L1_attn_all = _L1_attn_setup()
    _L1_attn_in = {k: v for k, v in _L1_attn_all.items() if k in ('Wq', 'Wk', 'Wv', 'Wo', 'qn_w', 'kn_w')}
    del _L1_attn_all

    def _L1_xattn_setup():
        import jax, jax.numpy as jnp
        import numpy as np
        B, S, H, NH, L = (2, 256, 256, 16, 64)
        HD = H // NH
        key = jax.random.key(seed)
        k1, k2, k3, k4, k5 = jax.random.split(key, 5)
        scale = 0.02
        return {'q': jax.random.normal(k1, (B, S, H), dtype=jnp.float32), 'latent_kv': jax.random.normal(k2, (B, S, L), dtype=jnp.float32), 'Wq': jax.random.normal(k3, (H, H), dtype=jnp.float32) * scale, 'Wkv_expand': jax.random.normal(k4, (2 * H, L), dtype=jnp.float32) * scale, 'Wout': jax.random.normal(k5, (H, H), dtype=jnp.float32) * scale}
    _L1_xattn_all = _L1_xattn_setup()
    _L1_xattn_in = {k: v for k, v in _L1_xattn_all.items() if k in ('Wq', 'Wkv_expand', 'Wout')}
    del _L1_xattn_all

    def _L1_ffn_setup():
        import jax, jax.numpy as jnp
        import numpy as np
        DIM_IN = 256
        DIM_HIDDEN = 1024
        key = jax.random.key(seed)
        k_x, k_g, k_u, k_d = jax.random.split(key, 4)
        s_in = 1.0 / np.sqrt(DIM_IN)
        s_hid = 1.0 / np.sqrt(DIM_HIDDEN)
        x = jax.random.normal(k_x, (4, 256, DIM_IN), dtype=jnp.float32)
        w_gate = jax.random.uniform(k_g, (DIM_HIDDEN, DIM_IN), jnp.float32, -s_in, s_in)
        w_up = jax.random.uniform(k_u, (DIM_HIDDEN, DIM_IN), jnp.float32, -s_in, s_in)
        w_down = jax.random.uniform(k_d, (DIM_IN, DIM_HIDDEN), jnp.float32, -s_hid, s_hid)
        return {'x': x, 'w_gate': w_gate, 'w_up': w_up, 'w_down': w_down}
    _L1_ffn_all = _L1_ffn_setup()
    _L1_ffn_in = {k: v for k, v in _L1_ffn_all.items() if k in ('w_gate', 'w_up', 'w_down')}
    del _L1_ffn_all
    return {'x': x, 'ctx_512': ctx_512, 'L0_attn_Wk': _L0_attn_in['Wk'], 'L0_attn_bk': _L0_attn_in['bk'], 'L0_attn_Wv': _L0_attn_in['Wv'], 'L0_attn_bv': _L0_attn_in['bv'], 'L0_attn_Wr': _L0_attn_in['Wr'], 'L0_attn_br': _L0_attn_in['br'], 'L0_attn_Wo': _L0_attn_in['Wo'], 'L0_attn_bo': _L0_attn_in['bo'], 'L0_attn_tmk': _L0_attn_in['tmk'], 'L0_attn_tmv': _L0_attn_in['tmv'], 'L0_attn_tmr': _L0_attn_in['tmr'], 'L0_attn_time_decay': _L0_attn_in['time_decay'], 'L0_attn_time_first': _L0_attn_in['time_first'], 'L0_ffn_rn_pre1': _L0_ffn_in['rn_pre1'], 'L0_ffn_rn_pre2': _L0_ffn_in['rn_pre2'], 'L0_ffn_rn_post1': _L0_ffn_in['rn_post1'], 'L0_ffn_rn_post2': _L0_ffn_in['rn_post2'], 'L0_ffn_rn_post': _L0_ffn_in['rn_post'], 'L0_ffn_w_gate': _L0_ffn_in['w_gate'], 'L0_ffn_w_up': _L0_ffn_in['w_up'], 'L0_ffn_w_down': _L0_ffn_in['w_down'], 'L0_ffn_router_w': _L0_ffn_in['router_w'], 'L0_ffn_router_scale': _L0_ffn_in['router_scale'], 'L0_ffn_per_expert_scale': _L0_ffn_in['per_expert_scale'], 'L0_ffn_we_gate': _L0_ffn_in['we_gate'], 'L0_ffn_we_up': _L0_ffn_in['we_up'], 'L0_ffn_we_down': _L0_ffn_in['we_down'], 'L1_attn_Wq': _L1_attn_in['Wq'], 'L1_attn_Wk': _L1_attn_in['Wk'], 'L1_attn_Wv': _L1_attn_in['Wv'], 'L1_attn_Wo': _L1_attn_in['Wo'], 'L1_attn_qn_w': _L1_attn_in['qn_w'], 'L1_attn_kn_w': _L1_attn_in['kn_w'], 'L1_xattn_Wq': _L1_xattn_in['Wq'], 'L1_xattn_Wkv_expand': _L1_xattn_in['Wkv_expand'], 'L1_xattn_Wout': _L1_xattn_in['Wout'], 'L1_ffn_w_gate': _L1_ffn_in['w_gate'], 'L1_ffn_w_up': _L1_ffn_in['w_up'], 'L1_ffn_w_down': _L1_ffn_in['w_down']}

def reference(x, ctx_512, L0_attn_Wk, L0_attn_bk, L0_attn_Wv, L0_attn_bv, L0_attn_Wr, L0_attn_br, L0_attn_Wo, L0_attn_bo, L0_attn_tmk, L0_attn_tmv, L0_attn_tmr, L0_attn_time_decay, L0_attn_time_first, L0_ffn_rn_pre1, L0_ffn_rn_pre2, L0_ffn_rn_post1, L0_ffn_rn_post2, L0_ffn_rn_post, L0_ffn_w_gate, L0_ffn_w_up, L0_ffn_w_down, L0_ffn_router_w, L0_ffn_router_scale, L0_ffn_per_expert_scale, L0_ffn_we_gate, L0_ffn_we_up, L0_ffn_we_down, L1_attn_Wq, L1_attn_Wk, L1_attn_Wv, L1_attn_Wo, L1_attn_qn_w, L1_attn_kn_w, L1_xattn_Wq, L1_xattn_Wkv_expand, L1_xattn_Wout, L1_ffn_w_gate, L1_ffn_w_up, L1_ffn_w_down):
    import jax
    import jax.numpy as jnp

    def _L0_attn_ref(x, Wk, bk, Wv, bv, Wr, br, Wo, bo, tmk, tmv, tmr, time_decay, time_first):
        import jax, jax.numpy as jnp
        import numpy as np
        import math
        H = 256
        B = 4
        T = 256
        LAYER_ID = 0
        N_LAYERS = 24

        def _init_params(key):
            ratio_0_to_1 = LAYER_ID / (N_LAYERS - 1)
            ratio_1_to_0 = 1.0 - LAYER_ID / N_LAYERS
            d = jnp.arange(H, dtype=jnp.float32) / max(H - 1, 1)
            tmk = jnp.power(d, ratio_1_to_0).reshape(1, 1, H)
            tmv = jnp.clip(jnp.power(d, ratio_1_to_0) + 0.3 * ratio_0_to_1, 0.0, 1.0).reshape(1, 1, H)
            tmr = jnp.power(d, 0.5 * ratio_1_to_0).reshape(1, 1, H)
            frac = jnp.arange(H, dtype=jnp.float32) / max(H - 1, 1)
            time_decay = -5.0 + 8.0 * jnp.power(frac, 0.7 + 1.3 * ratio_0_to_1)
            zigzag = ((jnp.arange(H) + 1) % 3 - 1).astype(jnp.float32) * 0.5
            time_first = jnp.full((H,), math.log(0.3), dtype=jnp.float32) + zigzag
            ks = jax.random.split(key, 4)
            lim = math.sqrt(6.0 / (H + H))
            Wk = jax.random.uniform(ks[0], (H, H), jnp.float32, -lim, lim)
            Wv = jax.random.uniform(ks[1], (H, H), jnp.float32, -lim, lim)
            Wr = jax.random.uniform(ks[2], (H, H), jnp.float32, -lim, lim)
            Wo = jax.random.normal(ks[3], (H, H), jnp.float32) * (0.02 / math.sqrt(N_LAYERS))
            z = jnp.zeros((H,), jnp.float32)
            return dict(Wk=Wk, bk=z, Wv=Wv, bv=z, Wr=Wr, br=z, Wo=Wo, bo=z, tmk=tmk, tmv=tmv, tmr=tmr, time_decay=time_decay, time_first=time_first)

        def _wkv_scan(k, v, time_decay, time_first):
            decay = -jnp.exp(time_decay)
            bonus = time_first
            b, t, h = k.shape
            aa0 = jnp.zeros((b, h), jnp.float32)
            bb0 = jnp.zeros((b, h), jnp.float32)
            pp0 = jnp.full((b, h), -1e+30, jnp.float32)

            def step(carry, kv):
                aa, bb, pp = carry
                kt, vt = kv
                ww = bonus + kt
                p = jnp.maximum(pp, ww)
                e1 = jnp.exp(pp - p)
                e2 = jnp.exp(ww - p)
                out = (e1 * aa + e2 * vt) / (e1 * bb + e2)
                ww2 = pp + decay
                p2 = jnp.maximum(ww2, kt)
                e1 = jnp.exp(ww2 - p2)
                e2 = jnp.exp(kt - p2)
                return ((e1 * aa + e2 * vt, e1 * bb + e2, p2), out)
            kT = jnp.swapaxes(k, 0, 1)
            vT = jnp.swapaxes(v, 0, 1)
            _, outs = jax.lax.scan(step, (aa0, bb0, pp0), (kT, vT))
            return jnp.swapaxes(outs, 0, 1)
        x_prev = jnp.concatenate([jnp.zeros_like(x[:, :1, :]), x[:, :-1, :]], axis=1)
        xk = x_prev + (x - x_prev) * tmk
        xv = x_prev + (x - x_prev) * tmv
        xr = x_prev + (x - x_prev) * tmr
        k = jnp.einsum('bth,oh->bto', xk, Wk) + bk
        v = jnp.einsum('bth,oh->bto', xv, Wv) + bv
        r = jnp.einsum('bth,oh->bto', xr, Wr) + br
        wkv = _wkv_scan(k, v, time_decay, time_first)
        rwkv = jax.nn.sigmoid(r) * wkv
        out = jnp.einsum('bth,oh->bto', rwkv, Wo) + bo
        return out

    def _L0_xattn_ref(q, k, v):
        import jax, jax.numpy as jnp
        import numpy as np
        import math
        NUM_Q_HEADS = 32
        NUM_KV_HEADS = 8
        B, S, E = q.shape
        H, KV = (NUM_Q_HEADS, NUM_KV_HEADS)
        D = E // H
        G = H // KV
        scale = math.sqrt(D)
        qh = q.reshape(B, S, KV, G, D).transpose(0, 2, 3, 1, 4)
        kh = k.reshape(B, S, KV, D).transpose(0, 2, 1, 3)
        vh = v.reshape(B, S, KV, D).transpose(0, 2, 1, 3)
        scores = jnp.einsum('bkgsd,bktd->bkgst', qh, kh) / scale
        weights = jax.nn.softmax(scores, axis=-1)
        out = jnp.einsum('bkgst,bktd->bkgsd', weights, vh)
        return out.transpose(0, 3, 1, 2, 4).reshape(B, S, E)

    def _L0_ffn_ref(hidden_states, rn_pre1, rn_pre2, rn_post1, rn_post2, rn_post, w_gate, w_up, w_down, router_w, router_scale, per_expert_scale, we_gate, we_up, we_down):
        import jax, jax.numpy as jnp
        import numpy as np
        H = 256
        I = 1024
        MI = 128
        E = 8
        K = 2
        B, S = (2, 128)
        EPS = 1e-06
        ROOT = H ** (-0.5)

        def _rms(x, w=None, eps=EPS):
            ms = jnp.mean(x * x, axis=-1, keepdims=True) + eps
            y = x * jax.lax.rsqrt(ms)
            return y * w if w is not None else y

        def _gelu_tanh(x):
            return jax.nn.gelu(x, approximate=True)
        b, s, h = hidden_states.shape
        T = b * s
        dense_in = _rms(hidden_states, rn_pre1)
        dense_out = _gelu_tanh(dense_in @ w_gate) * (dense_in @ w_up) @ w_down
        dense_out = _rms(dense_out, rn_post1)
        x = hidden_states.reshape(T, h)
        xr = _rms(x) * router_scale * ROOT
        router_logits = xr @ router_w
        probs = jax.nn.softmax(router_logits, axis=-1)
        top_w, top_i = jax.lax.top_k(probs, K)
        top_w = top_w / jnp.sum(top_w, axis=-1, keepdims=True)
        top_w = top_w * per_expert_scale[top_i]
        aff = jnp.zeros((T, E), x.dtype).at[jnp.arange(T)[:, None], top_i].set(top_w)
        moe_in = _rms(hidden_states, rn_pre2).reshape(T, h)
        g = jnp.einsum('th,ehm->tem', moe_in, we_gate)
        u = jnp.einsum('th,ehm->tem', moe_in, we_up)
        eo = jnp.einsum('tem,emh->teh', _gelu_tanh(g) * u, we_down)
        moe_out = jnp.einsum('te,teh->th', aff, eo).reshape(b, s, h)
        moe_out = _rms(moe_out, rn_post2)
        return _rms(dense_out + moe_out, rn_post)

    def _L1_attn_ref(x, Wq, Wk, Wv, Wo, qn_w, kn_w):
        import jax, jax.numpy as jnp
        import numpy as np
        HEADS, KV_HEADS, HEAD_DIM = (16, 4, 128)
        WINDOW, ROPE_THETA, EPS = (64, 10000.0, 1e-06)

        def _rms_norm(x, w):
            xf = x.astype(jnp.float32)
            y = xf * jax.lax.rsqrt(jnp.mean(xf * xf, axis=-1, keepdims=True) + EPS)
            return (y * (1.0 + w.astype(jnp.float32))).astype(x.dtype)

        def _rope_cos_sin(T, dtype):
            inv_freq = 1.0 / ROPE_THETA ** (jnp.arange(0, HEAD_DIM, 2, dtype=jnp.float32) / HEAD_DIM)
            pos = jnp.arange(T, dtype=jnp.float32)
            freqs = pos[:, None] * inv_freq[None, :]
            emb = jnp.concatenate([freqs, freqs], axis=-1)
            return (emb.astype(dtype), emb)

        def _rotate_half(x):
            x1, x2 = jnp.split(x, 2, axis=-1)
            return jnp.concatenate([-x2, x1], axis=-1)
        B, T, D = x.shape
        H, Hkv, Dh = (HEADS, KV_HEADS, HEAD_DIM)
        G = H // Hkv
        q = (x @ Wq.T).reshape(B, T, H, Dh).transpose(0, 2, 1, 3)
        k = (x @ Wk.T).reshape(B, T, Hkv, Dh).transpose(0, 2, 1, 3)
        v = (x @ Wv.T).reshape(B, T, Hkv, Dh).transpose(0, 2, 1, 3)
        q = _rms_norm(q, qn_w)
        k = _rms_norm(k, kn_w)
        emb_c, emb_f = _rope_cos_sin(T, x.dtype)
        cos = jnp.cos(emb_f).astype(x.dtype)[None, None]
        sin = jnp.sin(emb_f).astype(x.dtype)[None, None]
        q = q * cos + _rotate_half(q) * sin
        k = k * cos + _rotate_half(k) * sin
        q = q * Dh ** (-0.5)
        qg = q.reshape(B, Hkv, G, T, Dh)
        scores = jnp.einsum('bhgtd,bhkd->bhgtk', qg.astype(jnp.float32), k.astype(jnp.float32))
        dist = jnp.arange(T)[:, None] - jnp.arange(T)[None, :]
        mask = (dist >= 0) & (dist <= WINDOW)
        scores = jnp.where(mask[None, None, None], scores, jnp.finfo(jnp.float32).min)
        att = jax.nn.softmax(scores, axis=-1).astype(x.dtype)
        ctx = jnp.einsum('bhgtk,bhkd->bhgtd', att, v)
        out = ctx.reshape(B, H, T, Dh).transpose(0, 2, 1, 3).reshape(B, T, H * Dh)
        return out @ Wo.T

    def _L1_xattn_ref(q, latent_kv, Wq, Wkv_expand, Wout):
        import jax, jax.numpy as jnp
        import numpy as np
        B, S, H, NH, L = (2, 256, 256, 16, 64)
        HD = H // NH
        b, sq, _ = q.shape
        sk = latent_kv.shape[1]
        qp = q @ Wq.T
        kv = latent_kv @ Wkv_expand.T
        k, v = jnp.split(kv, 2, axis=-1)
        qh = qp.reshape(b, sq, NH, HD).transpose(0, 2, 1, 3)
        kh = k.reshape(b, sk, NH, HD).transpose(0, 2, 1, 3)
        vh = v.reshape(b, sk, NH, HD).transpose(0, 2, 1, 3)
        inv_sqrt_d = 1.0 / jnp.sqrt(jnp.float32(HD))
        scores = jnp.einsum('bhqd,bhkd->bhqk', qh, kh) * inv_sqrt_d
        causal = jnp.tril(jnp.ones((sq, sk), dtype=bool))
        scores = jnp.where(causal, scores, jnp.finfo(scores.dtype).min)
        attn = jax.nn.softmax(scores, axis=-1)
        out = jnp.einsum('bhqk,bhkd->bhqd', attn, vh)
        out = out.transpose(0, 2, 1, 3).reshape(b, sq, H)
        return out @ Wout.T

    def _L1_ffn_ref(x, w_gate, w_up, w_down):
        import jax, jax.numpy as jnp
        import numpy as np
        DIM_IN = 256
        DIM_HIDDEN = 1024
        gate = jnp.einsum('bsd,hd->bsh', x, w_gate)
        up = jnp.einsum('bsd,hd->bsh', x, w_up)
        gated = jax.nn.silu(gate) * up
        return jnp.einsum('bsh,dh->bsd', gated, w_down)
    x = x + _L0_attn_ref(_layernorm(x, axis=-1), L0_attn_Wk, L0_attn_bk, L0_attn_Wv, L0_attn_bv, L0_attn_Wr, L0_attn_br, L0_attn_Wo, L0_attn_bo, L0_attn_tmk, L0_attn_tmv, L0_attn_tmr, L0_attn_time_decay, L0_attn_time_first)
    x = x + _L0_xattn_ref(_layernorm(x, axis=-1), ctx_512, ctx_512)
    x = x + _L0_ffn_ref(_layernorm(x, axis=-1), L0_ffn_rn_pre1, L0_ffn_rn_pre2, L0_ffn_rn_post1, L0_ffn_rn_post2, L0_ffn_rn_post, L0_ffn_w_gate, L0_ffn_w_up, L0_ffn_w_down, L0_ffn_router_w, L0_ffn_router_scale, L0_ffn_per_expert_scale, L0_ffn_we_gate, L0_ffn_we_up, L0_ffn_we_down)
    x = x + _L1_attn_ref(_layernorm(x, axis=-1), L1_attn_Wq, L1_attn_Wk, L1_attn_Wv, L1_attn_Wo, L1_attn_qn_w, L1_attn_kn_w)
    x = x + _L1_xattn_ref(_layernorm(x, axis=-1), ctx_512, L1_xattn_Wq, L1_xattn_Wkv_expand, L1_xattn_Wout)
    x = x + _L1_ffn_ref(_layernorm(x, axis=-1), L1_ffn_w_gate, L1_ffn_w_up, L1_ffn_w_down)
    return x

_drawn_inputs = setup_inputs


def setup_inputs(seed=0):
    import zlib

    import numpy as np

    out = dict(_drawn_inputs(seed))
    spreads = {'L0_attn_bk': (0.0, 2.0),
     'L0_attn_bv': (0.0, 0.329),
     'L0_attn_br': (0.0, 2.0),
     'L0_attn_bo': (0.0, 0.1),
     'L0_ffn_rn_pre1': (1.0, 0.2),
     'L0_ffn_rn_pre2': (1.0, 0.2),
     'L0_ffn_rn_post1': (1.0, 0.2),
     'L0_ffn_rn_post2': (1.0, 0.2),
     'L0_ffn_rn_post': (1.0, 0.2),
     'L0_ffn_router_scale': (1.0, 0.2),
     'L0_ffn_per_expert_scale': (1.0, 0.2)}
    factors = {'L0_attn_time_first': 113.736,
     'L1_attn_qn_w': 8.0,
     'L1_attn_kn_w': 21.524,
     'L1_xattn_Wq': 8.0,
     'L1_xattn_Wkv_expand': 3.69,
     'L1_xattn_Wout': 3.802,
     'L0_attn_tmr': 4.292}
    for name, (base, spread) in spreads.items():
        noise = np.random.default_rng([zlib.crc32(name.encode()), seed]).standard_normal(out[name].shape)
        drawn = base * np.exp(spread * noise) if base else spread * noise
        out[name] = jnp.asarray(drawn.astype(out[name].dtype))
    for name, factor in factors.items():
        out[name] = (out[name] * factor).astype(out[name].dtype)
    return out
```

```python
from contextlib import ExitStack

import numpy as np

import concourse.bass as bass
from concourse import mybir

ALU = mybir.AluOpType
ACT = mybir.ActivationFunctionType
AX = mybir.AxisListType
F32 = mybir.dt.float32
BF16 = mybir.dt.bfloat16
F32R = mybir.dt.float32r

P = 128
NB = 16
D = 256
KC = D // P
GB = 4
NG = NB // GB
BANK = 512
LN_EPS = 1e-5
RMS_EPS = 1e-6
FAR = -1e30

ROW = P + 1
CHUNK = GB * ROW
Q_HEADS, KV_HEADS, HD = 32, 8, 8
CTX = KV_HEADS * HD
HIDDEN = 1024
HC = HIDDEN // P
EXPERTS, TOP = 8, 2
HEADS, KVH, DH = 16, 4, 128
WINDOW, THETA = 64, 10000.0
XHEADS, XHD = 16, 16

FVEC = ["L0_attn_bk", "L0_attn_bv", "L0_attn_br", "L0_attn_tmk", "L0_attn_tmv", "L0_attn_tmr",
        "L0_attn_time_decay", "L0_attn_time_first", "L0_ffn_rn_pre1", "L0_ffn_rn_pre2",
        "L0_ffn_router_scale"]
BK, BV, BR, TMK, TMV, TMR, DECAY, FIRST, PRE1, PRE2, RSCALE = (2 * i for i in range(len(FVEC)))
ROWS = {}
_at = 0
for _name, _n in (("L0_attn_bo", D), ("L0_ffn_rn_post1", D), ("L0_ffn_rn_post2", D),
                  ("L0_ffn_rn_post", D), ("L1_attn_qn_w", DH), ("L1_attn_kn_w", DH),
                  ("L0_ffn_per_expert_scale", EXPERTS)):
    ROWS[_name] = slice(_at, _at + _n)
    _at += _n
ROWS_N = _at
CONST = {}
_at = 0
for _name, _n in (("ident", P), ("cos", P), ("sin", P), ("window", P), ("causal", P),
                  ("odd", 1), ("half", 2), ("before", EXPERTS * EXPERTS)):
    CONST[_name] = slice(_at, _at + _n)
    _at += _n
CONST_N = _at


class Net:
    pass


def need(engine, sem, count):
    if not isinstance(count, int) or count > 0:
        engine.wait_ge(sem, count)


class Own:

    def __init__(self, engine, sem):
        self.engine, self.sem, self.n = engine, sem, 0

    def did(self, instruction):
        instruction.then_inc(self.sem, 1)
        self.n += 1
        return self.n

    def wait(self, n=None):
        self.engine.wait_ge(self.sem, self.n if n is None else n)

    def again(self):
        self.wait()
        self.engine.sem_clear(self.sem)
        self.n = 0


def wide(column, shape):
    return column.unsqueeze(len(shape) - 1).broadcast_to(shape)


def rounds(engine, one):
    one(0, True, False)
    with engine.Fori(1, NG - 1) as g:
        one(g, False, False)
    one(NG - 1, False, True)


def load(nc, net):
    sp, dram = nc.sync, net.dram
    sp.dma_start(net.fvec[:], dram["fvec"]).then_inc(net.in_small, 16)
    sp.dma_start(net.const[:], dram["const"]).then_inc(net.in_small, 16)
    for g in range(NG):
        sp.dma_start(net.x[:, GB * g:GB * g + GB, :],
                     dram["x"].rearrange("b t d -> t b d")[:, GB * g:GB * g + GB, :]).then_inc(net.in_x[g], 16)
        if g == 0:
            sp.dma_start(net.rwkv_w[:], dram["rwkv_w"]).then_inc(net.in_rwkv, 16)
            sp.dma_start(net.rows[:], dram["rows"]).then_inc(net.in_small, 16)
    sp.dma_start(net.ctx[:], dram["ctx"].rearrange("b t d -> t b d")).then_inc(net.in_ctx, 16)
    sp.dma_start(net.router_w[:], dram["router_w"]).then_inc(net.in_ffn0, 16)
    for tile, source in ((net.gate0, dram["gate0"]), (net.up0, dram["up0"]), (net.down0, dram["down0"]),
                         (net.egate, dram["egate"]), (net.eup, dram["eup"]), (net.edown, dram["edown"])):
        sp.dma_start(tile[:], source).then_inc(net.in_ffn0, 16)
    for tile, source in ((net.wq, dram["wq"]), (net.wk, dram["wk"]), (net.wv, dram["wv"]), (net.wo, dram["wo"])):
        sp.dma_start(tile[:], source).then_inc(net.in_attn1, 16)


def load_late(nc, net):
    for tile, source in ((net.xwq, net.dram["xwq"]), (net.xwkv, net.dram["xwkv"]), (net.xwout, net.dram["xwout"]),
                         (net.gate1, net.dram["gate1"]), (net.up1, net.dram["up1"]), (net.down1, net.dram["down1"])):
        nc.sync.dma_start(tile[:], source).then_inc(net.in_late, 16)


def aggregate(dve, net, done):
    for b in range(NB):
        dve.bn_aggr(net.mean_var[:, b, :], net.stats[:, b, :]).then_inc(done, 1)


def inverse_root(pool, own, out, value, scratch, scale, eps, half):
    own.wait(own.did(pool.tensor_scalar(scratch, value, scale, eps, ALU.mult, ALU.add)))
    return pool.tensor_tensor(out, scratch, half, ALU.pow)


def first(nc, net, sem):
    with ExitStack() as ctx:
        block = ctx.enter_context(nc.Block("first"))

        @block.sync
        def _(sp):
            load(nc, net)

        @block.vector
        def _(dve):
            for g in range(NG):
                dve.wait_ge(net.in_x[g], 16)
                for j in range(GB):
                    dve.bn_stats(net.stats[:, GB * g + j, :], net.x[:, GB * g + j, :])


def rwkv(nc, net, sem):
    with ExitStack() as ctx:
        def sb(name, shape, dt=F32):
            return ctx.enter_context(nc.sbuf_tensor(name, shape, dt))

        row_tile = [P, KC * GB * ROW]
        h_tok = sb("rw_h_tok", [P, GB, D])
        hp = sb("rw_h_padded", row_tile)
        diff = sb("rw_diff", [P, KC, GB * P])
        mixed = sb("rw_mixed", [P, 3, KC, GB * P])
        k, v, er = sb("rw_k", row_tile), sb("rw_v", row_tile), sb("rw_exp_minus_r", row_tile)
        decay = sb("rw_decay", row_tile)
        state = {n: sb(f"rw_{n}", [P, KC * GB * ROW + 1]) for n in ("pp", "aa", "bb")}
        e1, e2, e2v = sb("rw_e1", row_tile), sb("rw_e2", row_tile), sb("rw_e2v", row_tile)
        f1, f2 = sb("rw_f1", row_tile), sb("rw_f2", row_tile)
        rw = sb("rw_out", [P, KC, GB * P])
        neg_br, exp_decay = sb("rw_neg_br", [P, KC]), sb("rw_exp_decay", [P, KC])
        scratch = sb("rw_scratch", [P, NB])
        ps = ctx.enter_context(nc.psum_tensor("rw_psum", [P, 8, BANK], F32))

        preset = sem("rw_preset")
        decay_exp = sem("rw_decay_exp")
        constants = sem("rw_constants")
        aggregated = sem("rw_aggregated")
        rstd_ready = sem("rw_rstd")
        normed = sem("rw_normed")
        turned = sem("rw_turned")
        padded = sem("rw_padded")
        mixed_ready = sem("rw_mixed_ready")
        projected = sem("rw_projected")
        taken = sem("rw_taken")
        exponent = sem("rw_exponent")
        weight = sem("rw_weight")
        rw_ready = sem("rw_ready")
        out_ready = sem("rw_out_ready")
        added = sem("rw_added")
        own_dve, own_pool, own_act = sem("rw_own_dve"), sem("rw_own_pool"), sem("rw_own_act")
        block = ctx.enter_context(nc.Block("rwkv"))

        def flat(tile):
            return tile[:, 0:KC * GB * ROW]

        def tokens(tile, back=0, c=None):
            rows = flat(tile).rearrange("p (g w) -> p g w", w=ROW)[:, :, 1 - back:ROW - back]
            return rows if c is None else rows[:, GB * c:GB * c + GB, :]

        def now(name, c=None):
            rows = state[name][:, 1:1 + KC * GB * ROW].rearrange("p (g w) -> p g w", w=ROW)[:, :, 1:ROW]
            return rows if c is None else rows[:, GB * c:GB * c + GB, :]

        def before(name, c=None):
            return tokens(state[name], 0, c)

        def pads(tile):
            return flat(tile).rearrange("p (g w) -> p g w", w=ROW)[:, :, 0:1]

        def by_row(tile, c=None):
            rows = tile.rearrange("p c (j t) -> p (c j) t", t=P)
            return rows if c is None else rows[:, GB * c:GB * c + GB, :]

        def col(base, c):
            return net.fvec[:, base + c:base + c + 1]

        @block.gpsimd
        def _(pool):
            own = Own(pool, own_pool)
            for tile, value in ((hp, 0.0), (e1, 0.0), (e2, 0.0), (e2v, 0.0), (k, FAR), (decay, 0.0)):
                pool.memset(tile[:], value).then_inc(preset, 1)
            pool.memset(net.ones[:], 1.0).then_inc(preset, 1)
            pool.memset(state["pp"][:, 0:1], FAR).then_inc(preset, 1)
            for name in ("aa", "bb"):
                pool.memset(state[name][:, 0:1], 0.0).then_inc(preset, 1)
            own.did(pool.memset(net.half[:], -0.5))
            own.wait(own.n)
            pool.wait_ge(aggregated, NB)
            inverse_root(pool, own, net.rstd[:], net.mean_var[:, :, 1], scratch[:], 1.0, LN_EPS,
                         net.half[:, 0:NB]).then_inc(rstd_ready, 1)

        @block.tensor
        def _(pe):
            def turn(g):
                pe.wait_ge(normed, g + 1)
                need(pe, added, GB * (g - 1))
                need(pe, padded, KC * g)
                for c in range(KC):
                    for j in range(GB):
                        mm = pe.transpose(ps[:, c, j * P:j * P + P], h_tok[:, j, c * P:c * P + P], ident)
                mm.then_inc(turned, 1)

            def project(g):
                need(pe, taken, 3 * KC * g)
                for m in range(3):
                    pe.wait_ge(mixed_ready, 3 * KC * g + KC * (m + 1))
                    for oc in range(KC):
                        for c in range(KC):
                            mm = pe.matmul(ps[:, 2 + 2 * m + oc, :], net.rwkv_w[:, m, c, oc * P:oc * P + P],
                                           mixed[:, m, c, :], start=(c == 0), stop=(c == KC - 1))
                    mm.then_inc(projected, 1)

            def output(g, h_padded):
                pe.wait_ge(rw_ready, g + 1)
                pe.wait_ge(padded, h_padded)
                need(pe, added, GB * g)
                for j in range(GB):
                    out = ps[:, j // 2, (j % 2) * D:(j % 2) * D + D]
                    for c in range(KC):
                        pe.matmul(out, rw[:, c, j * P:j * P + P], net.rwkv_w[:, 3, c, :],
                                  start=(c == 0), stop=False)
                    mm = pe.matmul(out, net.ones[0:1, 0:P], net.rows[0:1, ROWS["L0_attn_bo"]],
                                   start=False, stop=True)
                    if j % 2 == 1:
                        mm.then_inc(out_ready, 1)

            ident = net.const[:, CONST["ident"]]
            pe.wait_ge(net.in_small, 16 * 3)
            pe.wait_ge(net.in_rwkv, 16)
            pe.wait_ge(preset, 10)
            def one(g, first, last):
                if not last:
                    turn(g + 1)
                    project(g + 1)
                output(g, KC * (g + 2 - last))

            turn(0)
            project(0)
            rounds(pe, one)

        @block.scalar
        def _(act):
            def pad_h(g):
                act.wait_ge(turned, g + 1)
                need(act, mixed_ready, 3 * KC * g)
                for c in range(KC):
                    act.activation(tokens(hp, 0, c), ps[:, c, :].rearrange("p (j t) -> p j t", t=P),
                                   ACT.Copy).then_inc(padded, 1)

            def take(g):
                need(act, rw_ready, g)
                for m, (tile, func, bias, scale) in enumerate((
                        (k, ACT.Identity, lambda c: col(BK, c), 1.0),
                        (v, ACT.Identity, lambda c: col(BV, c), 1.0),
                        (er, ACT.Exp, lambda c: neg_br[:, c:c + 1], -1.0))):
                    act.wait_ge(projected, 3 * g + m + 1)
                    for c in range(KC):
                        act.activation(tokens(tile, 0, c),
                                       ps[:, 2 + 2 * m + c, :].rearrange("p (j t) -> p j t", t=P),
                                       func, bias=bias(c), scale=scale).then_inc(taken, 1)

            def weigh(g, n, tile):
                act.wait_ge(exponent, 2 * 4 * g + 2 * (n + 1))
                act.activation(tokens(tile), tokens(tile), ACT.Exp).then_inc(weight, 1)

            act.wait_ge(net.in_small, 16 * 3)
            act.activation(exp_decay[:], net.fvec[:, DECAY:DECAY + KC], ACT.Exp).then_inc(decay_exp, 1)
            act.wait_ge(constants, 1)
            act.wait_ge(preset, 10)

            def one(g, first, last):
                take(g)
                weigh(g, 0, e1)
                weigh(g, 1, e2)
                if not last:
                    pad_h(g + 1)
                weigh(g, 2, f1)
                weigh(g, 3, f2)

            pad_h(0)
            rounds(act, one)

        @block.vector
        def _(dve):
            own = Own(dve, own_dve)

            def link(instruction):
                own.wait(own.did(instruction))

            def normalise(g):
                need(dve, turned, g)
                for j in range(GB):
                    b = GB * g + j
                    h = dve.tensor_scalar(h_tok[:, j, :], net.x[:, b, :], net.mean_var[:, b, 0:1],
                                          net.rstd[:, bass.ds(b, 1)], ALU.subtract, ALU.mult)
                h.then_inc(normed, 1)

            def mix(g):
                dve.wait_ge(padded, KC * (g + 1))
                link(dve.tensor_tensor(by_row(diff[:]), tokens(hp), tokens(hp, 1), ALU.subtract))
                need(dve, projected, 3 * g)
                for m, tm in enumerate((TMK, TMV, TMR)):
                    for c in range(KC):
                        dve.scalar_tensor_tensor(by_row(mixed[:, m], c), by_row(diff[:], c), col(tm, c),
                                                 tokens(hp, 1, c), ALU.mult, ALU.add).then_inc(mixed_ready, 1)

            def scan(g, more):
                dve.wait_ge(taken, 3 * KC * g + KC)
                link(dve.tensor_tensor_scan(state["pp"][:, 1:], flat(decay), flat(k), FAR, ALU.add, ALU.max))
                for c in range(KC):
                    dve.scalar_tensor_tensor(tokens(e1, 0, c), before("pp", c), neg_exp_decay(c),
                                             now("pp", c), ALU.add, ALU.subtract).then_inc(exponent, 1)
                for c in range(KC):
                    dve.tensor_tensor(tokens(e2, 0, c), tokens(k, 0, c), now("pp", c),
                                      ALU.subtract).then_inc(exponent, 1)
                if more is not None:
                    normalise(more)
                for c in range(KC):
                    own.did(dve.scalar_tensor_tensor(by_row(diff[:], c), tokens(k, 0, c), col(FIRST, c),
                                                     before("pp", c), ALU.add, ALU.max))
                own.wait()
                for c in range(KC):
                    dve.tensor_tensor(tokens(f1, 0, c), before("pp", c), by_row(diff[:], c),
                                      ALU.subtract).then_inc(exponent, 1)
                for c in range(KC):
                    dve.scalar_tensor_tensor(tokens(f2, 0, c), tokens(k, 0, c), col(FIRST, c),
                                             by_row(diff[:], c), ALU.add, ALU.subtract).then_inc(exponent, 1)
                dve.wait_ge(weight, 4 * g + 2)
                dve.wait_ge(taken, 3 * KC * g + 2 * KC)
                link(dve.tensor_tensor(tokens(e2v), tokens(e2), tokens(v), ALU.mult))
                link(dve.tensor_tensor_scan(state["aa"][:, 1:], flat(e1), flat(e2v), 0.0, ALU.mult, ALU.add))
                own.did(dve.tensor_tensor_scan(state["bb"][:, 1:], flat(e1), flat(e2), 0.0, ALU.mult, ALU.add))
                if more is not None:
                    mix(more)
                dve.wait_ge(weight, 4 * g + 4)
                own.wait()
                own.did(dve.tensor_tensor(tokens(e1), tokens(f1), before("aa"), ALU.mult))
                own.did(dve.tensor_tensor(tokens(e2v), tokens(f2), tokens(v), ALU.mult))
                own.did(dve.tensor_tensor(tokens(e2), tokens(f1), before("bb"), ALU.mult))
                own.wait(own.n - 1)
                own.did(dve.tensor_tensor(tokens(e1), tokens(e1), tokens(e2v), ALU.add))
                own.wait(own.n - 1)
                link(dve.tensor_tensor(tokens(e2), tokens(e2), tokens(f2), ALU.add))
                dve.wait_ge(taken, 3 * KC * (g + 1))
                link(dve.scalar_tensor_tensor(tokens(e2), tokens(er), 1.0, tokens(e2), ALU.add, ALU.mult))
                link(dve.reciprocal(tokens(e2), tokens(e2)))
                need(dve, out_ready, 2 * g)
                dve.tensor_tensor(by_row(rw[:]), tokens(e1), tokens(e2), ALU.mult).then_inc(rw_ready, 1)

            def add(g):
                for j in range(GB):
                    dve.wait_ge(out_ready, 2 * g + j // 2 + 1)
                    b = GB * g + j
                    dve.tensor_tensor(net.x[:, b, :], net.x[:, b, :], ps[:, j // 2, (j % 2) * D:(j % 2) * D + D],
                                      ALU.add).then_inc(added, 1)
                    dve.wait_ge(added, GB * g + j + 1)
                    dve.bn_stats(net.stats[:, b, :], net.x[:, b, :])

            def neg_exp_decay(c):
                return flat(decay)[:, CHUNK * c + 1:CHUNK * c + 2]

            aggregate(dve, net, aggregated)
            dve.wait_ge(net.in_small, 16 * 3)
            dve.tensor_scalar(neg_br[:], net.fvec[:, BR:BR + KC], -1.0, None, ALU.mult).then_inc(constants, 1)
            dve.wait_ge(preset, 10)
            dve.wait_ge(decay_exp, 1)
            for c in range(KC):
                own.did(dve.tensor_scalar(tokens(decay, 0, c), tokens(decay, 0, c), exp_decay[:, c:c + 1], -1.0,
                                          ALU.add, ALU.mult))
            own.did(dve.memset(pads(decay), FAR))
            own.wait()
            dve.wait_ge(rstd_ready, 1)
            normalise(0)
            mix(0)
            own.again()

            def one(g, first, last):
                scan(g, None if last else g + 1)
                add(g)
                own.again()

            rounds(dve, one)


class Ring:

    def __init__(self, units, lag, at):
        self.units, self.lag, self.at = units, lag, at

    def unit(self, t, u):
        last = isinstance(t, int) and t == NB - 1
        return (self.units + 1) * t + u + 1 + (u + self.lag > self.at and not last)

    def head(self, t):
        if isinstance(t, int) and t == 0:
            return 0
        return (self.units + 1) * t - self.units + self.at - self.lag + 1

    def unit_bank(self, t, s, u):
        return self.unit(t if isinstance(t, int) else s + 2, u) % 2

    def head_bank(self, t, s):
        return self.head(t if isinstance(t, int) else s + 2) % 2


def pairs(engine, one, steps=NB):
    for s in range(2):
        one(s, s, s == 0, False)
    with engine.Fori(1, steps // 2 - 1) as p:
        for s in range(2):
            one(2 * p + s, s, False, False)
    for s in range(2):
        one(steps - 2 + s, s, False, s == 1)


def earlier(t, s, u, n, units):
    return (t, s, u - n) if u >= n else (t - 1, 1 - s, u - n + units)


def gqa(nc, net, sem):
    U, RINGS, PTS = KV_HEADS, 4, 4
    VW = 32
    SCALE = float(HD) ** -0.5
    LAG = 3
    PARTS = 4

    def unit(t, u):
        if isinstance(t, int) and t == NB - 1:
            return 10 * t + 2 + u
        return 10 * t + (2, 4, 5, 7, 8, 9, 10, 11)[u]

    def half(t, c):
        return c if isinstance(t, int) and t == 0 else 10 * t - (7, 4)[c]

    def bank(number, t, *at):
        return TR + number(t if isinstance(t, int) else 2, *at) % 2

    with ExitStack() as ctx:
        def sb(name, shape, dt=F32):
            return ctx.enter_context(nc.sbuf_tensor(name, shape, dt))

        h_tok, h_parts = sb("gq_h_tok", [P, 2, D]), sb("gq_h_parts", [P, U * 4, PARTS, HD], F32R)
        h_t = sb("gq_h_t", [P, 2, U, P], F32R)
        keys, key_parts = sb("gq_keys", [P, U * P]), sb("gq_key_parts", [P, U * P], F32R)
        kbd = sb("gq_keys_diagonal", [P, 2, U, 4, P], F32R)
        values = sb("gq_values", [P, 2, KV_HEADS, VW])
        weights, weights_t = sb("gq_weights", [P, RINGS, BANK]), sb("gq_weights_t", [P, PTS, BANK])
        top = sb("gq_top", [P, 4, 4])
        out_t = sb("gq_out_t", [P, 2, BANK])
        rsum, out = sb("gq_rsum", [P, 2, 4, 4]), sb("gq_out", [P, 2, 4, 4, HD])
        scratch = sb("gq_scratch", [P, NB])
        ps = ctx.enter_context(nc.psum_tensor("gq_psum", [P, 8, BANK], F32))
        TR, O = 4, 6

        aggregated = sem("gq_aggregated")
        rstd_ready = sem("gq_rstd")
        zeroed = sem("gq_zeroed")
        keys_in = sem("gq_keys_in")
        keys_split = sem("gq_keys_split")
        keys_set = [sem(f"gq_keys_set{s}") for s in range(2)]
        h_split = sem("gq_h_split")
        ones_set = sem("gq_ones_set")
        values_in = sem("gq_values_in")
        normed = sem("gq_normed")
        turned = sem("gq_turned")
        taken = sem("gq_taken")
        scored = sem("gq_scored")
        topped = sem("gq_topped")
        shifted = sem("gq_shifted")
        weighed = sem("gq_weighed")
        attended = sem("gq_attended")
        out_taken = sem("gq_out_taken")
        out_turned = sem("gq_out_turned")
        out_read = sem("gq_out_read")
        own_dve, own_pool = sem("gq_own_dve"), sem("gq_own_pool")
        block = ctx.enter_context(nc.Block("gqa"))

        def set_by(t, s):
            return (t - s) * 32 + 64

        @block.sync
        def _(sp):
            def fetch(t):
                sp.dma_start(keys[:], net.dram["ctx_keys"][t]).then_inc(keys_in, 16)

            def one(t, s, first, last):
                sp.wait_ge(keys_split, t + 1)
                if not last:
                    fetch(t + 1)
                if isinstance(t, int) and t < 2:
                    sp.wait_ge(zeroed, t + 1)
                need(sp, scored, U * (t - 1))
                for j in range(4):
                    sp.dma_start(kbd[32 * j:32 * j + 32, s, :, j, :].bitcast(F32),
                                 key_parts[32 * j:32 * j + 32].bitcast(F32).rearrange("p (u t) -> p u t", t=P)
                                 ).then_inc(keys_set[s], 16)

            fetch(0)
            pairs(sp, one)

        @block.gpsimd
        def _(pool):
            own = Own(pool, own_pool)
            odd = net.const[:, CONST["odd"]].broadcast_to([P, U * P])
            ones = wide(net.ones[:, 0:U * 4], [P, U * 4, 2 * HD]).rearrange("p u (a d) -> p u a d", d=HD)

            def split_keys(t, s):
                pool.wait_ge(keys_in, 16 * (t + 1))
                if not (isinstance(t, int) and t == 0):
                    pool.wait_ge(keys_set[1 - s], set_by(t - 1, 1 - s))
                own.wait(own.did(pool.tensor_tensor(key_parts[:], keys[:], odd, ALU.mult)))
                pool.tensor_tensor(key_parts[:], keys[:], key_parts[:].bitcast(F32),
                                   ALU.subtract).then_inc(keys_split, 1)

            def split_h(t, s):
                h = h_tok[:, s].rearrange("p (u d) -> p u d", d=HD).unsqueeze(2).broadcast_to([P, U * 4, 2, HD])
                pool.wait_ge(normed, t + 1)
                if not (isinstance(t, int) and t == 0):
                    pool.wait_ge(turned, half(t - 1, 1) + 1)
                own.wait(own.did(pool.tensor_tensor(h_parts[:, :, 0:2, :], h, ones, ALU.mult)))
                pool.tensor_tensor(h_parts[:, :, 2:4, :], h, h_parts[:, :, 0:2, :].bitcast(F32),
                                   ALU.subtract).then_inc(h_split, 1)

            pool.wait_ge(aggregated, NB)
            inverse_root(pool, own, net.rstd[:], net.mean_var[:, :, 1], scratch[:], 1.0, LN_EPS,
                         net.half[:, 0:NB]).then_inc(rstd_ready, 1)
            pool.memset(values[:], 0.0).then_inc(ones_set, 1)
            pool.wait_ge(ones_set, 1)
            pool.memset(values[:, :, :, HD:HD + 1], 1.0).then_inc(ones_set, 1)
            pool.wait_ge(ones_set, 2)
            pool.wait_ge(net.in_ctx, 16)

            def one(t, s, first, last):
                split_keys(t, s)
                split_h(t, s)
                need(pool, attended, U * (t - 1))
                pool.tensor_copy(values[:, s, :, 0:HD],
                                 net.ctx[:, t, :].rearrange("p (h d) -> p h d", d=HD)).then_inc(values_in, 1)
                own.again()

            pairs(pool, one)
            fold_ffn0(pool, net)

        @block.tensor
        def _(pe):
            ident = net.const[:, CONST["ident"]]

            def head(t, c):
                pe.wait_ge(h_split, t + 1)
                need(pe, taken, half(t, c) - 1)
                for u in range(4):
                    mm = pe.transpose(ps[:, bank(half, t, c), u * P:u * P + P],
                                      h_parts[:, 16 * c + 4 * u:16 * c + 4 * u + 4].bitcast(F32), ident)
                mm.then_inc(turned, 1)

            def scores(t, s, u):
                if u % 4 == 0:
                    pe.wait_ge(taken, half(t, u // 4) + 1)
                if u == 0:
                    pe.wait_ge(keys_set[s], set_by(t, s))
                need(pe, shifted, U * t + u - 3)
                pe.matmul(ps[:, u % 4, :], h_t[:, s, u, :], kbd[:, s, u, :, :],
                          start=True, stop=True).then_inc(scored, 1)

            def turn(t, s, u):
                pe.wait_ge(weighed, U * t + u + 1)
                need(pe, taken, unit(t, u) - 1)
                for j in range(4):
                    mm = pe.transpose(ps[:, bank(unit, t, u), j * P:j * P + P],
                                      weights[:, u % RINGS, j * P:j * P + P], ident)
                mm.then_inc(turned, 1)

            def attend(t, s, u):
                pe.wait_ge(taken, unit(t, u) + 1)
                c, g = u // 4, 32 * (u % 4)
                if u == 0:
                    pe.wait_ge(values_in, t + 1)
                if u % 4 == 0:
                    need(pe, out_read, 2 * t + c - 1)
                pe.matmul(ps[g:g + VW, O + c, :], values[:, s, u, :], weights_t[:, u % PTS],
                          start=True, stop=True).then_inc(attended, 1)

            def turn_out(t, c):
                pe.wait_ge(out_taken, 2 * t + c + 1)
                for j in range(4):
                    mm = pe.transpose(ps[:, O + c, j * P:j * P + P], out_t[:, c, j * P:j * P + P], ident)
                mm.then_inc(out_turned, 1)

            def one(t, s, first, last):
                for u in range(U):
                    if u < U - 1:
                        scores(t, s, u + 1)
                    elif not last:
                        scores(t + 1, 1 - s, 0)
                    if u >= LAG or not first:
                        turn(*earlier(t, s, u, LAG, U))
                    if u in (3, 5) and not last:
                        head(t + 1, u // 4)
                    if u > LAG or not first:
                        attend(*earlier(t, s, u, LAG + 1, U))
                    if u in (1, 5) and not first:
                        turn_out(t - 1, u // 4)

            for c in range(2):
                head(0, c)
            scores(0, 0, 0)
            pairs(pe, one)
            t, s = NB - 1, 1
            for u in range(U - LAG, U):
                turn(t, s, u)
                attend(t, s, u - 1)
            attend(t, s, U - 1)
            for c in range(2):
                turn_out(t, c)

        @block.scalar
        def _(act):
            def take_head(t, s, c):
                act.wait_ge(turned, half(t, c) + 1)
                need(act, scored, U * (t - 2) + 4 * c + 4)
                act.activation(h_t[:, s, 4 * c:4 * c + 4].rearrange("p u t -> p (u t)"), ps[:, bank(half, t, c), :],
                               ACT.Copy).then_inc(taken, 1)

            def weigh(t, u):
                act.wait_ge(shifted, U * t + u + 1)
                act.activation(weights[:, u % RINGS], weights[:, u % RINGS], ACT.Exp,
                               scale=SCALE).then_inc(weighed, 1)

            def take(t, s, u):
                act.wait_ge(turned, unit(t, u) + 1)
                need(act, attended, U * t + u - 3)
                act.activation(weights_t[:, u % PTS], ps[:, bank(unit, t, u), :],
                               ACT.Copy).then_inc(taken, 1)

            def take_out(t, c):
                act.wait_ge(attended, U * t + 4 * c + 4)
                need(act, out_turned, 2 * t + c - 1)
                act.activation(out_t[:, c], ps[:, O + c, :], ACT.Copy).then_inc(out_taken, 1)

            def one(t, s, first, last):
                for u in range(U):
                    if u >= LAG or not first:
                        take(*earlier(t, s, u, LAG, U))
                    if u in (3, 5) and not last:
                        take_head(t + 1, 1 - s, u // 4)
                    weigh(t, u)
                    if u in (0, 4) and not first:
                        take_out(t - 1, u // 4)

            for c in range(2):
                take_head(0, 0, c)
            pairs(act, one)
            take_out(NB - 1, 0)
            for u in range(U - LAG, U):
                take(NB - 1, 1, u)
            take_out(NB - 1, 1)

        @block.vector
        def _(dve):
            own = Own(dve, own_dve)

            def normalise(t, s):
                need(dve, h_split, t - 1)
                dve.tensor_scalar(h_tok[:, s, :], net.x[:, t, :], net.mean_var[:, t, 0:1],
                                  net.rstd[:, bass.ds(t, 1)], ALU.subtract, ALU.mult).then_inc(normed, 1)

            def rows(u):
                return ps[:, u % 4, :].rearrange("p (j t) -> p j t", t=P)

            def maximum(t, u):
                dve.wait_ge(scored, U * t + u + 1)
                need(dve, shifted, U * t + u - 3)
                dve.tensor_reduce(top[:, u % 4, :], rows(u), AX.X, ALU.max).then_inc(topped, 1)

            def shift(t, s, u):
                dve.wait_ge(topped, U * t + u + 1)
                if not (isinstance(t, int) and t == 0 and u < RINGS):
                    bt, _, bu = earlier(t, s, u, RINGS, U)
                    dve.wait_ge(turned, unit(bt, bu) + 1)
                dve.tensor_tensor(weights[:, u % RINGS].rearrange("p (j t) -> p j t", t=P), rows(u),
                                  wide(top[:, u % 4, :], [P, 4, P]), ALU.subtract).then_inc(shifted, 1)

            def finish(t, c):
                dve.wait_ge(out_turned, 2 * t + c + 1)
                heads = ps[:, O + c, :].rearrange("p (j g v) -> p g j v", j=4, v=VW)
                own.wait(own.did(dve.reciprocal(rsum[:, c], heads[:, :, :, HD])))
                dve.tensor_tensor(out[:, c], heads[:, :, :, 0:HD], wide(rsum[:, c], [P, 4, 4, HD]),
                                  ALU.mult).then_inc(out_read, 1)
                if c == 1:
                    dve.wait_ge(out_read, 2 * t + 2)
                    own.wait(own.did(dve.tensor_tensor(net.x[:, t, :], net.x[:, t, :],
                                                       out.rearrange("p c g j d -> p (c g j d)"), ALU.add)))
                    own.did(dve.bn_stats(net.stats[:, t, :], net.x[:, t, :]))

            def one(t, s, first, last):
                for u in range(U):
                    if u < U - 1:
                        maximum(t, u + 1)
                    elif not last:
                        maximum(t + 1, 0)
                    shift(t, s, u)
                    if u == 0 and not last:
                        normalise(t + 1, 1 - s)
                    if u in (2, 6) and not first:
                        finish(t - 1, u // 4)
                own.again()

            aggregate(dve, net, aggregated)
            dve.memset(kbd[:, 0].bitcast(F32), 0.0).then_inc(zeroed, 1)
            dve.wait_ge(rstd_ready, 1)
            normalise(0, 0)
            dve.memset(kbd[:, 1].bitcast(F32), 0.0).then_inc(zeroed, 1)
            maximum(0, 0)
            pairs(dve, one)
            for c in range(2):
                finish(NB - 1, c)


def fold_ffn0(pool, net):
    pool.wait_ge(net.in_ffn0, 16 * 7)
    for c in range(KC):
        for tile, base, extra in ((net.gate0, PRE1, 1.0), (net.up0, PRE1, 1.0), (net.egate, PRE2, 1.0),
                                  (net.eup, PRE2, 1.0), (net.router_w, RSCALE, float(D) ** -0.5)):
            pool.tensor_scalar(tile[:, c, :], tile[:, c, :], net.fvec[:, base + c:base + c + 1], extra,
                               ALU.mult, ALU.mult)


def experts(nc, net, sem):
    STEPS = HC + EXPERTS
    with ExitStack() as ctx:
        def sb(name, shape, dt=F32):
            return ctx.enter_context(nc.sbuf_tensor(name, shape, dt))

        h_tok, h_t = sb("ex_h_tok", [P, GB, D]), sb("ex_h_t", [P, KC, GB * P])
        gated, hidden = sb("ex_gated", [P, 2, BANK]), sb("ex_hidden", [P, 2, BANK])
        dense, mixture = sb("ex_dense", [P, GB, D]), sb("ex_mixture", [P, GB, D])
        junk = sb("ex_junk", [P, D])
        squares, norm = sb("ex_squares", [P, 3, GB]), sb("ex_norm", [P, 3, GB])
        scratch, scratch2 = sb("ex_scratch", [P, NB]), sb("ex_scratch2", [P, NB])
        scratch3, eps = sb("ex_scratch3", [P, GB]), sb("ex_eps", [P, GB])
        prob, top = sb("ex_prob", [P, GB, EXPERTS]), sb("ex_top", [P, GB])
        above, equal = (sb(f"ex_{n}", [P, GB, EXPERTS, EXPERTS]) for n in ("above", "equal"))
        rank, share = sb("ex_rank", [P, GB, EXPERTS]), sb("ex_share", [P, GB, EXPERTS])
        total = sb("ex_total", [P, GB])
        ps = ctx.enter_context(nc.psum_tensor("ex_psum", [P, 8, BANK], F32))
        ROUTER = 6

        aggregated = sem("ex_aggregated")
        rstd_ready = sem("ex_rstd")
        normed = sem("ex_normed")
        turned = sem("ex_turned")
        taken = sem("ex_taken")
        routed = sem("ex_routed")
        logits_read = sem("ex_logits_read")
        prob_ready = sem("ex_prob_ready")
        gate_full, up_full = sem("ex_gate_full"), sem("ex_up_full")
        gelu_done = sem("ex_gelu_done")
        hidden_ready = sem("ex_hidden_ready")
        down_done = sem("ex_down_done")
        squared = sem("ex_squared")
        norm_ready = sem("ex_norm_ready")
        dense_ready = sem("ex_dense_ready")
        weighed = sem("ex_weighed")
        summed = sem("ex_summed")
        own_dve, own_pool = sem("ex_own_dve"), sem("ex_own_pool")
        block = ctx.enter_context(nc.Block("experts"))

        def down_bank(q):
            return 4 if q < HC or q % 2 == 1 else 6

        def row(name):
            return net.rows[:, ROWS[name]]

        @block.gpsimd
        def _(pool):
            own = Own(pool, own_pool)

            def link(instruction):
                own.wait(own.did(instruction))

            pool.wait_ge(aggregated, NB)
            var = net.mean_var[:, :, 1]
            half = net.half[:, 0:NB]
            link(inverse_root(pool, own, net.rstd[:], var, scratch[:], 1.0, LN_EPS, half))
            link(pool.tensor_tensor(scratch[:], net.rstd[:], net.rstd[:], ALU.mult))
            link(pool.tensor_tensor(scratch[:], scratch[:], var, ALU.mult))
            link(inverse_root(pool, own, scratch2[:], scratch[:], scratch[:], 1.0, RMS_EPS, half))
            pool.tensor_tensor(net.rstd[:], net.rstd[:], scratch2[:], ALU.mult).then_inc(rstd_ready, 1)

            def normalise(g, n):
                pool.wait_ge(squared, 3 * GB * g + GB * (n + 1))
                link(pool.tensor_tensor(scratch3[:], squares[:, n], eps[:], ALU.add))
                pool.tensor_tensor(norm[:, n], scratch3[:], net.half[:, 0:GB], ALU.pow).then_inc(norm_ready, 1)
                own.again()

            link(pool.memset(eps[:], RMS_EPS))
            own.again()
            with pool.Fori(0, NG) as g:
                for n in range(3):
                    normalise(g, n)

        @block.tensor
        def _(pe):
            ident = net.const[:, CONST["ident"]]

            def turn(g):
                pe.wait_ge(normed, g + 1)
                need(pe, hidden_ready, STEPS * g - 1)
                for c in range(KC):
                    for j in range(GB):
                        mm = pe.transpose(ps[:, c, j * P:j * P + P], h_tok[:, j, c * P:c * P + P], ident)
                mm.then_inc(turned, 1)

            def route(g):
                pe.wait_ge(taken, KC * (g + 1))
                need(pe, weighed, EXPERTS * g - 1)
                for j in range(GB):
                    for c in range(KC):
                        mm = pe.matmul(ps[:, ROUTER, j * EXPERTS:(j + 1) * EXPERTS],
                                       h_t[:, c, j * P:j * P + P], net.router_w[:, c, :],
                                       start=(c == 0), stop=(c == KC - 1))
                mm.then_inc(routed, 1)

            def gate_up(g, q):
                need(pe, hidden_ready, STEPS * g + q - 1)
                weights = (net.gate0, net.up0) if q < HC else (net.egate, net.eup)
                at = (q % HC) * P
                for m, (w, full) in enumerate(zip(weights, (gate_full, up_full))):
                    for c in range(KC):
                        mm = pe.matmul(ps[:, 2 * (q % 2) + m, :], w[:, c, at:at + P], h_t[:, c, :],
                                       start=(c == 0), stop=(c == KC - 1))
                    mm.then_inc(full, 1)

            def down(g, q):
                pe.wait_ge(hidden_ready, STEPS * g + q + 1)
                if q == 0:
                    need(pe, weighed, EXPERTS * g)
                if q == HC:
                    pe.wait_ge(logits_read, g + 1)
                if q == HC + 1:
                    pe.wait_ge(dense_ready, GB * (g + 1))
                if q > HC + 1:
                    pe.wait_ge(weighed, EXPERTS * g + q - HC - 1)
                w = net.down0[:, q, :] if q < HC else net.edown[:, q - HC, :]
                for j in range(GB):
                    mm = pe.matmul(ps[:, down_bank(q) + j // 2, (j % 2) * D:(j % 2) * D + D],
                                   hidden[:, q % 2, j * P:j * P + P], w,
                                   start=(q >= HC or (q == 0 and j % 2 == 0)), stop=(q >= HC - 1),
                                   skip_group_check=True)
                mm.then_inc(down_done, 1)

            def one(g, first, last):
                route(g)
                for q in range(STEPS):
                    gate_up(g, q)
                    if q > 0:
                        down(g, q - 1)
                if not last:
                    turn(g + 1)
                down(g, STEPS - 1)

            turn(0)
            rounds(pe, one)

        @block.scalar
        def _(act):
            def take(g):
                act.wait_ge(turned, g + 1)
                need(act, up_full, STEPS * g)
                for c in range(KC):
                    act.activation(h_t[:, c, :], ps[:, c, :], ACT.Copy).then_inc(taken, 1)

            def square(g, n, source):
                need(act, norm_ready, 3 * g + (n > 0))
                for j in range(GB):
                    if not (isinstance(g, int) and g == 0 and n == 0 and j == 0):
                        act.wait_ge(squared, 3 * GB * g + GB * n + j)
                    act.activation(junk[:], source(j), ACT.Square, scale=float(D) ** -0.5,
                                   accum_out=squares[:, n, j:j + 1]).then_inc(squared, 1)

            def one(g, first, last):
                for q in range(STEPS):
                    act.wait_ge(gate_full, STEPS * g + q + 1)
                    need(act, hidden_ready, STEPS * g + q - 1)
                    act.activation(gated[:, q % 2, :], ps[:, 2 * (q % 2), :],
                                   ACT.Gelu_apprx_tanh).then_inc(gelu_done, 1)
                    if q == 1:
                        act.wait_ge(logits_read, g + 1)
                        act.activation(prob[:], prob[:], ACT.Exp).then_inc(prob_ready, 1)
                        if not first:
                            mixture_squares(g - 1)
                    if q == 4 and not first:
                        sum_squares(g - 1)
                    if q == HC:
                        act.wait_ge(down_done, STEPS * g + HC)
                        square(g, 0, lambda j: ps[:, 4 + j // 2, (j % 2) * D:(j % 2) * D + D])
                if not last:
                    take(g + 1)

            def mixture_squares(g):
                act.wait_ge(weighed, EXPERTS * (g + 1))
                square(g, 1, lambda j: mixture[:, j, :])

            def sum_squares(g):
                act.wait_ge(summed, GB * (g + 1))
                square(g, 2, lambda j: mixture[:, j, :])

            take(0)
            rounds(act, one)
            mixture_squares(NG - 1)
            sum_squares(NG - 1)

        @block.vector
        def _(dve):
            own = Own(dve, own_dve)

            def link(instruction):
                own.wait(own.did(instruction))

            def normalise(g):
                need(dve, turned, g)
                for j in range(GB):
                    b = GB * g + j
                    h = dve.tensor_scalar(h_tok[:, j, :], net.x[:, b, :], net.mean_var[:, b, 0:1],
                                          net.rstd[:, bass.ds(b, 1)], ALU.subtract, ALU.mult)
                h.then_inc(normed, 1)

            def read_logits(g):
                dve.wait_ge(routed, g + 1)
                logits = ps[:, ROUTER, 0:GB * EXPERTS].rearrange("p (j e) -> p j e", e=EXPERTS)
                link(dve.tensor_reduce(top[:], logits, AX.X, ALU.max))
                dve.tensor_tensor(prob[:], logits, wide(top[:], [P, GB, EXPERTS]),
                                  ALU.subtract).then_inc(logits_read, 1)

            def choose(g):
                dve.wait_ge(prob_ready, g + 1)
                shape = [P, GB, EXPERTS, EXPERTS]
                this, other = wide(prob[:], shape), prob[:].unsqueeze(2).broadcast_to(shape)
                first = net.const[:, CONST["before"]].rearrange("p (e f) -> p e f", f=EXPERTS)
                own.did(dve.tensor_tensor(above[:], other, this, ALU.is_gt))
                link(dve.tensor_tensor(equal[:], other, this, ALU.is_equal))
                link(dve.tensor_tensor(equal[:], equal[:], first.unsqueeze(1).broadcast_to(shape), ALU.mult))
                link(dve.tensor_tensor(above[:], above[:], equal[:], ALU.add))
                link(dve.tensor_reduce(rank[:], above[:], AX.X, ALU.add))
                link(dve.scalar_tensor_tensor(share[:], rank[:], float(TOP), prob[:], ALU.is_lt, ALU.mult))
                link(dve.tensor_reduce(total[:], share[:], AX.X, ALU.add))
                link(dve.reciprocal(total[:], total[:]))
                link(dve.tensor_tensor(share[:], share[:], wide(total[:], [P, GB, EXPERTS]), ALU.mult))
                link(dve.tensor_tensor(share[:], share[:], row("L0_ffn_per_expert_scale").unsqueeze(1)
                                       .broadcast_to([P, GB, EXPERTS]), ALU.mult))

            def hide(g, q):
                dve.wait_ge(gelu_done, STEPS * g + q + 1)
                dve.wait_ge(up_full, STEPS * g + q + 1)
                need(dve, down_done, STEPS * g + q - 1)
                dve.tensor_tensor(hidden[:, q % 2, :], gated[:, q % 2, :], ps[:, 2 * (q % 2) + 1, :],
                                  ALU.mult).then_inc(hidden_ready, 1)

            def scale_dense(g):
                dve.wait_ge(norm_ready, 3 * g + 1)
                for j in range(GB):
                    dve.scalar_tensor_tensor(dense[:, j, :], ps[:, 4 + j // 2, (j % 2) * D:(j % 2) * D + D],
                                             norm[:, 0, j:j + 1], row("L0_ffn_rn_post1"),
                                             ALU.mult, ALU.mult).then_inc(dense_ready, 1)

            def weigh(g, e):
                q = HC + e
                dve.wait_ge(down_done, STEPS * g + q + 1)
                if e > 0:
                    dve.wait_ge(weighed, EXPERTS * g + e)
                    own.wait()
                for j in range(GB):
                    y = ps[:, down_bank(q) + j // 2, (j % 2) * D:(j % 2) * D + D]
                    if e == 0:
                        w = dve.tensor_scalar(mixture[:, j, :], y, share[:, j, e:e + 1], None, ALU.mult)
                    else:
                        w = dve.scalar_tensor_tensor(mixture[:, j, :], y, share[:, j, e:e + 1],
                                                     mixture[:, j, :], ALU.mult, ALU.add)
                    if j < GB - 1:
                        own.did(w)
                w.then_inc(weighed, 1)

            def combine(g):
                dve.wait_ge(norm_ready, 3 * g + 2)
                dve.wait_ge(dense_ready, GB * (g + 1))
                for j in range(GB):
                    own.did(dve.scalar_tensor_tensor(mixture[:, j, :], mixture[:, j, :], norm[:, 1, j:j + 1],
                                                     row("L0_ffn_rn_post2"), ALU.mult, ALU.mult))
                own.wait()
                for j in range(GB):
                    dve.tensor_tensor(mixture[:, j, :], mixture[:, j, :], dense[:, j, :],
                                      ALU.add).then_inc(summed, 1)

            def finish(g):
                dve.wait_ge(norm_ready, 3 * g + 3)
                for j in range(GB):
                    own.did(dve.scalar_tensor_tensor(mixture[:, j, :], mixture[:, j, :], norm[:, 2, j:j + 1],
                                                     row("L0_ffn_rn_post"), ALU.mult, ALU.mult))
                own.wait()
                for j in range(GB):
                    b = GB * g + j
                    own.did(dve.tensor_tensor(net.x[:, b, :], net.x[:, b, :], mixture[:, j, :], ALU.add))
                own.wait()
                for j in range(GB):
                    b = GB * g + j
                    own.did(dve.bn_stats(net.stats[:, b, :], net.x[:, b, :]))

            def one(g, first, last):
                for q in range(STEPS):
                    if q == 0:
                        read_logits(g)
                    hide(g, q)
                    if q == 0 and not first:
                        weigh(g - 1, EXPERTS - 1)
                    if q == 3 and not first:
                        combine(g - 1)
                    if q == 6 and not first:
                        finish(g - 1)
                    if q == 7:
                        choose(g)
                    if q == HC and not last:
                        normalise(g + 1)
                    if q == HC + 1:
                        scale_dense(g)
                    if q >= HC + 1:
                        weigh(g, q - HC - 1)
                own.again()

            aggregate(dve, net, aggregated)
            dve.wait_ge(rstd_ready, 1)
            normalise(0)
            rounds(dve, one)
            own.did(dve.engine_nop())
            weigh(NG - 1, EXPERTS - 1)
            combine(NG - 1)
            finish(NG - 1)


def windowed(nc, net, sem):
    U = KVH
    ORDER = [("p", -1, 3), ("q", 0, 1), ("p", 0, 0), ("q", 0, 2), ("h", 1, 0), ("p", 0, 1),
             ("q", 0, 3), ("p", 0, 2), ("k", 1, 0), ("q", 1, 0)]
    PJ, SC, TR, AV, OUT = 0, 2, 4, 6, 7
    K = 2

    def bank_of(what, g=0):
        return TR + next(i for i, (w, _, h) in enumerate(ORDER) if (w, h) == (what, g)) % 2

    def number(what, t, g=0):
        if what == "h" and isinstance(t, int) and t == 0:
            return 0
        if what == "q" and g == 3 and isinstance(t, int) and t == NB - 1:
            return 6 * t + 5
        return 6 * t + {"h": -1, "k": 1, "q": (2, 3, 4, 6)[g]}[what]

    with ExitStack() as ctx:
        def sb(name, shape, dt=F32):
            return ctx.enter_context(nc.sbuf_tensor(name, shape, dt))

        h_tok, h_t = sb("wi_h_tok", [P, 2, D]), sb("wi_h_t", [P, 2, KC, P])
        values = sb("wi_values", [P, 2, KVH * DH])
        raw, square = sb("wi_raw", [P, 3, 4, DH]), sb("wi_square", [P, 2, 4, DH])
        straight, crossed = sb("wi_straight", [P, 3, 4, DH]), sb("wi_crossed", [P, 3, 4, DH])
        q_t, k_t = sb("wi_q_t", [P, 2, 4, P]), sb("wi_k_t", [P, 2, KVH, P])
        weights, weights_t = sb("wi_weights", [P, 2, 4, P]), sb("wi_weights_t", [P, 2, BANK])
        out_t = sb("wi_out_t", [P, 2, 4, P])
        tables = {n: sb(f"wi_{n}", [P, DH]) for n in ("cos_q", "sin_q", "cos_k", "sin_k")}
        sums, scale = sb("wi_sums", [P, 3, 4]), sb("wi_scale", [P, 5, 4])
        top, bias = sb("wi_top", [P, 2, 4]), sb("wi_bias", [P, 2, 4])
        total, inverse = sb("wi_total", [P, 2, 4]), sb("wi_inverse", [P, 2, 4])
        scratch, scratch2 = sb("wi_scratch", [P, NB]), sb("wi_scratch2", [P, 4])
        eps = sb("wi_eps", [P, 4])
        mask, ident_b = sb("wi_mask", [P, 4, P], BF16), sb("wi_ident", [P, P], BF16)
        ps = ctx.enter_context(nc.psum_tensor("wi_psum", [P, 8, BANK], F32))

        aggregated = sem("wi_aggregated")
        rstd_ready = sem("wi_rstd")
        tables_ready = sem("wi_tables")
        normed = sem("wi_normed")
        projected = sem("wi_projected")
        proj_taken = sem("wi_proj_taken")
        squared = sem("wi_squared")
        summed = sem("wi_summed")
        parts = sem("wi_parts")
        rotated = sem("wi_rotated")
        turned = sem("wi_turned")
        turned_taken = sem("wi_turned_taken")
        turned_p = sem("wi_turned_p")
        turned_p_taken = sem("wi_turned_p_taken")
        scored = sem("wi_scored")
        bias_ready = sem("wi_bias")
        weighed = sem("wi_weighed")
        inverted = sem("wi_inverted")
        normalised = sem("wi_normalised")
        attended = sem("wi_attended")
        attended_taken = sem("wi_attended_taken")
        output = sem("wi_output")
        added = sem("wi_added")
        own_dve, own_pool = sem("wi_own_dve"), sem("wi_own_pool")
        block = ctx.enter_context(nc.Block("windowed"))

        def ahead(t, s, g, last):
            if g < 2:
                return [("q", t, s, g + 2)]
            if last:
                return []
            kv = [("v", t + 1, 1 - s, 0), ("k", t + 1, 1 - s, 0)] if g == 2 else []
            return kv + [("q", t + 1, 1 - s, g - 2)]

        FIRST_ITEMS = [("v", 0, 0, 0), ("k", 0, 0, 0), ("q", 0, 0, 0), ("q", 0, 0, 1)]

        def of_six(what, t, g):
            return 6 * t + {"v": 0, "k": 1, "q": 2 + g}[what]

        def of_five(what, t, g):
            return 5 * t + {"k": 0, "q": 1 + g}[what]

        def square_slot(what, t, s, g):
            return (s + of_five(what, 0, g)) % 2

        def slot(what, g):
            return K if what == "k" else g % 2

        @block.sync
        def _(sp):
            load_late(nc, net)

        @block.gpsimd
        def _(pool):
            own = Own(pool, own_pool)

            def link(instruction):
                own.wait(own.did(instruction))

            link(pool.memset(eps[:], DH * RMS_EPS))
            pool.wait_ge(aggregated, NB)
            inverse_root(pool, own, net.rstd[:], net.mean_var[:, :, 1], scratch[:], 1.0, LN_EPS,
                         net.half[:, 0:NB]).then_inc(rstd_ready, 1)

            def find_scale(what, t, s, g):
                n, at = of_five(what, t, g), slot(what, g)
                scale_at = 4 if what == "k" else g
                pool.wait_ge(summed, n + 1)
                link(pool.tensor_tensor(scratch2[:], sums[:, at], eps[:], ALU.add))
                link(pool.tensor_tensor(scale[:, scale_at], scratch2[:], net.half[:, 0:4], ALU.pow))

            def join(what, t, s, g):
                n, at = of_five(what, t, g), slot(what, g)
                scale_at = 4 if what == "k" else g
                pool.wait_ge(parts, 3 * (n + 1))
                added_up = pool.tensor_tensor(straight[:, at], straight[:, at], crossed[:, at], ALU.add)
                if what == "k":
                    link(added_up)
                    added_up = pool.tensor_tensor(straight[:, at], straight[:, at],
                                                  wide(scale[:, scale_at], [P, 4, DH]), ALU.mult)
                added_up.then_inc(rotated, 1)

            def normalise(t, g):
                pool.wait_ge(inverted, U * t + g + 1)
                pool.tensor_tensor(weights[:, g % 2], weights[:, g % 2], wide(inverse[:, g % 2], [P, 4, P]),
                                   ALU.mult).then_inc(normalised, 1)

            def one(t, s, first, last):
                for g in range(U):
                    items = [item for item in ahead(t, s, g, last) if item[0] != "v"]
                    for item in items[:1]:
                        find_scale(*item)
                    normalise(t, g)
                    for item in items[:1]:
                        join(*item)
                    for item in items[1:]:
                        find_scale(*item)
                        join(*item)
                own.again()

            for item in FIRST_ITEMS[1:]:
                find_scale(*item)
                join(*item)
            pairs(pool, one)

        @block.tensor
        def _(pe):
            ident = net.const[:, CONST["ident"]]

            def turn_h(t, s):
                pe.wait_ge(normed, t + 1)
                if not (isinstance(t, int) and t == 0):
                    pe.wait_ge(turned_p_taken, U * (t - 1) + 1)
                for c in range(KC):
                    mm = pe.transpose(ps[:, bank_of("h"), c * P:c * P + P], h_tok[:, s, c * P:c * P + P], ident)
                mm.then_inc(turned, 1)

            def turn_heads(what, t, g):
                pe.wait_ge(rotated, of_five(what, t, g) + 1)
                if what == "k":
                    need(pe, turned_taken, number("h", t) + 2 if not (isinstance(t, int) and t == 0) else 1)
                elif g == 0:
                    need(pe, turned_p_taken, U * (t - 1) + 3)
                elif g == 3:
                    pe.wait_ge(turned_taken, number("q", t, 3))
                else:
                    pe.wait_ge(turned_taken, number("q", t, g - 1) + 1)
                for j in range(4):
                    mm = pe.transpose(ps[:, bank_of(what, g), j * P:j * P + P], straight[:, slot(what, g), j, :], ident)
                mm.then_inc(turned, 1)

            def turn_weights(t, g):
                pe.wait_ge(normalised, U * t + g + 1)
                if g == 3:
                    pe.wait_ge(turned_taken, (number("k", t + 1) + 1) if not (isinstance(t, int) and t == NB - 1)
                               else number("q", t, 3) + 1)
                elif g == 1:
                    pe.wait_ge(turned_taken, number("q", t, 2) + 1)
                else:
                    need(pe, turned_p_taken, U * t + g)
                for j in range(4):
                    mm = pe.transpose(ps[:, bank_of("p", g), j * P:j * P + P], weights[:, g % 2, j, :], ident)
                mm.then_inc(turned_p, 1)

            def project(what, t, s, g):
                n = of_six(what, t, g)
                need(pe, proj_taken, n - 1)
                if what == "v":
                    pe.wait_ge(turned_taken, number("h", t) + 1)
                w = {"v": net.wv, "k": net.wk, "q": net.wq}[what]
                for c in range(KC):
                    mm = pe.matmul(ps[:, PJ + of_six(what, 0, g) % 2, :], h_t[:, s, c, :],
                                   w[:, c, g * BANK:g * BANK + BANK], start=(c == 0), stop=(c == KC - 1))
                mm.then_inc(projected, 1)

            def scores(t, s, g):
                if g == 0:
                    pe.wait_ge(turned_taken, number("k", t) + 1)
                pe.wait_ge(turned_taken, number("q", t, g) + 1)
                need(pe, weighed, 4 * (U * t + g - 1))
                bank = ps[:, SC + g % 2, :]
                pe.matmul(bank, ident_b[:], mask.rearrange("p j t -> p (j t)"), start=True, stop=False,
                          skip_group_check=True)
                for j in range(4):
                    mm = pe.matmul(bank[:, j * P:j * P + P], q_t[:, g % 2, j, :], k_t[:, s, g, :],
                                   start=False, stop=(j == 3), skip_group_check=True)
                mm.then_inc(scored, 1)

            def attend(t, s, g):
                pe.wait_ge(turned_p_taken, U * t + g + 1)
                need(pe, attended_taken, U * t + g)
                pe.matmul(ps[:, AV, :], values[:, s, g * DH:g * DH + DH], weights_t[:, g % 2],
                          start=True, stop=True).then_inc(attended, 1)

            def project_out(t, g):
                pe.wait_ge(attended_taken, U * t + g + 1)
                if g == 0:
                    need(pe, added, t)
                for j in range(4):
                    mm = pe.matmul(ps[:, OUT, 0:D], out_t[:, g % 2, j, :], net.wo[:, 4 * g + j, :],
                                   start=(g == 0 and j == 0), stop=(g == 3 and j == 3), skip_group_check=True)
                mm.then_inc(output, 1)

            def one(t, s, first, last):
                for g in range(U):
                    for item in ahead(t, s, g, last):
                        project(*item)
                    scores(t, s, g)
                    if g > 0 or not first:
                        pt, _, pg = earlier(t, s, g, 1, U)
                        turn_weights(pt, pg)
                    if g > 1 or not first:
                        pt, _, pg = earlier(t, s, g, 2, U)
                        project_out(pt, pg)
                    if g < 3:
                        turn_heads("q", t, g + 1)
                    elif not last:
                        turn_heads("k", t + 1, 0)
                        turn_heads("q", t + 1, 0)
                    if g == 1 and not last:
                        turn_h(t + 1, 1 - s)
                    if g > 0 or not first:
                        attend(*earlier(t, s, g, 1, U))

            pe.wait_ge(tables_ready, 2)
            pe.wait_ge(net.in_attn1, 16 * 4)
            turn_h(0, 0)
            for item in FIRST_ITEMS:
                project(*item)
            turn_heads("k", 0, 0)
            turn_heads("q", 0, 0)
            pairs(pe, one)
            turn_weights(NB - 1, 3)
            project_out(NB - 1, 2)
            attend(NB - 1, 1, 3)
            project_out(NB - 1, 3)

        @block.scalar
        def _(act):
            def take(what, t, s, g):
                act.wait_ge(projected, of_six(what, t, g) + 1)
                bank = ps[:, PJ + of_six(what, 0, g) % 2, :]
                if what == "v":
                    need(act, attended, U * (t - 1))
                    act.activation(values[:, s], bank, ACT.Copy).then_inc(proj_taken, 1)
                    return
                n, at = of_five(what, t, g), slot(what, g)
                if what == "k":
                    need(act, parts, 3 * (of_five("k", t - 1, 0) + 1))
                else:
                    need(act, parts, 3 * (of_five("q", t, g - 2) + 1) if g >= 2
                         else 3 * (of_five("q", t - 1, g + 2) + 1))
                act.activation(raw[:, at].rearrange("p j d -> p (j d)"), bank, ACT.Copy).then_inc(proj_taken, 1)
                act.wait_ge(proj_taken, of_six(what, t, g) + 1)
                need(act, summed, n - 1)
                act.activation(square[:, square_slot(what, t, s, g)], raw[:, at], ACT.Square).then_inc(squared, 1)

            def take_turned(what, t, s, g=0):
                act.wait_ge(turned, number(what, t, g) + 1)
                bank = ps[:, bank_of(what, g), :]
                if what == "h":
                    need(act, projected, of_six("q", t - 2, 3) + 1)
                    act.activation(h_t[:, s].rearrange("p c t -> p (c t)"), bank[:, 0:D],
                                   ACT.Copy).then_inc(turned_taken, 1)
                    return
                need(act, scored, U * (t - 1) if what == "k" else U * t + g - 1)
                tile = k_t[:, s] if what == "k" else q_t[:, g % 2]
                act.activation(tile.rearrange("p j t -> p (j t)"), bank, ACT.Copy).then_inc(turned_taken, 1)

            def weigh(t, g):
                w = U * t + g
                act.wait_ge(bias_ready, w + 1)
                need(act, turned_p, w - 1)
                need(act, inverted, w - 1)
                for j in range(4):
                    act.activation(weights[:, g % 2, j, :], ps[:, SC + g % 2, j * P:j * P + P], ACT.Exp,
                                   bias=bias[:, g % 2, j:j + 1], scale=scale[:, g, j:j + 1],
                                   accum_out=total[:, g % 2, j:j + 1]).then_inc(weighed, 1)

            def take_attended(t, g):
                act.wait_ge(attended, U * t + g + 1)
                need(act, output, U * t + g - 1)
                act.activation(out_t[:, g % 2].rearrange("p j t -> p (j t)"), ps[:, AV, :],
                               ACT.Copy).then_inc(attended_taken, 1)

            def one(t, s, first, last):
                for g in range(U):
                    for item in ahead(t, s, g, last):
                        take(*item)
                    weigh(t, g)
                    if g < 3:
                        take_turned("q", t, s, g + 1)
                    elif not last:
                        take_turned("k", t + 1, 1 - s)
                        take_turned("q", t + 1, 1 - s, 0)
                    if g == 1 and not last:
                        take_turned("h", t + 1, 1 - s)
                    if g > 0 or not first:
                        pt, _, pg = earlier(t, s, g, 1, U)
                        take_attended(pt, pg)

            take_turned("h", 0, 0)
            for item in FIRST_ITEMS:
                take(*item)
            take_turned("k", 0, 0)
            take_turned("q", 0, 0, 0)
            pairs(act, one)
            take_attended(NB - 1, 3)

        @block.vector
        def _(dve):
            own = Own(dve, own_dve)

            def link(instruction):
                own.wait(own.did(instruction))

            def normalise(t, s):
                if not (isinstance(t, int) and t < 2):
                    dve.wait_ge(turned, number("h", t - 2) + 1)
                dve.tensor_scalar(h_tok[:, s, :], net.x[:, t, :], net.mean_var[:, t, 0:1],
                                  net.rstd[:, bass.ds(t, 1)], ALU.subtract, ALU.mult).then_inc(normed, 1)

            def rotate(what, t, s, g):
                if what == "v":
                    return
                n, at = of_five(what, t, g), slot(what, g)
                dve.wait_ge(squared, n + 1)
                need(dve, rotated, of_five(what, t - 1, g) + 1 if what == "k" else
                     of_five("q", t, g - 2) + 1 if g >= 2 else of_five("q", t - 1, g + 2) + 1)
                dve.tensor_reduce(sums[:, at], square[:, square_slot(what, t, s, g)], AX.X,
                                  ALU.add).then_inc(summed, 1)
                if what == "k":
                    need(dve, turned, number("k", t - 1) + 1)
                elif g >= 2:
                    dve.wait_ge(turned, number("q", t, g - 2) + 1)
                elif not (isinstance(t, int) and t == 0):
                    dve.wait_ge(turned, number("q", t - 1, g + 2) + 1)
                cos, sin = (tables[f"{n}_{what}"] for n in ("cos", "sin"))
                half = DH // 2

                def over_heads(table):
                    return table.unsqueeze(1).broadcast_to([P, 4, table.shape[-1]])

                dve.tensor_tensor(straight[:, at], raw[:, at], over_heads(cos[:]), ALU.mult).then_inc(parts, 1)
                for to, source in ((slice(0, half), slice(half, DH)), (slice(half, DH), slice(0, half))):
                    dve.tensor_tensor(crossed[:, at, :, to], raw[:, at, :, source], over_heads(sin[:, to]),
                                      ALU.mult).then_inc(parts, 1)

            def maximum(t, g):
                w = U * t + g
                dve.wait_ge(scored, w + 1)
                link(dve.tensor_reduce(top[:, g % 2], ps[:, SC + g % 2, :].rearrange("p (j t) -> p j t", t=P),
                                       AX.X, ALU.max))
                dve.wait_ge(rotated, of_five("q", t, g) + 1)
                need(dve, weighed, 4 * (w - 1))
                dve.scalar_tensor_tensor(bias[:, g % 2], top[:, g % 2], -1.0, scale[:, g], ALU.mult,
                                         ALU.mult).then_inc(bias_ready, 1)

            def take_weights(t, g):
                w = U * t + g
                dve.wait_ge(turned_p, w + 1)
                need(dve, attended, w - 1)
                dve.tensor_copy(weights_t[:, g % 2], ps[:, bank_of("p", g), :]).then_inc(turned_p_taken, 1)

            def invert(t, g):
                w = U * t + g
                dve.wait_ge(weighed, 4 * (w + 1))
                need(dve, normalised, w - 1)
                dve.reciprocal(inverse[:, g % 2], total[:, g % 2]).then_inc(inverted, 1)

            def finish(t):
                dve.wait_ge(output, U * (t + 1))
                dve.tensor_tensor(net.x[:, t, :], net.x[:, t, :], ps[:, OUT, 0:D], ALU.add).then_inc(added, 1)
                dve.wait_ge(added, t + 1)
                own.did(dve.bn_stats(net.stats[:, t, :], net.x[:, t, :]))

            def one(t, s, first, last):
                for g in range(U):
                    if g == 0 and not last:
                        normalise(t + 1, 1 - s)
                    maximum(t, g)
                    if g > 0 or not first:
                        pt, _, pg = earlier(t, s, g, 1, U)
                        take_weights(pt, pg)
                    items = [item for item in ahead(t, s, g, last) if item[0] != "v"]
                    for item in items[:1]:
                        rotate(*item)
                    invert(t, g)
                    for item in items[1:]:
                        rotate(*item)
                    if g == 1 and not first:
                        finish(t - 1)
                own.again()

            aggregate(dve, net, aggregated)
            for name, row, factor in (("q", "L1_attn_qn_w", 1.0), ("k", "L1_attn_kn_w", float(DH) ** 0.5)):
                w = net.rows[:, ROWS[row]]
                half = DH // 2
                own.did(dve.scalar_tensor_tensor(tables[f"cos_{name}"][:], w, 1.0, net.const[:, CONST["cos"]],
                                                 ALU.add, ALU.mult))
                for to, source in ((0, half), (half, 0)):
                    own.did(dve.scalar_tensor_tensor(
                        tables[f"sin_{name}"][:, to:to + half], w[:, source:source + half], 1.0,
                        net.const[:, CONST["sin"].start + to:CONST["sin"].start + to + half], ALU.add, ALU.mult))
                own.wait()
                if factor != 1.0:
                    for table in ("cos", "sin"):
                        own.did(dve.tensor_scalar(tables[f"{table}_{name}"][:], tables[f"{table}_{name}"][:],
                                                  factor, None, ALU.mult))
                    own.wait()
            dve.tensor_copy(ident_b[:], net.const[:, CONST["ident"]]).then_inc(tables_ready, 1)
            dve.tensor_copy(mask[:], net.const[:, CONST["window"]].unsqueeze(1)
                            .broadcast_to([P, 4, P])).then_inc(tables_ready, 1)
            dve.wait_ge(rstd_ready, 1)
            normalise(0, 0)
            for item in FIRST_ITEMS:
                rotate(*item)
            pairs(dve, one)
            take_weights(NB - 1, 3)
            finish(NB - 1)


def cross(nc, net, sem):
    U, VW = 4, 32
    SCALE = float(XHD) ** -0.5
    ORDER = [("p", 2), ("p", 3), ("h", 0), ("p", 0), ("p", 1), ("o", 0)]
    TR, AV, PJ = 4, 6, 7

    def bank_of(what, u=0):
        return TR + ORDER.index((what, u)) % 2

    def number(what, t, u=0):
        if what == "h":
            return 0 if isinstance(t, int) and t == 0 else 5 * t - 4
        return 5 * t + 2 + u - (isinstance(t, int) and t == NB - 1)

    def begun(t, n):
        return not (isinstance(t, int) and t < n)

    with ExitStack() as ctx:
        def sb(name, shape, dt=F32):
            return ctx.enter_context(nc.sbuf_tensor(name, shape, dt))

        h_tok, h_t = sb("cr_h_tok", [P, 2, D]), sb("cr_h_t", [P, KC, P])
        context = sb("cr_context", [CTX, 2, P])
        qk, kbd = sb("cr_qk", [P, 2, 2, KC, P]), sb("cr_keys_diagonal", [P, 2, KC, 2, P])
        values = sb("cr_values", [P, 2, XHEADS, VW])
        weights, weights_t = sb("cr_weights", [P, U, BANK]), sb("cr_weights_t", [P, U, BANK])
        top, out_t = sb("cr_top", [P, 2, 4]), sb("cr_out_t", [P, BANK])
        rsum, out = sb("cr_rsum", [P, XHEADS]), sb("cr_out", [P, KC, U, 2, XHD])
        out_f = sb("cr_out_f", [P, KC, P])
        scratch = sb("cr_scratch", [P, NB])
        mask, ident_b = sb("cr_mask", [P, 4, P], BF16), sb("cr_ident", [P, P], BF16)
        ps = ctx.enter_context(nc.psum_tensor("cr_psum", [P, 8, BANK], F32))

        aggregated = sem("cr_aggregated")
        rstd_ready = sem("cr_rstd")
        tables_ready = sem("cr_tables")
        values_set = sem("cr_values_set")
        context_in = [sem(f"cr_context_in{s}") for s in range(2)]
        normed = sem("cr_normed")
        turned = sem("cr_turned")
        taken = sem("cr_taken")
        projected = sem("cr_projected")
        proj_taken = sem("cr_proj_taken")
        spread = sem("cr_spread")
        scored = sem("cr_scored")
        shifted = sem("cr_shifted")
        weighed = sem("cr_weighed")
        attended = sem("cr_attended")
        out_taken = sem("cr_out_taken")
        out_turned = sem("cr_out_turned")
        out_ready = sem("cr_out_ready")
        out_f_turned = sem("cr_out_f_turned")
        out_f_taken = sem("cr_out_f_taken")
        result = sem("cr_result")
        added = sem("cr_added")
        own_dve, own_pool = sem("cr_own_dve"), sem("cr_own_pool")
        block = ctx.enter_context(nc.Block("cross"))

        @block.sync
        def _(sp):
            def one(t, s, first, last):
                need(sp, projected, 2 * (t - 1))
                sp.dma_start(context[:, s], net.dram["ctx_t"][t]).then_inc(context_in[s], 16)

            pairs(sp, one)

        @block.gpsimd
        def _(pool):
            own = Own(pool, own_pool)
            pool.memset(values[:], 0.0).then_inc(values_set, 1)
            pool.wait_ge(values_set, 1)
            pool.memset(values[:, :, :, XHD:XHD + 1], 1.0).then_inc(values_set, 1)
            pool.wait_ge(aggregated, NB)
            inverse_root(pool, own, net.rstd[:], net.mean_var[:, :, 1], scratch[:], 1.0, LN_EPS,
                         net.half[:, 0:NB]).then_inc(rstd_ready, 1)

            def one(t, s, first, last):
                pool.wait_ge(proj_taken, 2 * t + 1)
                need(pool, scored, U * (t - 1))
                for c in range(KC):
                    pool.tensor_tensor(kbd[:, s, c], qk[:, s, 1, c:c + 1, :].broadcast_to([P, 2, P]),
                                       wide(net.const[:, CONST["half"]], [P, 2, P]), ALU.mult).then_inc(spread, 1)

            pairs(pool, one)

        @block.tensor
        def _(pe):
            ident = net.const[:, CONST["ident"]]

            def turn_h(t, s):
                pe.wait_ge(normed, t + 1)
                if begun(t, 2):
                    pe.wait_ge(taken, number("p", t - 2, 2) + 1)
                for c in range(KC):
                    mm = pe.transpose(ps[:, bank_of("h"), c * P:c * P + P], h_tok[:, s, c * P:c * P + P], ident)
                mm.then_inc(turned, 1)

            def project_qk(t, s):
                pe.wait_ge(taken, number("h", t) + 1)
                pe.wait_ge(context_in[s], (t - s) * 8 + 16)
                need(pe, added, t - 2)
                for oc in range(KC):
                    for c in range(KC):
                        pe.matmul(ps[:, PJ, oc * P:oc * P + P], net.xwq[:, c, oc * P:oc * P + P], h_t[:, c, :],
                                  start=(c == 0), stop=(c == KC - 1))
                for oc in range(KC):
                    mm = pe.matmul(ps[:, PJ, D + oc * P:D + oc * P + P], net.xwkv[:, oc * P:oc * P + P],
                                   context[:, s, :], start=True, stop=True)
                mm.then_inc(projected, 1)

            def project_v(t, s):
                pe.wait_ge(proj_taken, 2 * t + 1)
                pe.matmul(ps[:, PJ, 0:D], context[:, s, :], net.xwkv[:, D:2 * D],
                          start=True, stop=True).then_inc(projected, 1)

            def scores(t, s, u):
                if u == 0:
                    pe.wait_ge(spread, KC * (t + 1))
                need(pe, shifted, U * (t - 1) + u + 1)
                g = 32 * u
                pe.matmul(ps[:, u, :], ident_b[:], mask.rearrange("p j t -> p (j t)"), start=True, stop=False,
                          skip_group_check=True)
                for c in range(KC):
                    mm = pe.matmul(ps[:, u, c * D:c * D + D], qk[g:g + 32, s, 0, c, :], kbd[g:g + 32, s, c, :, :],
                                   start=False, stop=True, skip_group_check=True)
                mm.then_inc(scored, 1)

            def turn_weights(t, s, u):
                pe.wait_ge(weighed, U * t + u + 1)
                if u == 3:
                    need(pe, out_ready, KC * t)
                elif u == 2:
                    pe.wait_ge(taken, number("p", t, 1) + 1)
                elif u == 0:
                    need(pe, taken, number("p", t - 1, 3) + 1)
                else:
                    pe.wait_ge(taken, number("p", t, 0))
                for j in range(4):
                    mm = pe.transpose(ps[:, bank_of("p", u), j * P:j * P + P], weights[:, u, j * P:j * P + P], ident)
                mm.then_inc(turned, 1)

            def attend(t, s, u):
                pe.wait_ge(taken, number("p", t, u) + 1)
                if u == 0:
                    pe.wait_ge(proj_taken, 2 * t + 2)
                    need(pe, out_taken, t)
                for i in range(4):
                    c, j = i // 2, i % 2
                    mm = pe.matmul(ps[32 * i:32 * i + VW, AV, u * P:u * P + P], values[:, s, 8 * c + 2 * u + j, :],
                                   weights_t[:, u, i * P:i * P + P], start=True, stop=True)
                mm.then_inc(attended, 1)

            def turn_out(t):
                pe.wait_ge(out_taken, t + 1)
                pe.wait_ge(taken, number("p", t + 1, 0) + 1 if not (isinstance(t, int) and t == NB - 1)
                           else number("p", t, 3) + 1)
                for u in range(U):
                    mm = pe.transpose(ps[:, bank_of("o"), u * P:u * P + P], out_t[:, u * P:u * P + P], ident)
                mm.then_inc(out_turned, 1)

            def turn_out_f(t):
                pe.wait_ge(out_ready, KC * (t + 1))
                pe.wait_ge(proj_taken, 2 * (t + 3) if not (isinstance(t, int) and t >= NB - 2) else 2 * NB)
                if isinstance(t, int) and t == NB - 1:
                    pe.wait_ge(added, t)
                for c in range(KC):
                    mm = pe.transpose(ps[:, PJ, c * P:c * P + P], out.rearrange("p c u j d -> p c (u j d)")[:, c, :], ident)
                mm.then_inc(out_f_turned, 1)

            def project_out(t):
                pe.wait_ge(out_f_taken, t + 1)
                for c in range(KC):
                    mm = pe.matmul(ps[:, PJ, 0:D], out_f[:, c, :], net.xwout[:, c, :], start=(c == 0), stop=(c == KC - 1))
                mm.then_inc(result, 1)

            def one(t, s, first, last):
                for u in range(U):
                    scores(t, s, u)
                    if u >= 2 or not first:
                        turn_weights(*earlier(t, s, u, 2, U))
                    if u == 1 and not last:
                        turn_h(t + 1, 1 - s)
                    if u == 3 and not first:
                        turn_out(t - 1)
                    if u >= 3 or not first:
                        attend(*earlier(t, s, u, 3, U))
                    if u == 0 and begun(t, 2):
                        turn_out_f(t - 2)
                    if u == 1 and begun(t, 2):
                        project_out(t - 2)
                    if u == 2 and not last:
                        project_qk(t + 1, 1 - s)
                    if u == 3 and not last:
                        project_v(t + 1, 1 - s)

            pe.wait_ge(tables_ready, 2)
            pe.wait_ge(net.in_late, 16 * 6)
            turn_h(0, 0)
            project_qk(0, 0)
            project_v(0, 0)
            pairs(pe, one)
            t, s = NB - 1, 1
            turn_weights(t, s, 2)
            attend(t, s, 1)
            turn_out_f(t - 1)
            turn_weights(t, s, 3)
            attend(t, s, 2)
            project_out(t - 1)
            attend(t, s, 3)
            turn_out(t)
            turn_out_f(t)
            project_out(t)

        @block.scalar
        def _(act):
            def take_h(t):
                act.wait_ge(turned, number("h", t) + 1)
                need(act, projected, 2 * t - 1)
                act.activation(h_t.rearrange("p c t -> p (c t)"), ps[:, bank_of("h"), 0:D],
                               ACT.Copy).then_inc(taken, 1)

            def take_projected(t, s, n):
                act.wait_ge(projected, 2 * t + n + 1)
                if n == 0:
                    need(act, scored, U * (t - 1))
                    need(act, spread, KC * (t - 1))
                    act.activation(qk[:, s].rearrange("p m c t -> p (m c t)"), ps[:, PJ, :],
                                   ACT.Copy).then_inc(proj_taken, 1)
                else:
                    need(act, attended, U * (t - 1))
                    act.activation(values[:, s, :, 0:XHD], ps[:, PJ, 0:D].rearrange("p (h d) -> p h d", d=XHD),
                                   ACT.Copy).then_inc(proj_taken, 1)

            def weigh(t, u):
                act.wait_ge(shifted, U * t + u + 1)
                act.activation(weights[:, u], weights[:, u], ACT.Exp, scale=SCALE).then_inc(weighed, 1)

            def take_weights(t, s, u):
                act.wait_ge(turned, number("p", t, u) + 1)
                need(act, attended, U * (t - 1) + u + 1)
                act.activation(weights_t[:, u], ps[:, bank_of("p", u), :], ACT.Copy).then_inc(taken, 1)

            def take_out(t):
                act.wait_ge(attended, U * (t + 1))
                need(act, out_turned, t)
                act.activation(out_t[:], ps[:, AV, :], ACT.Copy).then_inc(out_taken, 1)

            def take_out_f(t):
                act.wait_ge(out_f_turned, t + 1)
                act.activation(out_f.rearrange("p c t -> p (c t)"), ps[:, PJ, 0:D],
                               ACT.Copy).then_inc(out_f_taken, 1)

            def one(t, s, first, last):
                for u in range(U):
                    weigh(t, u)
                    if u >= 2 or not first:
                        take_weights(*earlier(t, s, u, 2, U))
                    if u == 1 and not last:
                        take_h(t + 1)
                    if u == 0 and begun(t, 2):
                        take_out_f(t - 2)
                    if u == 2 and not first:
                        take_out(t - 1)
                    if u == 2 and not last:
                        take_projected(t + 1, 1 - s, 0)
                    if u == 3 and not last:
                        take_projected(t + 1, 1 - s, 1)

            act.wait_ge(values_set, 2)
            take_h(0)
            take_projected(0, 0, 0)
            take_projected(0, 0, 1)
            pairs(act, one)
            t, s = NB - 1, 1
            take_weights(t, s, 2)
            take_out_f(t - 1)
            take_weights(t, s, 3)
            take_out(t)
            take_out_f(t)

        @block.vector
        def _(dve):
            own = Own(dve, own_dve)

            def link(instruction):
                own.wait(own.did(instruction))

            def normalise(t, s):
                if begun(t, 2):
                    dve.wait_ge(turned, number("h", t - 2) + 1)
                dve.tensor_scalar(h_tok[:, s, :], net.x[:, t, :], net.mean_var[:, t, 0:1],
                                  net.rstd[:, bass.ds(t, 1)], ALU.subtract, ALU.mult).then_inc(normed, 1)

            def shift(t, s, u):
                dve.wait_ge(scored, U * t + u + 1)
                rows = ps[:, u, :].rearrange("p (j t) -> p j t", t=P)
                link(dve.tensor_reduce(top[:, u % 2, :], rows, AX.X, ALU.max))
                if begun(t, 1):
                    dve.wait_ge(turned, number("p", t - 1, u) + 1)
                dve.tensor_tensor(weights[:, u].rearrange("p (j t) -> p j t", t=P), rows,
                                  wide(top[:, u % 2, :], [P, 4, P]), ALU.subtract).then_inc(shifted, 1)

            def divide(t):
                dve.wait_ge(out_turned, t + 1)
                heads = ps[:, bank_of("o"), :].rearrange("p (h v) -> p h v", v=VW)
                link(dve.reciprocal(rsum[:], heads[:, :, XHD]))
                need(dve, out_f_turned, t)
                by_unit = ps[:, bank_of("o"), :].rearrange("p (u c j v) -> p c u j v", u=U, c=KC, v=VW)
                shares = rsum.rearrange("p (u c j) -> p c u j", u=U, c=KC)
                for c in range(KC):
                    dve.tensor_tensor(out[:, c], by_unit[:, c, :, :, 0:XHD], wide(shares[:, c], [P, U, 2, XHD]),
                                      ALU.mult).then_inc(out_ready, 1)

            def finish(t):
                dve.wait_ge(result, t + 1)
                dve.tensor_tensor(net.x[:, t, :], net.x[:, t, :], ps[:, PJ, 0:D], ALU.add).then_inc(added, 1)
                dve.wait_ge(added, t + 1)
                own.did(dve.bn_stats(net.stats[:, t, :], net.x[:, t, :]))

            def one(t, s, first, last):
                for u in range(U):
                    shift(t, s, u)
                    if u == 0 and not last:
                        normalise(t + 1, 1 - s)
                    if u == 1 and begun(t, 2):
                        finish(t - 2)
                    if u == 3 and not first:
                        divide(t - 1)
                own.again()

            aggregate(dve, net, aggregated)
            dve.tensor_copy(ident_b[:], net.const[:, CONST["ident"]]).then_inc(tables_ready, 1)
            dve.tensor_copy(mask[:], net.const[:, CONST["causal"]].unsqueeze(1)
                            .broadcast_to([P, 4, P])).then_inc(tables_ready, 1)
            dve.wait_ge(rstd_ready, 1)
            normalise(0, 0)
            pairs(dve, one)
            finish(NB - 2)
            divide(NB - 1)
            finish(NB - 1)


def silu_ffn(nc, net, sem):
    with ExitStack() as ctx:
        def sb(name, shape, dt=F32):
            return ctx.enter_context(nc.sbuf_tensor(name, shape, dt))

        h_tok, h_t = sb("ff_h_tok", [P, GB, D]), sb("ff_h_t", [P, KC, GB * P])
        gated, hidden = sb("ff_gated", [P, 2, BANK]), sb("ff_hidden", [P, 2, BANK])
        scratch = sb("ff_scratch", [P, NB])
        ps = ctx.enter_context(nc.psum_tensor("ff_psum", [P, 8, BANK], F32))
        DOWN, TURN = 4, 6

        aggregated = sem("ff_aggregated")
        rstd_ready = sem("ff_rstd")
        normed = sem("ff_normed")
        turned = sem("ff_turned")
        taken = sem("ff_taken")
        gate_full, up_full = sem("ff_gate_full"), sem("ff_up_full")
        silu_done = sem("ff_silu_done")
        hidden_ready = sem("ff_hidden_ready")
        down_done = sem("ff_down_done")
        added = sem("ff_added")
        stored = sem("ff_stored")
        block = ctx.enter_context(nc.Block("silu_ffn"))

        @block.sync
        def _(sp):
            with sp.Fori(0, NG) as g:
                sp.wait_ge(added, GB * (g + 1))
                sp.dma_start(net.dram["out"].rearrange("(g j) t d -> g t j d", j=GB)[g],
                             net.x.rearrange("p (g j) d -> p g j d", j=GB)[:, g]).then_inc(stored, 16)
            sp.wait_ge(stored, 16 * NG)

        @block.gpsimd
        def _(pool):
            own = Own(pool, net.own_last)
            pool.wait_ge(aggregated, NB)
            inverse_root(pool, own, net.rstd[:], net.mean_var[:, :, 1], scratch[:], 1.0, LN_EPS,
                         net.half[:, 0:NB]).then_inc(rstd_ready, 1)

        @block.tensor
        def _(pe):
            ident = net.const[:, CONST["ident"]]

            def turn(g):
                pe.wait_ge(normed, g + 1)
                need(pe, taken, KC * g)
                for c in range(KC):
                    for j in range(GB):
                        mm = pe.transpose(ps[:, TURN + c, j * P:j * P + P], h_tok[:, j, c * P:c * P + P], ident)
                mm.then_inc(turned, 1)

            def gate_up(g, q):
                if q == 0:
                    pe.wait_ge(taken, KC * (g + 1))
                need(pe, hidden_ready, HC * g + q - 1)
                for m, (w, full) in enumerate(((net.gate1, gate_full), (net.up1, up_full))):
                    for c in range(KC):
                        mm = pe.matmul(ps[:, 2 * (q % 2) + m, :], w[:, c, q * P:q * P + P], h_t[:, c, :],
                                       start=(c == 0), stop=(c == KC - 1))
                    mm.then_inc(full, 1)

            def down(g, q):
                pe.wait_ge(hidden_ready, HC * g + q + 1)
                if q == 0:
                    need(pe, added, GB * g)
                for j in range(GB):
                    mm = pe.matmul(ps[:, DOWN + j // 2, (j % 2) * D:(j % 2) * D + D],
                                   hidden[:, q % 2, j * P:j * P + P], net.down1[:, q, :],
                                   start=(q == 0 and j % 2 == 0), stop=(q == HC - 1), skip_group_check=True)
                mm.then_inc(down_done, 1)

            def one(g, first, last):
                for q in range(HC):
                    gate_up(g, q)
                    if q > 0:
                        down(g, q - 1)
                if not last:
                    turn(g + 1)
                down(g, HC - 1)

            pe.wait_ge(net.in_late, 16 * 6)
            turn(0)
            rounds(pe, one)

        @block.scalar
        def _(act):
            def take(g):
                act.wait_ge(turned, g + 1)
                need(act, up_full, HC * g)
                for c in range(KC):
                    act.activation(h_t[:, c, :], ps[:, TURN + c, :], ACT.Copy).then_inc(taken, 1)

            def one(g, first, last):
                for q in range(HC):
                    act.wait_ge(gate_full, HC * g + q + 1)
                    need(act, hidden_ready, HC * g + q - 1)
                    act.activation(gated[:, q % 2, :], ps[:, 2 * (q % 2), :], ACT.Silu).then_inc(silu_done, 1)
                if not last:
                    take(g + 1)

            take(0)
            rounds(act, one)

        @block.vector
        def _(dve):
            def normalise(g):
                need(dve, turned, g)
                for j in range(GB):
                    b = GB * g + j
                    h = dve.tensor_scalar(h_tok[:, j, :], net.x[:, b, :], net.mean_var[:, b, 0:1],
                                          net.rstd[:, bass.ds(b, 1)], ALU.subtract, ALU.mult)
                h.then_inc(normed, 1)

            def finish(g):
                dve.wait_ge(down_done, HC * (g + 1))
                for j in range(GB):
                    b = GB * g + j
                    dve.tensor_tensor(net.x[:, b, :], net.x[:, b, :],
                                      ps[:, DOWN + j // 2, (j % 2) * D:(j % 2) * D + D], ALU.add).then_inc(added, 1)

            def one(g, first, last):
                for q in range(HC):
                    dve.wait_ge(silu_done, HC * g + q + 1)
                    dve.wait_ge(up_full, HC * g + q + 1)
                    need(dve, down_done, HC * g + q - 1)
                    dve.tensor_tensor(hidden[:, q % 2, :], gated[:, q % 2, :], ps[:, 2 * (q % 2) + 1, :],
                                      ALU.mult).then_inc(hidden_ready, 1)
                    if q == 0 and not first:
                        finish(g - 1)
                    if q == 2 and not last:
                        normalise(g + 1)

            aggregate(dve, net, aggregated)
            dve.wait_ge(rstd_ready, 1)
            normalise(0)
            rounds(dve, one)
            finish(NG - 1)


def decoder(nc, dram):
    with ExitStack() as ctx:
        def sb(name, shape, dt=F32):
            return ctx.enter_context(nc.sbuf_tensor(name, shape, dt))

        def sem(name):
            return ctx.enter_context(nc.semaphore(name))

        net = Net()
        net.dram = dram
        net.fvec, net.rows, net.const = sb("fvec", [P, KC * len(FVEC)]), sb("rows", [P, ROWS_N]), sb("const", [P, CONST_N])
        net.x, net.ctx = sb("x", [P, NB, D]), sb("ctx", [P, NB, CTX])
        net.stats = sb("stats", [P, NB, 6])
        net.mean_var, net.rstd = sb("mean_var", [P, NB, 2]), sb("rstd", [P, NB])
        net.ones, net.half = sb("ones", [P, P]), sb("minus_half", [P, NB * EXPERTS])
        net.rwkv_w, net.router_w = sb("rwkv_w", [P, 4, KC, D]), sb("router_w", [P, KC, EXPERTS])
        net.wq, net.wk = sb("wq", [P, KC, HEADS * DH]), sb("wk", [P, KC, KVH * DH])
        net.wv, net.wo = sb("wv", [P, KC, KVH * DH]), sb("wo", [P, HEADS, D])
        net.in_small, net.in_rwkv, net.in_ctx = sem("in_small"), sem("in_rwkv"), sem("in_ctx")
        net.in_ffn0, net.in_attn1, net.in_late = sem("in_ffn0"), sem("in_attn1"), sem("in_late")
        net.in_x = [sem(f"in_x{g}") for g in range(NG)]
        with ExitStack() as early:
            def early_sb(name, shape):
                return early.enter_context(nc.sbuf_tensor(name, shape, F32))

            net.gate0, net.up0 = early_sb("gate0", [P, KC, HIDDEN]), early_sb("up0", [P, KC, HIDDEN])
            net.egate, net.eup = early_sb("egate", [P, KC, HIDDEN]), early_sb("eup", [P, KC, HIDDEN])
            net.down0, net.edown = early_sb("down0", [P, HC, D]), early_sb("edown", [P, EXPERTS, D])
            first(nc, net, sem)
            for sublayer in (rwkv, gqa, experts):
                sublayer(nc, net, sem)
        net.xwq, net.xwout = sb("xwq", [P, KC, D]), sb("xwout", [P, KC, D])
        net.xwkv, net.own_last = sb("xwkv", [CTX, 2 * D]), sem("own_last")
        net.gate1, net.up1, net.down1 = sb("gate1", [P, KC, HIDDEN]), sb("up1", [P, KC, HIDDEN]), sb("down1", [P, HC, D])
        for sublayer in (windowed, cross, silu_ffn):
            sublayer(nc, net, sem)


def constants():
    const = np.zeros((P, CONST_N), np.float32)
    p = np.arange(P)
    const[:, CONST["ident"]] = np.eye(P)
    inv_freq = (1.0 / np.float32(THETA) ** (np.arange(0, DH, 2, dtype=np.float32) / np.float32(DH))).astype(np.float32)
    angle = p[:, None].astype(np.float32) * inv_freq[None, :]
    const[:, CONST["cos"]] = np.tile(np.cos(angle.astype(np.float64)), 2)
    const[:, CONST["sin"]] = np.concatenate([-np.sin(angle.astype(np.float64)), np.sin(angle.astype(np.float64))], 1)
    distance = p[:, None] - p[None, :]
    const[:, CONST["window"]] = np.where((distance >= 0) & (distance <= WINDOW), 0.0, FAR)
    const[:, CONST["causal"]] = np.where(distance >= 0, 0.0, FAR)
    const[:, CONST["odd"]] = (p[:, None] // HD) % 2
    const[:, CONST["half"]] = (p[:, None] // XHD) % 2 == np.arange(2)[None, :]
    e = np.arange(EXPERTS)
    const[:, CONST["before"]] = (e[None, :] < e[:, None]).reshape(1, -1)
    return const


def laid_out(inputs):
    a = {n: np.asarray(v) for n, v in inputs.items()}

    def chunks(w):
        return w.reshape(-1, P, w.shape[-1]).transpose(1, 0, 2)

    ctx = a["ctx_512"]
    keys = ctx.reshape(NB, P, KV_HEADS, HD).transpose(0, 3, 2, 1).reshape(NB, 1, HD, KV_HEADS * P)
    return {
        "x": a["x"], "ctx": ctx,
        "ctx_keys": np.broadcast_to(keys, (NB, P // HD, HD, KV_HEADS * P)).reshape(NB, P, -1),
        "ctx_t": ctx.transpose(0, 2, 1),
        "fvec": np.stack([a[n].reshape(KC, P) for n in FVEC]).transpose(2, 0, 1).reshape(P, -1),
        "rows": np.broadcast_to(np.concatenate([a[n] for n in ROWS]), (P, ROWS_N)),
        "const": constants(),
        "rwkv_w": np.stack([chunks(a[f"L0_attn_W{n}"].T) for n in "kvro"], 1),
        "router_w": chunks(a["L0_ffn_router_w"]),
        "gate0": chunks(a["L0_ffn_w_gate"]), "up0": chunks(a["L0_ffn_w_up"]), "down0": chunks(a["L0_ffn_w_down"]),
        "egate": chunks(a["L0_ffn_we_gate"].transpose(1, 0, 2).reshape(D, -1)),
        "eup": chunks(a["L0_ffn_we_up"].transpose(1, 0, 2).reshape(D, -1)),
        "edown": a["L0_ffn_we_down"].transpose(1, 0, 2),
        "wq": chunks(a["L1_attn_Wq"].T), "wk": chunks(a["L1_attn_Wk"].T), "wv": chunks(a["L1_attn_Wv"].T),
        "wo": chunks(a["L1_attn_Wo"].T),
        "xwq": chunks(a["L1_xattn_Wq"].T), "xwkv": a["L1_xattn_Wkv_expand"].T, "xwout": chunks(a["L1_xattn_Wout"].T),
        "gate1": chunks(a["L1_ffn_w_gate"].T), "up1": chunks(a["L1_ffn_w_up"].T), "down1": chunks(a["L1_ffn_w_down"].T),
    }


def kernel(**inputs):
    import concourse.bacc as bacc
    from concourse.bass_utils import run_bass_kernel_spmd

    nc = bacc.Bacc("TRN2", target_bir_lowering=False, num_devices=1)
    arrays, dram = {}, {}
    for name, a in laid_out(inputs).items():
        a = np.ascontiguousarray(a)
        arrays[f"in_{name}_dram"] = a
        dram[name] = nc.dram_tensor(f"in_{name}_dram", a.shape, mybir.dt.from_np(a.dtype), kind="ExternalInput").ap()
    dram["out"] = nc.dram_tensor("out_0_dram", (NB, P, D), F32, kind="ExternalOutput").ap()
    decoder(nc, dram)
    r = run_bass_kernel_spmd(nc, [arrays], core_ids=[0])
    return r.results[0]["out_0_dram"]
```

```python
from contextlib import ExitStack

import numpy as np

import concourse.bass as bass
from concourse import mybir

ALU = mybir.AluOpType
ACT = mybir.ActivationFunctionType
AX = mybir.AxisListType
F32 = mybir.dt.float32
BF16 = mybir.dt.bfloat16
F32R = mybir.dt.float32r

P = 128
NB = 16
D = 256
KC = D // P
GB = 4
NG = NB // GB
BANK = 512
LN_EPS = 1e-5
RMS_EPS = 1e-6
FAR = -1e30

ROW = P + 1
CHUNK = GB * ROW
Q_HEADS, KV_HEADS, HD = 32, 8, 8
CTX = KV_HEADS * HD
HIDDEN = 1024
HC = HIDDEN // P
EXPERTS, TOP = 8, 2
HEADS, KVH, DH = 16, 4, 128
WINDOW, THETA = 64, 10000.0
XHEADS, XHD = 16, 16

FVEC = ["L0_attn_bk", "L0_attn_bv", "L0_attn_br", "L0_attn_tmk", "L0_attn_tmv", "L0_attn_tmr",
        "L0_attn_time_decay", "L0_attn_time_first", "L0_ffn_rn_pre1", "L0_ffn_rn_pre2",
        "L0_ffn_router_scale"]
BK, BV, BR, TMK, TMV, TMR, DECAY, FIRST, PRE1, PRE2, RSCALE = (2 * i for i in range(len(FVEC)))
ROWS = {}
_at = 0
for _name, _n in (("L0_attn_bo", D), ("L0_ffn_rn_post1", D), ("L0_ffn_rn_post2", D),
                  ("L0_ffn_rn_post", D), ("L1_attn_qn_w", DH), ("L1_attn_kn_w", DH),
                  ("L0_ffn_per_expert_scale", EXPERTS)):
    ROWS[_name] = slice(_at, _at + _n)
    _at += _n
ROWS_N = _at
CONST = {}
_at = 0
for _name, _n in (("ident", P), ("cos", P), ("sin", P), ("window", P), ("causal", P),
                  ("odd", 1), ("half", 2), ("before", EXPERTS * EXPERTS)):
    CONST[_name] = slice(_at, _at + _n)
    _at += _n
CONST_N = _at


class Net:
    pass


def need(engine, sem, count):
    if not isinstance(count, int) or count > 0:
        engine.wait_ge(sem, count)


class Own:

    def __init__(self, engine, sem):
        self.engine, self.sem, self.n = engine, sem, 0

    def did(self, instruction):
        instruction.then_inc(self.sem, 1)
        self.n += 1
        return self.n

    def wait(self, n=None):
        self.engine.wait_ge(self.sem, self.n if n is None else n)

    def again(self):
        self.wait()
        self.engine.sem_clear(self.sem)
        self.n = 0


def wide(column, shape):
    return column.unsqueeze(len(shape) - 1).broadcast_to(shape)


def in_place(nc, name, place, shape):
    return nc.alloc_sbuf_tensor_at(name, shape, F32R, offset=place)


def rounds(engine, one):
    one(0, True, False)
    with engine.Fori(1, NG - 1) as g:
        one(g, False, False)
    one(NG - 1, False, True)


def load(nc, net):
    sp, dram = nc.sync, net.dram
    sp.dma_start(net.fvec[:], dram["fvec"]).then_inc(net.in_small, 16)
    sp.dma_start(net.const[:], dram["const"]).then_inc(net.in_small, 16)
    sp.dma_start(net.rows[:], dram["rows"]).then_inc(net.in_small, 16)
    for g in range(NG):
        sp.dma_start(net.x[:, GB * g:GB * g + GB, :],
                     dram["x"].rearrange("b t d -> t b d")[:, GB * g:GB * g + GB, :]).then_inc(net.in_x[g], 16)
        if g == 0:
            sp.dma_start(net.rwkv_w[:], dram["rwkv_w"]).then_inc(net.in_rwkv, 16)
    sp.dma_start(net.ctx[:], dram["ctx"].rearrange("b t d -> t b d")).then_inc(net.in_ctx, 16)
    sp.dma_start(net.router_w[:], dram["router_w"]).then_inc(net.in_ffn0, 16)
    for tile, source in ((net.gate0, dram["gate0"]), (net.up0, dram["up0"]), (net.down0, dram["down0"]),
                         (net.egate, dram["egate"]), (net.eup, dram["eup"]), (net.edown, dram["edown"])):
        sp.dma_start(tile[:], source).then_inc(net.in_ffn0, 16)
    for tile, source in ((net.wq, dram["wq"]), (net.wk, dram["wk"]), (net.wv, dram["wv"]), (net.wo, dram["wo"])):
        sp.dma_start(tile[:], source).then_inc(net.in_attn1, 16)


def load_late(nc, net):
    for tile, source in ((net.xwq, net.dram["xwq"]), (net.xwkv, net.dram["xwkv"]), (net.xwout, net.dram["xwout"]),
                         (net.gate1, net.dram["gate1"]), (net.up1, net.dram["up1"]), (net.down1, net.dram["down1"])):
        nc.sync.dma_start(tile[:], source).then_inc(net.in_late, 16)


def aggregate(dve, net, done):
    for b in range(NB):
        dve.bn_aggr(net.mean_var[:, b, :], net.stats[:, b, :]).then_inc(done, 1)


def inverse_root(pool, own, out, value, scratch, scale, eps, half):
    own.wait(own.did(pool.tensor_scalar(scratch, value, scale, eps, ALU.mult, ALU.add)))
    return pool.tensor_tensor(out, scratch, half, ALU.pow)


def scale_of(pool, own, net, scratch, aggregated, ready, first, end):
    of = slice(first, end)
    pool.wait_ge(aggregated, end)
    inverse_root(pool, own, net.rstd[:, of], net.mean_var[:, of, 1], scratch[:, of], 1.0, LN_EPS,
                 net.half[:, of]).then_inc(ready, 1)


def layer_norm_scale(pool, own, net, scratch, aggregated, ready, head):
    for first, end in ((0, head), (head, NB)):
        scale_of(pool, own, net, scratch, aggregated, ready, first, end)


def rwkv(nc, net, sem):
    with ExitStack() as ctx:
        def sb(name, shape, dt=F32):
            return ctx.enter_context(nc.sbuf_tensor(name, shape, dt))

        row_tile = [P, KC * GB * ROW]
        h_tok = sb("rw_h_tok", [P, GB, D])
        hp = sb("rw_h_padded", row_tile)
        diff, peak = sb("rw_diff", [P, KC, GB * P]), sb("rw_peak", [P, KC, GB * P])
        w_mix = sb("rw_w_mix", [P, 3, KC, D])
        k, v, er = sb("rw_k", row_tile), sb("rw_v", row_tile), sb("rw_exp_minus_r", row_tile)
        decay = sb("rw_decay", row_tile)
        state = {n: sb(f"rw_{n}", [P, KC * GB * ROW + 1]) for n in ("pp", "aa", "bb")}
        e1, e2, e2v = sb("rw_e1", row_tile), sb("rw_e2", row_tile), sb("rw_e2v", row_tile)
        f1, f2 = sb("rw_f1", row_tile), sb("rw_f2", row_tile)
        rw = sb("rw_out", [P, KC, GB * P])
        neg_br, exp_decay = sb("rw_neg_br", [P, KC]), sb("rw_exp_decay", [P, KC])
        scratch = sb("rw_scratch", [P, NB])
        ps = ctx.enter_context(nc.psum_tensor("rw_psum", [P, 8, BANK], F32))

        preset = sem("rw_preset")
        decay_exp = sem("rw_decay_exp")
        constants = sem("rw_constants")
        aggregated = sem("rw_aggregated")
        rstd_ready = sem("rw_rstd")
        normed = sem("rw_normed")
        turned = sem("rw_turned")
        padded = sem("rw_padded")
        w_mixed = sem("rw_w_mixed")
        differed = sem("rw_differed")
        projected = sem("rw_projected")
        taken = sem("rw_taken")
        exponent = sem("rw_exponent")
        weight = sem("rw_weight")
        v_read, er_read = sem("rw_v_read"), sem("rw_er_read")
        rw_ready = sem("rw_ready")
        out_ready = sem("rw_out_ready")
        added = sem("rw_added")
        own_dve, own_pool, own_act = sem("rw_own_dve"), sem("rw_own_pool"), sem("rw_own_act")
        block = ctx.enter_context(nc.Block("rwkv"))

        @block.sync
        def _(sp):
            load(nc, net)

        def flat(tile):
            return tile[:, 0:KC * GB * ROW]

        def tokens(tile, back=0, c=None):
            rows = flat(tile).rearrange("p (g w) -> p g w", w=ROW)[:, :, 1 - back:ROW - back]
            return rows if c is None else rows[:, GB * c:GB * c + GB, :]

        def now(name, c=None):
            rows = state[name][:, 1:1 + KC * GB * ROW].rearrange("p (g w) -> p g w", w=ROW)[:, :, 1:ROW]
            return rows if c is None else rows[:, GB * c:GB * c + GB, :]

        def before(name, c=None):
            return tokens(state[name], 0, c)

        def pads(tile):
            return flat(tile).rearrange("p (g w) -> p g w", w=ROW)[:, :, 0:1]

        def by_row(tile, c=None):
            rows = tile.rearrange("p c (j t) -> p (c j) t", t=P)
            return rows if c is None else rows[:, GB * c:GB * c + GB, :]

        def col(base, c):
            return net.fvec[:, base + c:base + c + 1]

        @block.gpsimd
        def _(pool):
            own = Own(pool, own_pool)
            for tile, value in ((hp, 0.0), (e1, 0.0), (e2, 0.0), (e2v, 0.0), (k, FAR), (decay, 0.0)):
                pool.memset(tile[:], value).then_inc(preset, 1)
            pool.memset(net.ones[:], 1.0).then_inc(preset, 1)
            pool.memset(state["pp"][:, 0:1], FAR).then_inc(preset, 1)
            for name in ("aa", "bb"):
                pool.memset(state[name][:, 0:1], 0.0).then_inc(preset, 1)
            own.did(pool.memset(net.half[:], -0.5))
            own.wait(own.n)
            scale_of(pool, own, net, scratch, aggregated, rstd_ready, 0, GB)

            def differ(g, first, last):
                pool.wait_ge(padded, KC * (g + 1))
                need(pool, projected, 3 * g)
                pool.tensor_tensor(by_row(diff[:]), tokens(hp), tokens(hp, 1), ALU.subtract).then_inc(differed, 1)
                if first:
                    scale_of(pool, own, net, scratch, aggregated, rstd_ready, GB, NB)

            rounds(pool, differ)

        @block.tensor
        def _(pe):
            def turn(g):
                pe.wait_ge(normed, g + 1)
                need(pe, added, GB * (g - 1))
                need(pe, padded, KC * g)
                for c in range(KC):
                    for j in range(GB):
                        mm = pe.transpose(ps[:, c, j * P:j * P + P], h_tok[:, j, c * P:c * P + P], ident)
                mm.then_inc(turned, 1)

            def project(g, which):
                pe.wait_ge(padded, KC * (g + 1))
                for m in which:
                    need(pe, taken, 3 * KC * (g - 1) + KC * (m + 1))
                    for oc in range(KC):
                        for c in range(KC):
                            pe.matmul(ps[:, 2 + 2 * m + oc, :].rearrange("p (j t) -> p j t", t=P),
                                      net.rwkv_w[:, m, c, oc * P:oc * P + P], tokens(hp, 1, c),
                                      start=(c == 0), stop=False)
                    pe.wait_ge(differed, g + 1)
                    if isinstance(g, int) and g == 0:
                        pe.wait_ge(w_mixed, KC * (m + 1))
                    for oc in range(KC):
                        for c in range(KC):
                            mm = pe.matmul(ps[:, 2 + 2 * m + oc, :], w_mix[:, m, c, oc * P:oc * P + P], diff[:, c, :],
                                           start=False, stop=(c == KC - 1))
                    mm.then_inc(projected, 1)

            def output(g, h_padded):
                pe.wait_ge(rw_ready, g + 1)
                pe.wait_ge(padded, h_padded)
                need(pe, added, GB * g)
                for j in range(GB):
                    out = ps[:, j // 2, (j % 2) * D:(j % 2) * D + D]
                    for c in range(KC):
                        pe.matmul(out, rw[:, c, j * P:j * P + P], net.rwkv_w[:, 3, c, :],
                                  start=(c == 0), stop=False)
                    mm = pe.matmul(out, net.ones[0:1, 0:P], net.rows[0:1, ROWS["L0_attn_bo"]],
                                   start=False, stop=True)
                    if j % 2 == 1:
                        mm.then_inc(out_ready, 1)

            ident = net.const[:, CONST["ident"]]
            pe.wait_ge(net.in_small, 16 * 3)
            pe.wait_ge(net.in_rwkv, 16)
            pe.wait_ge(preset, 10)
            def one(g, first, last):
                if not last:
                    turn(g + 1)
                    project(g + 1, (0, 1))
                output(g, KC * (g + 2 - last))
                if not last:
                    project(g + 1, (2,))

            turn(0)
            project(0, (0, 1, 2))
            rounds(pe, one)

        @block.scalar
        def _(act):
            def pad_h(g):
                act.wait_ge(turned, g + 1)
                need(act, projected, 3 * g)
                for c in range(KC):
                    act.activation(tokens(hp, 0, c), ps[:, c, :].rearrange("p (j t) -> p j t", t=P),
                                   ACT.Copy).then_inc(padded, 1)

            def take(g, m):
                tile, func, bias, scale, read, times = (
                    (k, ACT.Identity, lambda c: col(BK, c), 1.0, exponent, 2 * 4),
                    (v, ACT.Identity, lambda c: col(BV, c), 1.0, v_read, 1),
                    (er, ACT.Exp, lambda c: neg_br[:, c:c + 1], -1.0, er_read, 1))[m]
                act.wait_ge(projected, 3 * g + m + 1)
                need(act, read, times * g)
                for c in range(KC):
                    act.activation(tokens(tile, 0, c),
                                   ps[:, 2 + 2 * m + c, :].rearrange("p (j t) -> p j t", t=P),
                                   func, bias=bias(c), scale=scale).then_inc(taken, 1)

            def weigh(g, n, tile):
                act.wait_ge(exponent, 2 * 4 * g + 2 * (n + 1))
                act.activation(tokens(tile), tokens(tile), ACT.Exp).then_inc(weight, 1)

            act.wait_ge(net.in_small, 16 * 3)
            act.activation(exp_decay[:], net.fvec[:, DECAY:DECAY + KC], ACT.Exp).then_inc(decay_exp, 1)
            act.wait_ge(constants, 1)
            act.wait_ge(preset, 10)

            def one(g, first, last):
                take(g, 0)
                take(g, 1)
                weigh(g, 0, e1)
                weigh(g, 1, e2)
                weigh(g, 2, f1)
                weigh(g, 3, f2)
                if not last:
                    pad_h(g + 1)
                take(g, 2)

            pad_h(0)
            rounds(act, one)

        @block.vector
        def _(dve):
            own = Own(dve, own_dve)

            def link(instruction):
                own.wait(own.did(instruction))

            def normalise(g):
                need(dve, turned, g)
                for j in range(GB):
                    b = GB * g + j
                    h = dve.tensor_scalar(h_tok[:, j, :], net.x[:, b, :], net.mean_var[:, b, 0:1],
                                          net.rstd[:, bass.ds(b, 1)], ALU.subtract, ALU.mult)
                h.then_inc(normed, 1)

            def scan(g, more, first):
                dve.wait_ge(taken, 3 * KC * g + KC)
                link(dve.tensor_tensor_scan(state["pp"][:, 1:], flat(decay), flat(k), FAR, ALU.add, ALU.max))
                need(dve, rw_ready, g)
                for c in range(KC):
                    dve.scalar_tensor_tensor(tokens(e1, 0, c), before("pp", c), neg_exp_decay(c),
                                             now("pp", c), ALU.add, ALU.subtract).then_inc(exponent, 1)
                for c in range(KC):
                    dve.tensor_tensor(tokens(e2, 0, c), tokens(k, 0, c), now("pp", c),
                                      ALU.subtract).then_inc(exponent, 1)
                if more is not None:
                    normalise(more)
                for c in range(KC):
                    own.did(dve.scalar_tensor_tensor(by_row(peak[:], c), tokens(k, 0, c), col(FIRST, c),
                                                     before("pp", c), ALU.add, ALU.max))
                own.wait()
                for c in range(KC):
                    dve.tensor_tensor(tokens(f1, 0, c), before("pp", c), by_row(peak[:], c),
                                      ALU.subtract).then_inc(exponent, 1)
                for c in range(KC):
                    dve.scalar_tensor_tensor(tokens(f2, 0, c), tokens(k, 0, c), col(FIRST, c),
                                             by_row(peak[:], c), ALU.add, ALU.subtract).then_inc(exponent, 1)
                if not first:
                    add(g - 1)
                dve.wait_ge(weight, 4 * g + 2)
                dve.wait_ge(taken, 3 * KC * g + 2 * KC)
                link(dve.tensor_tensor(tokens(e2v), tokens(e2), tokens(v), ALU.mult))
                link(dve.tensor_tensor_scan(state["aa"][:, 1:], flat(e1), flat(e2v), 0.0, ALU.mult, ALU.add))
                own.did(dve.tensor_tensor_scan(state["bb"][:, 1:], flat(e1), flat(e2), 0.0, ALU.mult, ALU.add))
                dve.wait_ge(weight, 4 * g + 4)
                own.wait()
                own.did(dve.tensor_tensor(tokens(e1), tokens(f1), before("aa"), ALU.mult))
                dve.tensor_tensor(tokens(e2v), tokens(f2), tokens(v), ALU.mult).then_inc(v_read, 1)
                own.did(dve.tensor_tensor(tokens(e2), tokens(f1), before("bb"), ALU.mult))
                own.wait(own.n - 1)
                dve.wait_ge(v_read, g + 1)
                own.did(dve.tensor_tensor(tokens(e1), tokens(e1), tokens(e2v), ALU.add))
                own.wait(own.n - 1)
                link(dve.tensor_tensor(tokens(e2), tokens(e2), tokens(f2), ALU.add))
                dve.wait_ge(taken, 3 * KC * (g + 1))
                dve.scalar_tensor_tensor(tokens(e2), tokens(er), 1.0, tokens(e2), ALU.add,
                                         ALU.mult).then_inc(er_read, 1)
                dve.wait_ge(er_read, g + 1)
                link(dve.reciprocal(tokens(e2), tokens(e2)))
                need(dve, out_ready, 2 * g)
                dve.tensor_tensor(by_row(rw[:]), tokens(e1), tokens(e2), ALU.mult).then_inc(rw_ready, 1)

            def add(g):
                for j in range(GB):
                    dve.wait_ge(out_ready, 2 * g + j // 2 + 1)
                    b = GB * g + j
                    dve.tensor_tensor(net.x[:, b, :], net.x[:, b, :], ps[:, j // 2, (j % 2) * D:(j % 2) * D + D],
                                      ALU.add).then_inc(added, 1)
                for j in range(GB):
                    dve.wait_ge(added, GB * g + j + 1)
                    dve.bn_stats(net.stats[:, GB * g + j, :], net.x[:, GB * g + j, :])

            def neg_exp_decay(c):
                return flat(decay)[:, CHUNK * c + 1:CHUNK * c + 2]

            def statistics(g):
                dve.wait_ge(net.in_x[g], 16)
                for b in range(GB * g, GB * g + GB):
                    own.did(dve.bn_stats(net.stats[:, b, :], net.x[:, b, :]))
                own.wait()
                for b in range(GB * g, GB * g + GB):
                    dve.bn_aggr(net.mean_var[:, b, :], net.stats[:, b, :]).then_inc(aggregated, 1)

            dve.wait_ge(net.in_small, 16 * 3)
            dve.tensor_scalar(neg_br[:], net.fvec[:, BR:BR + KC], -1.0, None, ALU.mult).then_inc(constants, 1)
            dve.wait_ge(preset, 10)
            dve.wait_ge(decay_exp, 1)
            for c in range(KC):
                own.did(dve.tensor_scalar(tokens(decay, 0, c), tokens(decay, 0, c), exp_decay[:, c:c + 1], -1.0,
                                          ALU.add, ALU.mult))
            own.did(dve.memset(pads(decay), FAR))
            own.wait()
            statistics(0)
            dve.wait_ge(rstd_ready, 1)
            dve.wait_ge(aggregated, GB)
            normalise(0)
            statistics(1)
            dve.wait_ge(net.in_rwkv, 16)
            for m, tm in enumerate((TMK, TMV, TMR)):
                for c in range(KC):
                    dve.tensor_scalar(w_mix[:, m, c, :], net.rwkv_w[:, m, c, :], col(tm, c), None,
                                      ALU.mult).then_inc(w_mixed, 1)
            for g in range(2, NG):
                statistics(g)
            dve.wait_ge(rstd_ready, 2)
            dve.wait_ge(aggregated, NB)
            own.again()

            def one(g, first, last):
                scan(g, None if last else g + 1, first)
                own.again()

            rounds(dve, one)
            add(NG - 1)


class Ring:

    def __init__(self, units, lag, at):
        self.units, self.lag, self.at = units, lag, at

    def unit(self, t, u):
        last = isinstance(t, int) and t == NB - 1
        return (self.units + 1) * t + u + 1 + (u + self.lag > self.at and not last)

    def head(self, t):
        if isinstance(t, int) and t == 0:
            return 0
        return (self.units + 1) * t - self.units + self.at - self.lag + 1

    def unit_bank(self, t, s, u):
        return self.unit(t if isinstance(t, int) else s + 2, u) % 2

    def head_bank(self, t, s):
        return self.head(t if isinstance(t, int) else s + 2) % 2


def pairs(engine, one, steps=NB):
    for s in range(2):
        one(s, s, s == 0, False)
    with engine.Fori(1, steps // 2 - 1) as p:
        for s in range(2):
            one(2 * p + s, s, False, False)
    for s in range(2):
        one(steps - 2 + s, s, False, s == 1)


def earlier(t, s, u, n, units):
    return (t, s, u - n) if u >= n else (t - 1, 1 - s, u - n + units)


def gqa(nc, net, sem):
    U, RINGS, PTS = KV_HEADS, 4, 4
    VW = 32
    SCALE = float(HD) ** -0.5
    LAG = 3
    PARTS = 4

    def unit(t, u):
        if isinstance(t, int) and t == NB - 1:
            return 10 * t + 2 + u
        return 10 * t + (2, 4, 5, 7, 8, 9, 10, 11)[u]

    def half(t, c):
        return c if isinstance(t, int) and t == 0 else 10 * t - (7, 4)[c]

    def bank(number, t, *at):
        return TR + number(t if isinstance(t, int) else 2, *at) % 2

    with ExitStack() as ctx:
        def sb(name, shape, dt=F32):
            return ctx.enter_context(nc.sbuf_tensor(name, shape, dt))

        h_tok, h_parts = sb("gq_h_tok", [P, 2, D]), sb("gq_h_parts", [P, U * 4, PARTS, HD], F32R)
        h_t = sb("gq_h_t", [P, 2, U, P], F32R)
        keys, key_parts = sb("gq_keys", [P, U * P]), sb("gq_key_parts", [P, U * P], F32R)
        kbd = sb("gq_keys_diagonal", [P, 2, U, 4, P], F32R)
        values = sb("gq_values", [P, 2, KV_HEADS, VW])
        weights, weights_t = sb("gq_weights", [P, RINGS, BANK]), sb("gq_weights_t", [P, PTS, BANK])
        top = sb("gq_top", [P, 4, 4])
        out_t = sb("gq_out_t", [P, 2, BANK])
        rsum, out = sb("gq_rsum", [P, 2, 4, 4]), sb("gq_out", [P, 2, 4, 4, HD])
        scratch = sb("gq_scratch", [P, NB])
        ps = ctx.enter_context(nc.psum_tensor("gq_psum", [P, 8, BANK], F32))
        TR, O = 4, 6

        aggregated = sem("gq_aggregated")
        rstd_ready = sem("gq_rstd")
        zeroed = sem("gq_zeroed")
        keys_in = sem("gq_keys_in")
        keys_split = sem("gq_keys_split")
        keys_set = [sem(f"gq_keys_set{s}") for s in range(2)]
        h_split = sem("gq_h_split")
        ones_set = sem("gq_ones_set")
        values_in = sem("gq_values_in")
        normed = sem("gq_normed")
        turned = sem("gq_turned")
        taken = sem("gq_taken")
        scored = sem("gq_scored")
        topped = sem("gq_topped")
        shifted = sem("gq_shifted")
        weighed = sem("gq_weighed")
        attended = sem("gq_attended")
        out_taken = sem("gq_out_taken")
        out_turned = sem("gq_out_turned")
        inverted = sem("gq_inverted")
        out_read = sem("gq_out_read")
        added = sem("gq_added")
        own_pool = sem("gq_own_pool")
        block = ctx.enter_context(nc.Block("gqa"))

        def set_by(t, s):
            return (t - s) * 32 + 64

        @block.sync
        def _(sp):
            def fetch(t):
                sp.dma_start(keys[:], net.dram["ctx_keys"][t]).then_inc(keys_in, 16)

            def one(t, s, first, last):
                sp.wait_ge(keys_split, t + 1)
                if not last:
                    fetch(t + 1)
                if isinstance(t, int) and t < 2:
                    sp.wait_ge(zeroed, t + 1)
                need(sp, scored, U * (t - 1))
                for j in range(4):
                    sp.dma_start(kbd[32 * j:32 * j + 32, s, :, j, :].bitcast(F32),
                                 key_parts[32 * j:32 * j + 32].bitcast(F32).rearrange("p (u t) -> p u t", t=P)
                                 ).then_inc(keys_set[s], 16)

            fetch(0)
            pairs(sp, one)

        @block.gpsimd
        def _(pool):
            own = Own(pool, own_pool)
            odd = net.const[:, CONST["odd"]].broadcast_to([P, U * P])
            ones = wide(net.ones[:, 0:U * 4], [P, U * 4, 2 * HD]).rearrange("p u (a d) -> p u a d", d=HD)

            def split_keys(t, s):
                pool.wait_ge(keys_in, 16 * (t + 1))
                if not (isinstance(t, int) and t == 0):
                    pool.wait_ge(keys_set[1 - s], set_by(t - 1, 1 - s))
                own.wait(own.did(pool.tensor_tensor(key_parts[:], keys[:], odd, ALU.mult)))
                pool.tensor_tensor(key_parts[:], keys[:], key_parts[:].bitcast(F32),
                                   ALU.subtract).then_inc(keys_split, 1)

            def split_h(t, s):
                h = h_tok[:, s].rearrange("p (u d) -> p u d", d=HD).unsqueeze(2).broadcast_to([P, U * 4, 2, HD])
                pool.wait_ge(normed, t + 1)
                if not (isinstance(t, int) and t == 0):
                    pool.wait_ge(turned, half(t - 1, 1) + 1)
                own.wait(own.did(pool.tensor_tensor(h_parts[:, :, 0:2, :], h, ones, ALU.mult)))
                pool.tensor_tensor(h_parts[:, :, 2:4, :], h, h_parts[:, :, 0:2, :].bitcast(F32),
                                   ALU.subtract).then_inc(h_split, 1)

            def add(t):
                pool.wait_ge(out_read, 2 * t + 2)
                pool.tensor_tensor(net.x[:, t, :], net.x[:, t, :], out.rearrange("p c g j d -> p (c g j d)"),
                                   ALU.add).then_inc(added, 1)

            layer_norm_scale(pool, own, net, scratch, aggregated, rstd_ready, 1)
            pool.memset(values[:], 0.0).then_inc(ones_set, 1)
            pool.wait_ge(ones_set, 1)
            pool.memset(values[:, :, :, HD:HD + 1], 1.0).then_inc(ones_set, 1)
            pool.wait_ge(ones_set, 2)
            pool.wait_ge(net.in_ctx, 16)

            def one(t, s, first, last):
                split_h(t, s)
                need(pool, attended, U * (t - 1))
                pool.tensor_copy(values[:, s, :, 0:HD],
                                 net.ctx[:, t, :].rearrange("p (h d) -> p h d", d=HD)).then_inc(values_in, 1)
                if not last:
                    split_keys(t + 1, 1 - s)
                if not (isinstance(t, int) and t < 2):
                    add(t - 2)
                own.again()

            split_keys(0, 0)
            pairs(pool, one)
            fold_ffn0(pool, net)
            add(NB - 2)
            add(NB - 1)

        @block.tensor
        def _(pe):
            ident = net.const[:, CONST["ident"]]

            def head(t, c):
                pe.wait_ge(h_split, t + 1)
                need(pe, taken, half(t, c) - 1)
                for u in range(4):
                    mm = pe.transpose(ps[:, bank(half, t, c), u * P:u * P + P],
                                      h_parts[:, 16 * c + 4 * u:16 * c + 4 * u + 4].bitcast(F32), ident)
                mm.then_inc(turned, 1)

            def scores(t, s, u):
                if u % 4 == 0:
                    pe.wait_ge(taken, half(t, u // 4) + 1)
                if u == 0:
                    pe.wait_ge(keys_set[s], set_by(t, s))
                need(pe, shifted, U * t + u - 3)
                pe.matmul(ps[:, u % 4, :], h_t[:, s, u, :], kbd[:, s, u, :, :],
                          start=True, stop=True).then_inc(scored, 1)

            def turn(t, s, u):
                pe.wait_ge(weighed, U * t + u + 1)
                need(pe, taken, unit(t, u) - 1)
                for j in range(4):
                    mm = pe.transpose(ps[:, bank(unit, t, u), j * P:j * P + P],
                                      weights[:, u % RINGS, j * P:j * P + P], ident)
                mm.then_inc(turned, 1)

            def attend(t, s, u):
                pe.wait_ge(taken, unit(t, u) + 1)
                c, g = u // 4, 32 * (u % 4)
                if u == 0:
                    pe.wait_ge(values_in, t + 1)
                if u % 4 == 0:
                    need(pe, out_read, 2 * t + c - 1)
                pe.matmul(ps[g:g + VW, O + c, :], values[:, s, u, :], weights_t[:, u % PTS],
                          start=True, stop=True).then_inc(attended, 1)

            def turn_out(t, c):
                pe.wait_ge(out_taken, 2 * t + c + 1)
                for j in range(4):
                    mm = pe.transpose(ps[:, O + c, j * P:j * P + P], out_t[:, c, j * P:j * P + P], ident)
                mm.then_inc(out_turned, 1)

            def one(t, s, first, last):
                for u in range(U):
                    if u < U - 1:
                        scores(t, s, u + 1)
                    elif not last:
                        scores(t + 1, 1 - s, 0)
                    if u >= LAG or not first:
                        turn(*earlier(t, s, u, LAG, U))
                    if u in (3, 5) and not last:
                        head(t + 1, u // 4)
                    if u > LAG or not first:
                        attend(*earlier(t, s, u, LAG + 1, U))
                    if u in (2, 6) and not first:
                        turn_out(t - 1, u // 4)

            for c in range(2):
                head(0, c)
            scores(0, 0, 0)
            pairs(pe, one)
            t, s = NB - 1, 1
            for u in range(U - LAG, U):
                turn(t, s, u)
                attend(t, s, u - 1)
            attend(t, s, U - 1)
            for c in range(2):
                turn_out(t, c)

        @block.scalar
        def _(act):
            def take_head(t, s, c):
                act.wait_ge(turned, half(t, c) + 1)
                need(act, scored, U * (t - 2) + 4 * c + 4)
                act.activation(h_t[:, s, 4 * c:4 * c + 4].rearrange("p u t -> p (u t)"), ps[:, bank(half, t, c), :],
                               ACT.Copy).then_inc(taken, 1)

            def weigh(t, u):
                act.wait_ge(shifted, U * t + u + 1)
                act.activation(weights[:, u % RINGS], weights[:, u % RINGS], ACT.Exp,
                               scale=SCALE).then_inc(weighed, 1)

            def take(t, s, u):
                act.wait_ge(turned, unit(t, u) + 1)
                need(act, attended, U * t + u - 3)
                act.activation(weights_t[:, u % PTS], ps[:, bank(unit, t, u), :],
                               ACT.Copy).then_inc(taken, 1)

            def take_out(t, c):
                act.wait_ge(attended, U * t + 4 * c + 4)
                need(act, out_turned, 2 * t + c - 1)
                act.activation(out_t[:, c], ps[:, O + c, :], ACT.Copy).then_inc(out_taken, 1)

            def one(t, s, first, last):
                for u in range(U):
                    if u >= LAG or not first:
                        take(*earlier(t, s, u, LAG, U))
                    if u in (3, 5) and not last:
                        take_head(t + 1, 1 - s, u // 4)
                    weigh(t, u)
                    if u in (0, 4) and not first:
                        take_out(t - 1, u // 4)

            for c in range(2):
                take_head(0, 0, c)
            pairs(act, one)
            take_out(NB - 1, 0)
            for u in range(U - LAG, U):
                take(NB - 1, 1, u)
            take_out(NB - 1, 1)

        @block.vector
        def _(dve):
            def normalise(t, s):
                need(dve, h_split, t - 1)
                dve.tensor_scalar(h_tok[:, s, :], net.x[:, t, :], net.mean_var[:, t, 0:1],
                                  net.rstd[:, bass.ds(t, 1)], ALU.subtract, ALU.mult).then_inc(normed, 1)

            def rows(u):
                return ps[:, u % 4, :].rearrange("p (j t) -> p j t", t=P)

            def maximum(t, u):
                dve.wait_ge(scored, U * t + u + 1)
                need(dve, shifted, U * t + u - 3)
                dve.tensor_reduce(top[:, u % 4, :], rows(u), AX.X, ALU.max).then_inc(topped, 1)

            def shift(t, s, u):
                dve.wait_ge(topped, U * t + u + 1)
                if not (isinstance(t, int) and t == 0 and u < RINGS):
                    bt, _, bu = earlier(t, s, u, RINGS, U)
                    dve.wait_ge(turned, unit(bt, bu) + 1)
                dve.tensor_tensor(weights[:, u % RINGS].rearrange("p (j t) -> p j t", t=P), rows(u),
                                  wide(top[:, u % 4, :], [P, 4, P]), ALU.subtract).then_inc(shifted, 1)

            def heads(c):
                return ps[:, O + c, :].rearrange("p (j g v) -> p g j v", j=4, v=VW)

            def invert(t, c):
                dve.wait_ge(out_turned, 2 * t + c + 1)
                dve.reciprocal(rsum[:, c], heads(c)[:, :, :, HD]).then_inc(inverted, 1)

            def divide(t, c):
                dve.wait_ge(inverted, 2 * t + c + 1)
                need(dve, added, t)
                dve.tensor_tensor(out[:, c], heads(c)[:, :, :, 0:HD], wide(rsum[:, c], [P, 4, 4, HD]),
                                  ALU.mult).then_inc(out_read, 1)

            def measure(t):
                dve.wait_ge(added, t + 1)
                dve.bn_stats(net.stats[:, t, :], net.x[:, t, :])

            def one(t, s, first, last):
                for u in range(U):
                    if u in (3, 7) and not first:
                        invert(t - 1, u // 4)
                    if u < U - 1:
                        maximum(t, u + 1)
                    elif not last:
                        maximum(t + 1, 0)
                    if u in (3, 7) and not first:
                        divide(t - 1, u // 4)
                    shift(t, s, u)
                    if u == 0 and not last:
                        if first:
                            dve.wait_ge(rstd_ready, 2)
                        normalise(t + 1, 1 - s)
                    if u == 5 and not (isinstance(t, int) and t < 2):
                        measure(t - 2)

            aggregate(dve, net, aggregated)
            dve.memset(kbd[:, 0].bitcast(F32), 0.0).then_inc(zeroed, 1)
            dve.wait_ge(rstd_ready, 1)
            normalise(0, 0)
            dve.memset(kbd[:, 1].bitcast(F32), 0.0).then_inc(zeroed, 1)
            maximum(0, 0)
            pairs(dve, one)
            for c in range(2):
                invert(NB - 1, c)
                divide(NB - 1, c)
            measure(NB - 2)
            measure(NB - 1)


def fold_ffn0(pool, net):
    pool.wait_ge(net.in_ffn0, 16 * 7)
    for c in range(KC):
        for tile, base, extra in ((net.gate0, PRE1, 1.0), (net.up0, PRE1, 1.0), (net.egate, PRE2, 1.0),
                                  (net.eup, PRE2, 1.0), (net.router_w, RSCALE, float(D) ** -0.5)):
            pool.tensor_scalar(tile[:, c, :], tile[:, c, :], net.fvec[:, base + c:base + c + 1], extra,
                               ALU.mult, ALU.mult)


def experts(nc, net, sem):
    STEPS = HC + EXPERTS
    with ExitStack() as ctx:
        def sb(name, shape, dt=F32):
            return ctx.enter_context(nc.sbuf_tensor(name, shape, dt))

        h_tok, h_t = sb("ex_h_tok", [P, GB, D]), sb("ex_h_t", [P, KC, GB * P])
        h_high, h_low = sb("ex_h_high", [P, KC, GB * P], F32R), sb("ex_h_low", [P, KC, GB * P], F32R)
        gated = sb("ex_gated", [P, 2, BANK])
        high, low = sb("ex_hidden_high", [P, 2, BANK], F32R), sb("ex_hidden_low", [P, 2, BANK], F32R)
        raw = {"gate0": net.gate0, "up0": net.up0, "egate": net.egate, "eup": net.eup,
               "down0": net.down0, "edown": net.edown}
        w_high = {n: sb(f"ex_{n}_high", w.shape, F32R) for n, w in raw.items()}
        w_low = {n: in_place(nc, f"ex_{n}_low", net.places[n], w.shape) for n, w in raw.items()}
        dense, mixture = sb("ex_dense", [P, GB, D]), sb("ex_mixture", [P, GB, D])
        junk = sb("ex_junk", [P, D])
        squares, norm = sb("ex_squares", [P, 3, GB]), sb("ex_norm", [P, 3, GB])
        scratch, scratch2 = sb("ex_scratch", [P, NB]), sb("ex_scratch2", [P, NB])
        scratch3, eps = sb("ex_scratch3", [P, GB]), sb("ex_eps", [P, GB])
        prob, top = sb("ex_prob", [P, GB, EXPERTS]), sb("ex_top", [P, GB])
        above, equal = (sb(f"ex_{n}", [P, GB, EXPERTS, EXPERTS]) for n in ("above", "equal"))
        rank, share = sb("ex_rank", [P, GB, EXPERTS]), sb("ex_share", [P, GB, EXPERTS])
        total = sb("ex_total", [P, GB])
        ps = ctx.enter_context(nc.psum_tensor("ex_psum", [P, 8, BANK], F32))
        ROUTER = 6

        aggregated = sem("ex_aggregated")
        rstd_ready = sem("ex_rstd")
        normed = sem("ex_normed")
        turned = sem("ex_turned")
        taken = sem("ex_taken")
        h_split = sem("ex_h_split")
        w_rounded = sem("ex_w_rounded")
        w_split = sem("ex_w_split")
        routed = sem("ex_routed")
        logits_read = sem("ex_logits_read")
        prob_ready = sem("ex_prob_ready")
        gate_full, up_full = sem("ex_gate_full"), sem("ex_up_full")
        gelu_done = sem("ex_gelu_done")
        hidden_ready = sem("ex_hidden_ready")
        high_ready = sem("ex_high_ready")
        low_ready = sem("ex_low_ready")
        down_done = sem("ex_down_done")
        squared = sem("ex_squared")
        norm_ready = sem("ex_norm_ready")
        dense_ready = sem("ex_dense_ready")
        weighed = sem("ex_weighed")
        summed = sem("ex_summed")
        own_dve, own_pool = sem("ex_own_dve"), sem("ex_own_pool")
        block = ctx.enter_context(nc.Block("experts"))

        def down_bank(q):
            return 4 if q < HC or q % 2 == 1 else 6

        def parts(q):
            at = (q % HC) * P
            names = ("gate0", "up0", "down0") if q < HC else ("egate", "eup", "edown")
            of = [(w_high[n][:, :, at:at + P], w_low[n][:, :, at:at + P], raw[n][:, :, at:at + P])
                  for n in names[:2]]
            n = names[2]
            return of + [(w_high[n][:, q % HC, :], w_low[n][:, q % HC, :], raw[n][:, q % HC, :])]

        def row(name):
            return net.rows[:, ROWS[name]]

        @block.gpsimd
        def _(pool):
            own = Own(pool, own_pool)

            def link(instruction):
                own.wait(own.did(instruction))

            for of, count in ((slice(0, GB), GB), (slice(GB, NB), NB)):
                pool.wait_ge(aggregated, count)
                var, rstd, half = net.mean_var[:, of, 1], net.rstd[:, of], net.half[:, of]
                a, b = scratch[:, of], scratch2[:, of]
                link(inverse_root(pool, own, rstd, var, a, 1.0, LN_EPS, half))
                link(pool.tensor_tensor(a, rstd, rstd, ALU.mult))
                link(pool.tensor_tensor(a, a, var, ALU.mult))
                link(inverse_root(pool, own, b, a, a, 1.0, RMS_EPS, half))
                pool.tensor_tensor(rstd, rstd, b, ALU.mult).then_inc(rstd_ready, 1)

            def normalise(g, n):
                pool.wait_ge(squared, 3 * GB * g + GB * (n + 1))
                link(pool.tensor_tensor(scratch3[:], squares[:, n], eps[:], ALU.add))
                pool.tensor_tensor(norm[:, n], scratch3[:], net.half[:, 0:GB], ALU.pow).then_inc(norm_ready, 1)
                own.again()

            link(pool.memset(eps[:], RMS_EPS))
            own.again()
            for q in range(STEPS):
                for m, (hi, lo, w) in enumerate(parts(q)):
                    pool.wait_ge(w_rounded, 3 * q + m + 1)
                    pool.tensor_tensor(lo, w, hi.bitcast(F32), ALU.subtract).then_inc(w_split, 1)
                if q == HC + 2:
                    normalise(0, 0)
            for n in (1, 2):
                normalise(0, n)
            with pool.Fori(1, NG) as g:
                for n in range(3):
                    normalise(g, n)

        @block.tensor
        def _(pe):
            ident = net.const[:, CONST["ident"]]

            def turn(g):
                pe.wait_ge(normed, g + 1)
                need(pe, hidden_ready, STEPS * g - 1)
                for c in range(KC):
                    for j in range(GB):
                        mm = pe.transpose(ps[:, c, j * P:j * P + P], h_tok[:, j, c * P:c * P + P], ident)
                mm.then_inc(turned, 1)

            def route(g):
                pe.wait_ge(taken, KC * (g + 1))
                need(pe, weighed, EXPERTS * g - 1)
                for j in range(GB):
                    for c in range(KC):
                        mm = pe.matmul(ps[:, ROUTER, j * EXPERTS:(j + 1) * EXPERTS],
                                       h_t[:, c, j * P:j * P + P], net.router_w[:, c, :],
                                       start=(c == 0), stop=(c == KC - 1))
                mm.then_inc(routed, 1)

            def gate_up(g, q):
                need(pe, hidden_ready, STEPS * g + q - 1)
                if isinstance(g, int) and g == 0:
                    pe.wait_ge(w_split, 3 * (q + 1))
                if q == 0:
                    pe.wait_ge(h_split, 2 * KC * g + KC)
                for m, full in enumerate((gate_full, up_full)):
                    hi, lo, _ = parts(q)[m]
                    for n, (w, h) in enumerate(((hi, h_high), (lo, h_high), (hi, h_low))):
                        if q == 0 and n == 2:
                            pe.wait_ge(h_split, 2 * KC * (g + 1))
                        for c in range(KC):
                            mm = pe.matmul(ps[:, 2 * (q % 2) + m, :], w[:, c, :], h[:, c, :],
                                           start=(n == 0 and c == 0), stop=(n == 2 and c == KC - 1))
                    mm.then_inc(full, 1)

            def down(g, q):
                pe.wait_ge(high_ready, STEPS * g + q + 1)
                if q == 0:
                    need(pe, weighed, EXPERTS * g)
                if q == HC:
                    pe.wait_ge(logits_read, g + 1)
                if q == HC + 1:
                    pe.wait_ge(dense_ready, GB * (g + 1))
                if q > HC + 1:
                    pe.wait_ge(weighed, EXPERTS * g + q - HC - 1)
                hi, lo, _ = parts(q)[2]
                for n, (h, w) in enumerate(((high, hi), (high, lo), (low, hi))):
                    if n == 2:
                        pe.wait_ge(low_ready, STEPS * g + q + 1)
                    for j in range(GB):
                        first = q >= HC or q == 0
                        mm = pe.matmul(ps[:, down_bank(q) + j // 2, (j % 2) * D:(j % 2) * D + D],
                                       h[:, q % 2, j * P:j * P + P], w,
                                       start=(first and n == 0 and j % 2 == 0), stop=(q >= HC - 1 and n == 2),
                                       skip_group_check=True)
                mm.then_inc(down_done, 1)

            def one(g, first, last):
                route(g)
                for q in range(STEPS):
                    gate_up(g, q)
                    if q > 0:
                        down(g, q - 1)
                if not last:
                    turn(g + 1)
                down(g, STEPS - 1)

            turn(0)
            rounds(pe, one)

        @block.scalar
        def _(act):
            def take(g):
                act.wait_ge(turned, g + 1)
                need(act, up_full, STEPS * g)
                for c in range(KC):
                    act.activation(h_t[:, c, :], ps[:, c, :], ACT.Copy).then_inc(taken, 1)
                for c in range(KC):
                    act.activation(h_high[:, c, :], ps[:, c, :], ACT.Copy).then_inc(h_split, 1)

            def round_weights(q):
                for hi, _, w in parts(q):
                    act.activation(hi, w, ACT.Copy).then_inc(w_rounded, 1)

            def square(g, n, source):
                need(act, norm_ready, 3 * g + (n > 0))
                for j in range(GB):
                    if not (isinstance(g, int) and g == 0 and n == 0 and j == 0):
                        act.wait_ge(squared, 3 * GB * g + GB * n + j)
                    act.activation(junk[:], source(j), ACT.Square, scale=float(D) ** -0.5,
                                   accum_out=squares[:, n, j:j + 1]).then_inc(squared, 1)

            def one(g, first, last):
                for q in range(STEPS):
                    if first and q + 2 < STEPS:
                        round_weights(q + 2)
                    act.wait_ge(gate_full, STEPS * g + q + 1)
                    need(act, low_ready, STEPS * g + q - 1)
                    act.activation(gated[:, q % 2, :], ps[:, 2 * (q % 2), :],
                                   ACT.Gelu_apprx_tanh).then_inc(gelu_done, 1)
                    act.wait_ge(hidden_ready, STEPS * g + q + 1)
                    need(act, down_done, STEPS * g + q - 1)
                    act.activation(high[:, q % 2, :], gated[:, q % 2, :], ACT.Copy).then_inc(high_ready, 1)
                    if q == 1:
                        act.wait_ge(logits_read, g + 1)
                        act.activation(prob[:], prob[:], ACT.Exp).then_inc(prob_ready, 1)
                        if not first:
                            mixture_squares(g - 1)
                    if q == 4 and not first:
                        sum_squares(g - 1)
                    if q == HC:
                        act.wait_ge(down_done, STEPS * g + HC)
                        square(g, 0, lambda j: ps[:, 4 + j // 2, (j % 2) * D:(j % 2) * D + D])
                if not last:
                    take(g + 1)

            def mixture_squares(g):
                act.wait_ge(weighed, EXPERTS * (g + 1))
                square(g, 1, lambda j: mixture[:, j, :])

            def sum_squares(g):
                act.wait_ge(summed, GB * (g + 1))
                square(g, 2, lambda j: mixture[:, j, :])

            for q in range(2):
                round_weights(q)
            take(0)
            rounds(act, one)
            mixture_squares(NG - 1)
            sum_squares(NG - 1)

        @block.vector
        def _(dve):
            own = Own(dve, own_dve)

            def link(instruction):
                own.wait(own.did(instruction))

            def normalise(g):
                need(dve, turned, g)
                for j in range(GB):
                    b = GB * g + j
                    h = dve.tensor_scalar(h_tok[:, j, :], net.x[:, b, :], net.mean_var[:, b, 0:1],
                                          net.rstd[:, bass.ds(b, 1)], ALU.subtract, ALU.mult)
                h.then_inc(normed, 1)

            def read_logits(g):
                dve.wait_ge(routed, g + 1)
                logits = ps[:, ROUTER, 0:GB * EXPERTS].rearrange("p (j e) -> p j e", e=EXPERTS)
                link(dve.tensor_reduce(top[:], logits, AX.X, ALU.max))
                dve.tensor_tensor(prob[:], logits, wide(top[:], [P, GB, EXPERTS]),
                                  ALU.subtract).then_inc(logits_read, 1)

            def choose(g):
                dve.wait_ge(prob_ready, g + 1)
                shape = [P, GB, EXPERTS, EXPERTS]
                this, other = wide(prob[:], shape), prob[:].unsqueeze(2).broadcast_to(shape)
                first = net.const[:, CONST["before"]].rearrange("p (e f) -> p e f", f=EXPERTS)
                own.did(dve.tensor_tensor(above[:], other, this, ALU.is_gt))
                link(dve.tensor_tensor(equal[:], other, this, ALU.is_equal))
                link(dve.tensor_tensor(equal[:], equal[:], first.unsqueeze(1).broadcast_to(shape), ALU.mult))
                link(dve.tensor_tensor(above[:], above[:], equal[:], ALU.add))
                link(dve.tensor_reduce(rank[:], above[:], AX.X, ALU.add))
                link(dve.scalar_tensor_tensor(share[:], rank[:], float(TOP), prob[:], ALU.is_lt, ALU.mult))
                link(dve.tensor_reduce(total[:], share[:], AX.X, ALU.add))
                link(dve.reciprocal(total[:], total[:]))
                link(dve.tensor_tensor(share[:], share[:], wide(total[:], [P, GB, EXPERTS]), ALU.mult))
                link(dve.tensor_tensor(share[:], share[:], row("L0_ffn_per_expert_scale").unsqueeze(1)
                                       .broadcast_to([P, GB, EXPERTS]), ALU.mult))

            def hide(g, q):
                dve.wait_ge(gelu_done, STEPS * g + q + 1)
                dve.wait_ge(up_full, STEPS * g + q + 1)
                dve.tensor_tensor(gated[:, q % 2, :], gated[:, q % 2, :], ps[:, 2 * (q % 2) + 1, :],
                                  ALU.mult).then_inc(hidden_ready, 1)

            def split_hidden(g, q):
                dve.wait_ge(high_ready, STEPS * g + q + 1)
                need(dve, down_done, STEPS * g + q - 1)
                dve.tensor_tensor(low[:, q % 2, :], gated[:, q % 2, :], high[:, q % 2, :].bitcast(F32),
                                  ALU.subtract).then_inc(low_ready, 1)

            def split_h(g):
                dve.wait_ge(h_split, 2 * KC * g + KC)
                need(dve, up_full, STEPS * g)
                for c in range(KC):
                    dve.tensor_tensor(h_low[:, c, :], h_t[:, c, :], h_high[:, c, :].bitcast(F32),
                                      ALU.subtract).then_inc(h_split, 1)

            def scale_dense(g):
                dve.wait_ge(norm_ready, 3 * g + 1)
                for j in range(GB):
                    dve.scalar_tensor_tensor(dense[:, j, :], ps[:, 4 + j // 2, (j % 2) * D:(j % 2) * D + D],
                                             norm[:, 0, j:j + 1], row("L0_ffn_rn_post1"),
                                             ALU.mult, ALU.mult).then_inc(dense_ready, 1)

            def weigh(g, e):
                q = HC + e
                dve.wait_ge(down_done, STEPS * g + q + 1)
                if e > 0:
                    dve.wait_ge(weighed, EXPERTS * g + e)
                    own.wait()
                for j in range(GB):
                    y = ps[:, down_bank(q) + j // 2, (j % 2) * D:(j % 2) * D + D]
                    if e == 0:
                        w = dve.tensor_scalar(mixture[:, j, :], y, share[:, j, e:e + 1], None, ALU.mult)
                    else:
                        w = dve.scalar_tensor_tensor(mixture[:, j, :], y, share[:, j, e:e + 1],
                                                     mixture[:, j, :], ALU.mult, ALU.add)
                    if j < GB - 1:
                        own.did(w)
                w.then_inc(weighed, 1)

            def combine(g):
                dve.wait_ge(norm_ready, 3 * g + 2)
                dve.wait_ge(dense_ready, GB * (g + 1))
                for j in range(GB):
                    own.did(dve.scalar_tensor_tensor(mixture[:, j, :], mixture[:, j, :], norm[:, 1, j:j + 1],
                                                     row("L0_ffn_rn_post2"), ALU.mult, ALU.mult))
                own.wait()
                for j in range(GB):
                    dve.tensor_tensor(mixture[:, j, :], mixture[:, j, :], dense[:, j, :],
                                      ALU.add).then_inc(summed, 1)

            def scale_sum(g):
                dve.wait_ge(norm_ready, 3 * g + 3)
                for j in range(GB):
                    own.did(dve.scalar_tensor_tensor(mixture[:, j, :], mixture[:, j, :], norm[:, 2, j:j + 1],
                                                     row("L0_ffn_rn_post"), ALU.mult, ALU.mult))

            def add_sum(g):
                own.wait()
                for j in range(GB):
                    b = GB * g + j
                    own.did(dve.tensor_tensor(net.x[:, b, :], net.x[:, b, :], mixture[:, j, :], ALU.add))

            def measure(g):
                own.wait()
                for j in range(GB):
                    b = GB * g + j
                    own.did(dve.bn_stats(net.stats[:, b, :], net.x[:, b, :]))

            def one(g, first, last):
                for q in range(STEPS):
                    if q == 0:
                        split_h(g)
                        read_logits(g)
                    hide(g, q)
                    if q == 0 and not first:
                        weigh(g - 1, EXPERTS - 1)
                    if q == 3 and not first:
                        combine(g - 1)
                    if q == 5 and not first:
                        scale_sum(g - 1)
                    if q == 6 and not first:
                        add_sum(g - 1)
                    if q == 7 and not first:
                        measure(g - 1)
                    if q == HC and not last:
                        normalise(g + 1)
                    if q == HC + 1:
                        scale_dense(g)
                    if q >= HC + 1:
                        weigh(g, q - HC - 1)
                    split_hidden(g, q)
                    if q == 1:
                        choose(g)
                own.again()

            aggregate(dve, net, aggregated)
            dve.wait_ge(rstd_ready, 1)
            normalise(0)
            dve.wait_ge(rstd_ready, 2)
            rounds(dve, one)
            own.did(dve.engine_nop())
            weigh(NG - 1, EXPERTS - 1)
            combine(NG - 1)
            scale_sum(NG - 1)
            add_sum(NG - 1)
            measure(NG - 1)


def windowed(nc, net, sem):
    PIECES = ["v", "k", "q0", "q1", "q2", "q3", "o0", "o1", "o2", "o3"]
    LOW_BY_DVE, LOW_BY_POOL = ["v", "k", "q0", "q1", "o2", "o3"], ["q2", "q3", "o0", "o1"]
    U = KVH
    ORDER = [("p", -1, 3), ("q", 0, 1), ("h", 1, 0), ("p", 0, 0), ("q", 0, 2), ("p", 0, 1),
             ("q", 0, 3), ("p", 0, 2), ("k", 1, 0), ("q", 1, 0)]
    PJ, SC, TR, AV, OUT = 0, 2, 4, 6, 7
    K = 2

    def bank_of(what, g=0):
        return TR + next(i for i, (w, _, h) in enumerate(ORDER) if (w, h) == (what, g)) % 2

    def number(what, t, g=0):
        if what == "h" and isinstance(t, int) and t == 0:
            return 0
        if what == "q" and g >= 2 and isinstance(t, int) and t == NB - 1:
            return 6 * t + 2 + g
        return 6 * t + {"h": -2, "k": 1, "q": (2, 3, 5, 6)[g]}[what]

    with ExitStack() as ctx:
        def sb(name, shape, dt=F32):
            return ctx.enter_context(nc.sbuf_tensor(name, shape, dt))

        h_tok, h_high = sb("wi_h_tok", [P, 2, D]), sb("wi_h_high", [P, 2, KC, P], F32R)
        h_low = sb("wi_h_low", [P, 2, KC, P], F32R)
        values = sb("wi_values", [P, 2, KVH * DH])
        raw, square = sb("wi_raw", [P, 3, 4, DH]), sb("wi_square", [P, 2, 4, DH])
        straight, crossed = sb("wi_straight", [P, 3, 4, DH]), sb("wi_crossed", [P, 3, 4, DH])
        q_t, k_t = sb("wi_q_t", [P, 2, 4, P]), sb("wi_k_t", [P, 2, KVH, P])
        weights, weights_t = sb("wi_weights", [P, 2, 4, P]), sb("wi_weights_t", [P, 2, BANK])
        out_high, out_low = sb("wi_out_high", [P, 2, 4, P], F32R), sb("wi_out_low", [P, 2, 4, P], F32R)
        raw_w = {"v": net.wv, "k": net.wk, "q": net.wq, "o": net.wo}
        w_high = {n: sb(f"wi_w{n}_high", w.shape, F32R) for n, w in raw_w.items()}
        w_low = {n: in_place(nc, f"wi_w{n}_low", net.places[f"w{n}"], w.shape) for n, w in raw_w.items()}
        tables = {n: sb(f"wi_{n}", [P, DH]) for n in ("cos_q", "sin_q", "cos_k", "sin_k")}
        sums, scale = sb("wi_sums", [P, 3, 4]), sb("wi_scale", [P, 5, 4])
        top, bias = sb("wi_top", [P, 2, 4]), sb("wi_bias", [P, 2, 4])
        total, inverse = sb("wi_total", [P, 2, 4]), sb("wi_inverse", [P, 2, 4])
        scratch, scratch2 = sb("wi_scratch", [P, NB]), sb("wi_scratch2", [P, 4])
        eps = sb("wi_eps", [P, 4])
        mask, ident_b = sb("wi_mask", [P, 4, P], BF16), sb("wi_ident", [P, P], BF16)
        ps = ctx.enter_context(nc.psum_tensor("wi_psum", [P, 8, BANK], F32))

        aggregated = sem("wi_aggregated")
        rstd_ready = sem("wi_rstd")
        tables_ready = sem("wi_tables")
        w_rounded = sem("wi_w_rounded")
        low_dve, low_pool = sem("wi_low_dve"), sem("wi_low_pool")
        h_low_ready = sem("wi_h_low")
        out_low_ready = sem("wi_out_low")
        normed = sem("wi_normed")
        projected = sem("wi_projected")
        proj_taken = sem("wi_proj_taken")
        squared = sem("wi_squared")
        summed = sem("wi_summed")
        parts = sem("wi_parts")
        rotated = sem("wi_rotated")
        scaled = sem("wi_scaled")
        turned = sem("wi_turned")
        turned_taken = sem("wi_turned_taken")
        turned_p = sem("wi_turned_p")
        turned_p_taken = sem("wi_turned_p_taken")
        scored = sem("wi_scored")
        bias_ready = sem("wi_bias")
        weighed = sem("wi_weighed")
        inverted = sem("wi_inverted")
        normalised = sem("wi_normalised")
        attended = sem("wi_attended")
        attended_taken = sem("wi_attended_taken")
        output = sem("wi_output")
        added = sem("wi_added")
        own_dve, own_pool = sem("wi_own_dve"), sem("wi_own_pool")
        block = ctx.enter_context(nc.Block("windowed"))

        def ahead(t, s, g, last):
            own = [("q", t, s, g + 2)] if g < 2 else []
            following = [[], [("v", 0)], [("k", 0), ("q", 0)], [("q", 1)]][g] if not last else []
            return own + [(what, t + 1, 1 - s, head) for what, head in following]

        FIRST_ITEMS = [("v", 0, 0, 0), ("k", 0, 0, 0), ("q", 0, 0, 0), ("q", 0, 0, 1)]

        def of_six(what, t, g):
            return 6 * t + {"v": 0, "k": 1, "q": 2 + g}[what]

        def of_five(what, t, g):
            return 5 * t + {"k": 0, "q": 1 + g}[what]

        def square_slot(what, t, s, g):
            return (s + of_five(what, 0, g)) % 2

        def piece(tiles, name):
            tile, g = tiles[name[0]], int(name[1:] or 0)
            return tile[:, 4 * g:4 * g + 4, :] if name[0] == "o" else tile[:, :, g * BANK:g * BANK + BANK]

        def take_low(engine, name, done):
            engine.wait_ge(w_rounded, PIECES.index(name) + 1)
            engine.tensor_tensor(piece(w_low, name), piece(raw_w, name), piece(w_high, name).bitcast(F32),
                                 ALU.subtract).then_inc(done, 1)

        def slot(what, g):
            return K if what == "k" else g % 2

        @block.sync
        def _(sp):
            load_late(nc, net)

        @block.gpsimd
        def _(pool):
            own = Own(pool, own_pool)

            def link(instruction):
                own.wait(own.did(instruction))

            link(pool.memset(eps[:], DH * RMS_EPS))
            layer_norm_scale(pool, own, net, scratch, aggregated, rstd_ready, 1)

            def find_scale(what, t, s, g):
                n, at = of_five(what, t, g), slot(what, g)
                scale_at = 4 if what == "k" else g
                pool.wait_ge(summed, n + 1)
                need(pool, scaled, U * t + (g if what == "q" else 0))
                link(pool.tensor_tensor(scratch2[:], sums[:, at], eps[:], ALU.add))
                found = pool.tensor_tensor(scale[:, scale_at], scratch2[:], net.half[:, 0:4], ALU.pow)
                if what == "k":
                    link(found)
                else:
                    found.then_inc(scaled, 1)

            def join(what, t, s, g):
                n, at = of_five(what, t, g), slot(what, g)
                scale_at = 4 if what == "k" else g
                pool.wait_ge(parts, 3 * (n + 1))
                added_up = pool.tensor_tensor(straight[:, at], straight[:, at], crossed[:, at], ALU.add)
                if what == "k":
                    link(added_up)
                    added_up = pool.tensor_tensor(straight[:, at], straight[:, at],
                                                  wide(scale[:, scale_at], [P, 4, DH]), ALU.mult)
                added_up.then_inc(rotated, 1)

            def normalise(t, g):
                pool.wait_ge(inverted, U * t + g + 1)
                pool.tensor_tensor(weights[:, g % 2], weights[:, g % 2], wide(inverse[:, g % 2], [P, 4, P]),
                                   ALU.mult).then_inc(normalised, 1)

            def one(t, s, first, last):
                for g in range(U):
                    items = [item for item in ahead(t, s, g, last) if item[0] != "v"]
                    for item in items[:1]:
                        find_scale(*item)
                    normalise(t, g)
                    for item in items[:1]:
                        join(*item)
                    for item in items[1:]:
                        join(*item)
                        find_scale(*item)
                own.again()

            for name in LOW_BY_POOL[:2]:
                take_low(pool, name, low_pool)
            find_scale(*FIRST_ITEMS[1])
            for item in FIRST_ITEMS[1:]:
                join(*item)
                if item[0] == "q":
                    find_scale(*item)
            for name in LOW_BY_POOL[2:]:
                take_low(pool, name, low_pool)
            pairs(pool, one)

        @block.tensor
        def _(pe):
            ident = net.const[:, CONST["ident"]]

            def turn_h(t, s):
                pe.wait_ge(normed, t + 1)
                need(pe, turned_p_taken, U * (t - 1))
                for c in range(KC):
                    mm = pe.transpose(ps[:, bank_of("h"), c * P:c * P + P], h_tok[:, s, c * P:c * P + P], ident)
                mm.then_inc(turned, 1)

            def turn_heads(what, t, g):
                pe.wait_ge(rotated, of_five(what, t, g) + 1)
                if what == "k":
                    pe.wait_ge(turned_taken, number("q", t - 1, 3) + 1 if not (isinstance(t, int) and t == 0) else 1)
                elif g == 0:
                    need(pe, turned_p_taken, U * (t - 1) + 3)
                elif g == 2 and isinstance(t, int) and t == NB - 1:
                    pe.wait_ge(turned_p_taken, U * t)
                elif g == 2:
                    pe.wait_ge(turned_taken, number("h", t + 1) + 1)
                    pe.wait_ge(h_low_ready, t + 2)
                else:
                    pe.wait_ge(turned_taken, number("q", t, g - 1) + 1)
                for j in range(4):
                    mm = pe.transpose(ps[:, bank_of(what, g), j * P:j * P + P], straight[:, slot(what, g), j, :], ident)
                mm.then_inc(turned, 1)

            def turn_weights(t, g):
                pe.wait_ge(normalised, U * t + g + 1)
                if g == 3:
                    pe.wait_ge(turned_taken, (number("k", t + 1) + 1) if not (isinstance(t, int) and t == NB - 1)
                               else number("q", t, 3) + 1)
                elif g == 0:
                    pe.wait_ge(turned_taken, number("q", t, 1) + 1)
                else:
                    pe.wait_ge(turned_p_taken, U * t + g)
                for j in range(4):
                    mm = pe.transpose(ps[:, bank_of("p", g), j * P:j * P + P], weights[:, g % 2, j, :], ident)
                mm.then_inc(turned_p, 1)

            def split(name):
                if name in LOW_BY_DVE:
                    pe.wait_ge(low_dve, LOW_BY_DVE.index(name) + 1)
                else:
                    pe.wait_ge(low_pool, LOW_BY_POOL.index(name) + 1)

            def project(what, t, s, g):
                n = of_six(what, t, g)
                need(pe, proj_taken, n - 1)
                if what == "v":
                    pe.wait_ge(turned_taken, number("h", t) + 1)
                    pe.wait_ge(h_low_ready, t + 1)
                name = f"q{g}" if what == "q" else what
                if isinstance(t, int) and t == 0:
                    split(name)
                hi, lo = piece(w_high, name), piece(w_low, name)
                for n, (h, w) in enumerate(((h_high, hi), (h_high, lo), (h_low, hi))):
                    for c in range(KC):
                        mm = pe.matmul(ps[:, PJ + of_six(what, 0, g) % 2, :], h[:, s, c, :], w[:, c, :],
                                       start=(n == 0 and c == 0), stop=(n == 2 and c == KC - 1))
                mm.then_inc(projected, 1)

            def scores(t, s, g):
                if g == 0:
                    pe.wait_ge(turned_taken, number("k", t) + 1)
                pe.wait_ge(turned_taken, number("q", t, g) + 1)
                need(pe, weighed, 4 * (U * t + g - 1))
                bank = ps[:, SC + g % 2, :]
                pe.matmul(bank, ident_b[:], mask.rearrange("p j t -> p (j t)"), start=True, stop=False,
                          skip_group_check=True)
                for j in range(4):
                    mm = pe.matmul(bank[:, j * P:j * P + P], q_t[:, g % 2, j, :], k_t[:, s, g, :],
                                   start=False, stop=(j == 3), skip_group_check=True)
                mm.then_inc(scored, 1)

            def attend(t, s, g):
                pe.wait_ge(turned_p_taken, U * t + g + 1)
                need(pe, attended_taken, U * t + g)
                need(pe, out_low_ready, U * t + g)
                pe.matmul(ps[:, AV, :], values[:, s, g * DH:g * DH + DH], weights_t[:, g % 2],
                          start=True, stop=True).then_inc(attended, 1)

            def project_out(t, g):
                pe.wait_ge(attended_taken, U * t + g + 1)
                pe.wait_ge(out_low_ready, U * t + g + 1)
                if g == 0:
                    need(pe, added, t)
                if isinstance(t, int) and t == 0:
                    split(f"o{g}")
                hi, lo = piece(w_high, f"o{g}"), piece(w_low, f"o{g}")
                for n, (out, w) in enumerate(((out_high, hi), (out_high, lo), (out_low, hi))):
                    for j in range(4):
                        mm = pe.matmul(ps[:, OUT, 0:D], out[:, g % 2, j, :], w[:, j, :],
                                       start=(g == 0 and n == 0 and j == 0), stop=(g == 3 and n == 2 and j == 3),
                                       skip_group_check=True)
                mm.then_inc(output, 1)

            def one(t, s, first, last):
                for g in range(U):
                    items = ahead(t, s, g, last)
                    for item in items:
                        if item[0] != "v":
                            project(*item)
                    scores(t, s, g)
                    for item in items:
                        if item[0] == "v":
                            project(*item)
                    if g > 0 or not first:
                        pt, _, pg = earlier(t, s, g, 1, U)
                        turn_weights(pt, pg)
                    if g > 1 or not first:
                        pt, _, pg = earlier(t, s, g, 2, U)
                        project_out(pt, pg)
                    if g > 0 or not first:
                        attend(*earlier(t, s, g, 1, U))
                    if g < 3:
                        turn_heads("q", t, g + 1)
                    elif not last:
                        turn_heads("k", t + 1, 0)
                        turn_heads("q", t + 1, 0)
                    if g == 0 and not last:
                        turn_h(t + 1, 1 - s)

            turn_h(0, 0)
            for item in FIRST_ITEMS:
                project(*item)
            pe.wait_ge(tables_ready, 2)
            turn_heads("k", 0, 0)
            turn_heads("q", 0, 0)
            pairs(pe, one)
            turn_weights(NB - 1, 3)
            project_out(NB - 1, 2)
            attend(NB - 1, 1, 3)
            project_out(NB - 1, 3)

        @block.scalar
        def _(act):
            def take(what, t, s, g):
                act.wait_ge(projected, of_six(what, t, g) + 1)
                bank = ps[:, PJ + of_six(what, 0, g) % 2, :]
                if what == "v":
                    need(act, attended, U * (t - 1))
                    act.activation(values[:, s], bank, ACT.Copy).then_inc(proj_taken, 1)
                    return
                n, at = of_five(what, t, g), slot(what, g)
                if what == "k":
                    need(act, parts, 3 * (of_five("k", t - 1, 0) + 1))
                else:
                    need(act, parts, 3 * (of_five("q", t, g - 2) + 1) if g >= 2
                         else 3 * (of_five("q", t - 1, g + 2) + 1))
                act.activation(raw[:, at].rearrange("p j d -> p (j d)"), bank, ACT.Copy).then_inc(proj_taken, 1)
                act.wait_ge(proj_taken, of_six(what, t, g) + 1)
                need(act, summed, n - 1)
                act.activation(square[:, square_slot(what, t, s, g)], raw[:, at], ACT.Square).then_inc(squared, 1)

            def take_high(name):
                act.activation(piece(w_high, name), piece(raw_w, name), ACT.Copy).then_inc(w_rounded, 1)

            def take_turned(what, t, s, g=0):
                act.wait_ge(turned, number(what, t, g) + 1)
                bank = ps[:, bank_of(what, g), :]
                if what == "h":
                    need(act, projected, of_six("q", t - 2, 3) + 1)
                    act.activation(h_high[:, s].rearrange("p c t -> p (c t)"), bank[:, 0:D],
                                   ACT.Copy).then_inc(turned_taken, 1)
                    return
                need(act, scored, U * (t - 1) if what == "k" else U * t + g - 1)
                tile = k_t[:, s] if what == "k" else q_t[:, g % 2]
                act.activation(tile.rearrange("p j t -> p (j t)"), bank, ACT.Copy).then_inc(turned_taken, 1)

            def weigh(t, g):
                w = U * t + g
                act.wait_ge(bias_ready, w + 1)
                need(act, turned_p, w - 1)
                need(act, inverted, w - 1)
                for j in range(4):
                    act.activation(weights[:, g % 2, j, :], ps[:, SC + g % 2, j * P:j * P + P], ACT.Exp,
                                   bias=bias[:, g % 2, j:j + 1], scale=scale[:, g, j:j + 1],
                                   accum_out=total[:, g % 2, j:j + 1]).then_inc(weighed, 1)

            def take_attended(t, g):
                act.wait_ge(attended, U * t + g + 1)
                need(act, output, U * t + g - 1)
                act.activation(out_high[:, g % 2].rearrange("p j t -> p (j t)"), ps[:, AV, :],
                               ACT.Copy).then_inc(attended_taken, 1)

            def one(t, s, first, last):
                for g in range(U):
                    for item in ahead(t, s, g, last):
                        take(*item)
                    weigh(t, g)
                    if g > 0 or not first:
                        pt, _, pg = earlier(t, s, g, 1, U)
                        take_attended(pt, pg)
                    if g < 3:
                        take_turned("q", t, s, g + 1)
                    elif not last:
                        take_turned("k", t + 1, 1 - s)
                        take_turned("q", t + 1, 1 - s, 0)
                    if g == 0 and not last:
                        take_turned("h", t + 1, 1 - s)

            act.wait_ge(net.in_attn1, 16 * 4)
            for name in PIECES[:2]:
                take_high(name)
            take_turned("h", 0, 0)
            for name in PIECES[2:6]:
                take_high(name)
            for item, name in zip(FIRST_ITEMS, PIECES[6:]):
                take(*item)
                take_high(name)
            take_turned("k", 0, 0)
            take_turned("q", 0, 0, 0)
            pairs(act, one)
            take_attended(NB - 1, 3)

        @block.vector
        def _(dve):
            own = Own(dve, own_dve)

            def link(instruction):
                own.wait(own.did(instruction))

            def normalise(t, s):
                if not (isinstance(t, int) and t < 2):
                    dve.wait_ge(turned, number("h", t - 2) + 1)
                dve.tensor_scalar(h_tok[:, s, :], net.x[:, t, :], net.mean_var[:, t, 0:1],
                                  net.rstd[:, bass.ds(t, 1)], ALU.subtract, ALU.mult).then_inc(normed, 1)

            def split_h(t, s):
                dve.wait_ge(turned_taken, number("h", t) + 1)
                need(dve, projected, of_six("q", t - 2, 3) + 1)
                dve.tensor_tensor(h_low[:, s].rearrange("p c t -> p (c t)"), ps[:, bank_of("h"), 0:D],
                                  h_high[:, s].bitcast(F32).rearrange("p c t -> p (c t)"),
                                  ALU.subtract).then_inc(h_low_ready, 1)

            def split_out(t, g):
                dve.wait_ge(attended_taken, U * t + g + 1)
                need(dve, output, U * t + g - 1)
                dve.tensor_tensor(out_low[:, g % 2].rearrange("p j t -> p (j t)"), ps[:, AV, :],
                                  out_high[:, g % 2].bitcast(F32).rearrange("p j t -> p (j t)"),
                                  ALU.subtract).then_inc(out_low_ready, 1)

            def rotate(what, t, s, g):
                if what == "v":
                    return
                n, at = of_five(what, t, g), slot(what, g)
                dve.wait_ge(squared, n + 1)
                if what == "k":
                    need(dve, rotated, of_five("k", t - 1, g) + 1)
                else:
                    need(dve, scaled, U * t + g - 1)
                dve.tensor_reduce(sums[:, at], square[:, square_slot(what, t, s, g)], AX.X,
                                  ALU.add).then_inc(summed, 1)
                if what == "k":
                    need(dve, turned, number("k", t - 1) + 1)
                elif g >= 2:
                    dve.wait_ge(turned, number("q", t, g - 2) + 1)
                elif not (isinstance(t, int) and t == 0):
                    dve.wait_ge(turned, number("q", t - 1, g + 2) + 1)
                cos, sin = (tables[f"{n}_{what}"] for n in ("cos", "sin"))
                half = DH // 2

                def over_heads(table):
                    return table.unsqueeze(1).broadcast_to([P, 4, table.shape[-1]])

                dve.tensor_tensor(straight[:, at], raw[:, at], over_heads(cos[:]), ALU.mult).then_inc(parts, 1)
                for to, source in ((slice(0, half), slice(half, DH)), (slice(half, DH), slice(0, half))):
                    dve.tensor_tensor(crossed[:, at, :, to], raw[:, at, :, source], over_heads(sin[:, to]),
                                      ALU.mult).then_inc(parts, 1)

            def maximum(t, g):
                dve.wait_ge(scored, U * t + g + 1)
                own.did(dve.tensor_reduce(top[:, g % 2], ps[:, SC + g % 2, :].rearrange("p (j t) -> p j t", t=P),
                                          AX.X, ALU.max))

            def shift(t, g):
                w = U * t + g
                own.wait()
                dve.wait_ge(scaled, w + 1)
                need(dve, weighed, 4 * (w - 1))
                dve.scalar_tensor_tensor(bias[:, g % 2], top[:, g % 2], -1.0, scale[:, g], ALU.mult,
                                         ALU.mult).then_inc(bias_ready, 1)

            def take_weights(t, g):
                w = U * t + g
                dve.wait_ge(turned_p, w + 1)
                need(dve, attended, w - 1)
                dve.tensor_copy(weights_t[:, g % 2], ps[:, bank_of("p", g), :]).then_inc(turned_p_taken, 1)

            def invert(t, g):
                w = U * t + g
                dve.wait_ge(weighed, 4 * (w + 1))
                need(dve, normalised, w - 1)
                dve.reciprocal(inverse[:, g % 2], total[:, g % 2]).then_inc(inverted, 1)

            def finish(t):
                dve.wait_ge(output, U * (t + 1))
                dve.tensor_tensor(net.x[:, t, :], net.x[:, t, :], ps[:, OUT, 0:D], ALU.add).then_inc(added, 1)
                dve.wait_ge(added, t + 1)
                own.did(dve.bn_stats(net.stats[:, t, :], net.x[:, t, :]))

            def one(t, s, first, last):
                for g in range(U):
                    if g == 0 and not last:
                        normalise(t + 1, 1 - s)
                    maximum(t, g)
                    if g > 0 or not first:
                        pt, _, pg = earlier(t, s, g, 1, U)
                        take_weights(pt, pg)
                    shift(t, g)
                    items = [item for item in ahead(t, s, g, last) if item[0] != "v"]
                    for item in items[:1]:
                        rotate(*item)
                    invert(t, g)
                    for item in items[1:]:
                        rotate(*item)
                    if g == 1 and not first:
                        finish(t - 1)
                    if g > 0 or not first:
                        pt, _, pg = earlier(t, s, g, 1, U)
                        split_out(pt, pg)
                    if g == 0 and not last:
                        split_h(t + 1, 1 - s)
                own.again()

            aggregate(dve, net, aggregated)
            dve.wait_ge(rstd_ready, 1)
            normalise(0, 0)
            take_low(dve, LOW_BY_DVE[0], low_dve)
            split_h(0, 0)
            for name in LOW_BY_DVE[1:4]:
                take_low(dve, name, low_dve)
            dve.wait_ge(rstd_ready, 2)
            for name, row, factor in (("q", "L1_attn_qn_w", 1.0), ("k", "L1_attn_kn_w", float(DH) ** 0.5)):
                w = net.rows[:, ROWS[row]]
                half = DH // 2
                own.did(dve.scalar_tensor_tensor(tables[f"cos_{name}"][:], w, 1.0, net.const[:, CONST["cos"]],
                                                 ALU.add, ALU.mult))
                for to, source in ((0, half), (half, 0)):
                    own.did(dve.scalar_tensor_tensor(
                        tables[f"sin_{name}"][:, to:to + half], w[:, source:source + half], 1.0,
                        net.const[:, CONST["sin"].start + to:CONST["sin"].start + to + half], ALU.add, ALU.mult))
                own.wait()
                if factor != 1.0:
                    for table in ("cos", "sin"):
                        own.did(dve.tensor_scalar(tables[f"{table}_{name}"][:], tables[f"{table}_{name}"][:],
                                                  factor, None, ALU.mult))
                    own.wait()
            dve.tensor_copy(ident_b[:], net.const[:, CONST["ident"]]).then_inc(tables_ready, 1)
            dve.tensor_copy(mask[:], net.const[:, CONST["window"]].unsqueeze(1)
                            .broadcast_to([P, 4, P])).then_inc(tables_ready, 1)
            for item in FIRST_ITEMS:
                rotate(*item)
            for name in LOW_BY_DVE[4:]:
                take_low(dve, name, low_dve)
            pairs(dve, one)
            take_weights(NB - 1, 3)
            split_out(NB - 1, 3)
            finish(NB - 1)


def cross(nc, net, sem):
    U, VW = 4, 32
    SCALE = float(XHD) ** -0.5
    ORDER = [("p", 2), ("p", 3), ("h", 0), ("p", 0), ("p", 1), ("o", 0)]
    TR, AV, PJ = 4, 6, 7

    def bank_of(what, u=0):
        return TR + ORDER.index((what, u)) % 2

    def number(what, t, u=0):
        if what == "h":
            return 0 if isinstance(t, int) and t == 0 else 5 * t - 4
        return 5 * t + 2 + u - (isinstance(t, int) and t == NB - 1)

    def begun(t, n):
        return not (isinstance(t, int) and t < n)

    with ExitStack() as ctx:
        def sb(name, shape, dt=F32):
            return ctx.enter_context(nc.sbuf_tensor(name, shape, dt))

        h_tok, h_t = sb("cr_h_tok", [P, 2, D]), sb("cr_h_t", [P, KC, P])
        context = sb("cr_context", [CTX, 2, P])
        qk, kbd = sb("cr_qk", [P, 2, 2, KC, P]), sb("cr_keys_diagonal", [P, 2, KC, 2, P])
        values = sb("cr_values", [P, 2, XHEADS, VW])
        weights, weights_t = sb("cr_weights", [P, U, BANK]), sb("cr_weights_t", [P, U, BANK])
        top, out_t = sb("cr_top", [P, 2, 4]), sb("cr_out_t", [P, BANK])
        rsum, out = sb("cr_rsum", [P, XHEADS]), sb("cr_out", [P, KC, U, 2, XHD])
        out_f = sb("cr_out_f", [P, KC, P])
        scratch = sb("cr_scratch", [P, NB])
        mask, ident_b = sb("cr_mask", [P, 4, P], BF16), sb("cr_ident", [P, P], BF16)
        ps = ctx.enter_context(nc.psum_tensor("cr_psum", [P, 8, BANK], F32))

        aggregated = sem("cr_aggregated")
        rstd_ready = sem("cr_rstd")
        tables_ready = sem("cr_tables")
        values_set = sem("cr_values_set")
        context_in = [sem(f"cr_context_in{s}") for s in range(2)]
        normed = sem("cr_normed")
        turned = sem("cr_turned")
        taken = sem("cr_taken")
        projected = sem("cr_projected")
        proj_taken = sem("cr_proj_taken")
        spread = sem("cr_spread")
        scored = sem("cr_scored")
        shifted = sem("cr_shifted")
        weighed = sem("cr_weighed")
        attended = sem("cr_attended")
        out_taken = sem("cr_out_taken")
        out_turned = sem("cr_out_turned")
        out_ready = sem("cr_out_ready")
        out_f_turned = sem("cr_out_f_turned")
        out_f_taken = sem("cr_out_f_taken")
        result = sem("cr_result")
        added = sem("cr_added")
        own_dve, own_pool = sem("cr_own_dve"), sem("cr_own_pool")
        block = ctx.enter_context(nc.Block("cross"))

        @block.sync
        def _(sp):
            def one(t, s, first, last):
                need(sp, projected, 2 * (t - 1))
                sp.dma_start(context[:, s], net.dram["ctx_t"][t]).then_inc(context_in[s], 16)

            pairs(sp, one)

        @block.gpsimd
        def _(pool):
            own = Own(pool, own_pool)
            layer_norm_scale(pool, own, net, scratch, aggregated, rstd_ready, 1)
            pool.memset(values[:], 0.0).then_inc(values_set, 1)
            pool.wait_ge(values_set, 1)
            pool.memset(values[:, :, :, XHD:XHD + 1], 1.0).then_inc(values_set, 1)

            def one(t, s, first, last):
                pool.wait_ge(proj_taken, 2 * t + 1)
                need(pool, scored, U * (t - 1))
                for c in range(KC):
                    pool.tensor_tensor(kbd[:, s, c], qk[:, s, 1, c:c + 1, :].broadcast_to([P, 2, P]),
                                       wide(net.const[:, CONST["half"]], [P, 2, P]), ALU.mult).then_inc(spread, 1)
                split_ffn1(t)
                own.again()

            def split_ffn1(t):
                piece = bass.ds(t * P, P)
                matrices = [[tile.rearrange("p c n -> p (c n)")[:, piece] for tile in of] for of in (
                    (net.gate1_high, net.gate1_low, net.gate1), (net.up1_high, net.up1_low, net.up1),
                    (net.down1_high, net.down1_low, net.down1))]
                for hi, _, w in matrices:
                    own.did(pool.tensor_tensor(hi, w, net.ones[:], ALU.mult))
                own.wait()
                for hi, lo, w in matrices:
                    own.did(pool.tensor_tensor(lo, w, hi.bitcast(F32), ALU.subtract))

            pool.wait_ge(net.in_late, 16 * 6)
            pairs(pool, one)

        @block.tensor
        def _(pe):
            ident = net.const[:, CONST["ident"]]

            def turn_h(t, s):
                pe.wait_ge(normed, t + 1)
                if begun(t, 2):
                    pe.wait_ge(taken, number("p", t - 2, 2) + 1)
                for c in range(KC):
                    mm = pe.transpose(ps[:, bank_of("h"), c * P:c * P + P], h_tok[:, s, c * P:c * P + P], ident)
                mm.then_inc(turned, 1)

            def project_qk(t, s):
                pe.wait_ge(context_in[s], (t - s) * 8 + 16)
                need(pe, added, t - 2)
                for oc in range(KC):
                    pe.matmul(ps[:, PJ, D + oc * P:D + oc * P + P], net.xwkv[:, oc * P:oc * P + P],
                              context[:, s, :], start=True, stop=True)
                pe.wait_ge(taken, number("h", t) + 1)
                for oc in range(KC):
                    for c in range(KC):
                        mm = pe.matmul(ps[:, PJ, oc * P:oc * P + P], net.xwq[:, c, oc * P:oc * P + P], h_t[:, c, :],
                                       start=(c == 0), stop=(c == KC - 1))
                mm.then_inc(projected, 1)

            def project_v(t, s):
                pe.wait_ge(proj_taken, 2 * t + 1)
                pe.matmul(ps[:, PJ, 0:D], context[:, s, :], net.xwkv[:, D:2 * D],
                          start=True, stop=True).then_inc(projected, 1)

            def scores(t, s, u):
                if u == 0:
                    pe.wait_ge(spread, KC * (t + 1))
                need(pe, shifted, U * (t - 1) + u + 1)
                g = 32 * u
                pe.matmul(ps[:, u, :], ident_b[:], mask.rearrange("p j t -> p (j t)"), start=True, stop=False,
                          skip_group_check=True)
                for c in range(KC):
                    mm = pe.matmul(ps[:, u, c * D:c * D + D], qk[g:g + 32, s, 0, c, :], kbd[g:g + 32, s, c, :, :],
                                   start=False, stop=True, skip_group_check=True)
                mm.then_inc(scored, 1)

            def turn_weights(t, s, u):
                pe.wait_ge(weighed, U * t + u + 1)
                if u == 3:
                    need(pe, out_ready, KC * t)
                elif u == 2:
                    pe.wait_ge(taken, number("p", t, 1) + 1)
                elif u == 0:
                    need(pe, taken, number("p", t - 1, 3) + 1)
                else:
                    pe.wait_ge(taken, number("p", t, 0))
                for j in range(4):
                    mm = pe.transpose(ps[:, bank_of("p", u), j * P:j * P + P], weights[:, u, j * P:j * P + P], ident)
                mm.then_inc(turned, 1)

            def attend(t, s, u):
                pe.wait_ge(taken, number("p", t, u) + 1)
                if u == 0:
                    pe.wait_ge(proj_taken, 2 * t + 2)
                    need(pe, out_taken, t)
                for i in range(4):
                    c, j = i // 2, i % 2
                    mm = pe.matmul(ps[32 * i:32 * i + VW, AV, u * P:u * P + P], values[:, s, 8 * c + 2 * u + j, :],
                                   weights_t[:, u, i * P:i * P + P], start=True, stop=True)
                mm.then_inc(attended, 1)

            def turn_out(t):
                pe.wait_ge(out_taken, t + 1)
                pe.wait_ge(taken, number("p", t + 1, 0) + 1 if not (isinstance(t, int) and t == NB - 1)
                           else number("p", t, 3) + 1)
                for u in range(U):
                    mm = pe.transpose(ps[:, bank_of("o"), u * P:u * P + P], out_t[:, u * P:u * P + P], ident)
                mm.then_inc(out_turned, 1)

            def turn_out_f(t):
                pe.wait_ge(out_ready, KC * (t + 1))
                pe.wait_ge(proj_taken, 2 * (t + 3) if not (isinstance(t, int) and t >= NB - 2) else 2 * NB)
                if isinstance(t, int) and t == NB - 1:
                    pe.wait_ge(added, t)
                for c in range(KC):
                    mm = pe.transpose(ps[:, PJ, c * P:c * P + P], out.rearrange("p c u j d -> p c (u j d)")[:, c, :], ident)
                mm.then_inc(out_f_turned, 1)

            def project_out(t):
                pe.wait_ge(out_f_taken, t + 1)
                for c in range(KC):
                    mm = pe.matmul(ps[:, PJ, 0:D], out_f[:, c, :], net.xwout[:, c, :], start=(c == 0), stop=(c == KC - 1))
                mm.then_inc(result, 1)

            def one(t, s, first, last):
                for u in range(U):
                    scores(t, s, u)
                    if u >= 2 or not first:
                        turn_weights(*earlier(t, s, u, 2, U))
                    if u == 1 and not last:
                        turn_h(t + 1, 1 - s)
                    if u == 3 and not first:
                        turn_out(t - 1)
                    if u >= 3 or not first:
                        attend(*earlier(t, s, u, 3, U))
                    if u == 0 and begun(t, 2):
                        turn_out_f(t - 2)
                    if u == 1 and begun(t, 2):
                        project_out(t - 2)
                    if u == 2 and not last:
                        project_qk(t + 1, 1 - s)
                    if u == 3 and not last:
                        project_v(t + 1, 1 - s)

            pe.wait_ge(net.in_late, 16 * 6)
            turn_h(0, 0)
            project_qk(0, 0)
            project_v(0, 0)
            pe.wait_ge(tables_ready, 2)
            pairs(pe, one)
            t, s = NB - 1, 1
            turn_weights(t, s, 2)
            attend(t, s, 1)
            turn_out_f(t - 1)
            turn_weights(t, s, 3)
            attend(t, s, 2)
            project_out(t - 1)
            attend(t, s, 3)
            turn_out(t)
            turn_out_f(t)
            project_out(t)

        @block.scalar
        def _(act):
            def take_h(t):
                act.wait_ge(turned, number("h", t) + 1)
                need(act, projected, 2 * t - 1)
                act.activation(h_t.rearrange("p c t -> p (c t)"), ps[:, bank_of("h"), 0:D],
                               ACT.Copy).then_inc(taken, 1)

            def take_projected(t, s, n):
                act.wait_ge(projected, 2 * t + n + 1)
                if n == 0:
                    need(act, scored, U * (t - 1))
                    need(act, spread, KC * (t - 1))
                    act.activation(qk[:, s].rearrange("p m c t -> p (m c t)"), ps[:, PJ, :],
                                   ACT.Copy).then_inc(proj_taken, 1)
                else:
                    need(act, attended, U * (t - 1))
                    act.activation(values[:, s, :, 0:XHD], ps[:, PJ, 0:D].rearrange("p (h d) -> p h d", d=XHD),
                                   ACT.Copy).then_inc(proj_taken, 1)

            def weigh(t, u):
                act.wait_ge(shifted, U * t + u + 1)
                act.activation(weights[:, u], weights[:, u], ACT.Exp, scale=SCALE).then_inc(weighed, 1)

            def take_weights(t, s, u):
                act.wait_ge(turned, number("p", t, u) + 1)
                need(act, attended, U * (t - 1) + u + 1)
                act.activation(weights_t[:, u], ps[:, bank_of("p", u), :], ACT.Copy).then_inc(taken, 1)

            def take_out(t):
                act.wait_ge(attended, U * (t + 1))
                need(act, out_turned, t)
                act.activation(out_t[:], ps[:, AV, :], ACT.Copy).then_inc(out_taken, 1)

            def take_out_f(t):
                act.wait_ge(out_f_turned, t + 1)
                act.activation(out_f.rearrange("p c t -> p (c t)"), ps[:, PJ, 0:D],
                               ACT.Copy).then_inc(out_f_taken, 1)

            def one(t, s, first, last):
                for u in range(U):
                    if u >= 2 or not first:
                        take_weights(*earlier(t, s, u, 2, U))
                    weigh(t, u)
                    if u == 1 and not last:
                        take_h(t + 1)
                    if u == 0 and begun(t, 2):
                        take_out_f(t - 2)
                    if u == 2 and not first:
                        take_out(t - 1)
                    if u == 2 and not last:
                        take_projected(t + 1, 1 - s, 0)
                    if u == 3 and not last:
                        take_projected(t + 1, 1 - s, 1)

            take_h(0)
            take_projected(0, 0, 0)
            act.wait_ge(values_set, 2)
            take_projected(0, 0, 1)
            pairs(act, one)
            t, s = NB - 1, 1
            take_weights(t, s, 2)
            take_out_f(t - 1)
            take_weights(t, s, 3)
            take_out(t)
            take_out_f(t)

        @block.vector
        def _(dve):
            own = Own(dve, own_dve)

            def link(instruction):
                own.wait(own.did(instruction))

            def normalise(t, s):
                if begun(t, 2):
                    dve.wait_ge(turned, number("h", t - 2) + 1)
                dve.tensor_scalar(h_tok[:, s, :], net.x[:, t, :], net.mean_var[:, t, 0:1],
                                  net.rstd[:, bass.ds(t, 1)], ALU.subtract, ALU.mult).then_inc(normed, 1)

            def shift(t, s, u):
                dve.wait_ge(scored, U * t + u + 1)
                rows = ps[:, u, :].rearrange("p (j t) -> p j t", t=P)
                link(dve.tensor_reduce(top[:, u % 2, :], rows, AX.X, ALU.max))
                if begun(t, 1):
                    dve.wait_ge(turned, number("p", t - 1, u) + 1)
                dve.tensor_tensor(weights[:, u].rearrange("p (j t) -> p j t", t=P), rows,
                                  wide(top[:, u % 2, :], [P, 4, P]), ALU.subtract).then_inc(shifted, 1)

            def divide(t):
                dve.wait_ge(out_turned, t + 1)
                heads = ps[:, bank_of("o"), :].rearrange("p (h v) -> p h v", v=VW)
                link(dve.reciprocal(rsum[:], heads[:, :, XHD]))
                need(dve, out_f_turned, t)
                by_unit = ps[:, bank_of("o"), :].rearrange("p (u c j v) -> p c u j v", u=U, c=KC, v=VW)
                shares = rsum.rearrange("p (u c j) -> p c u j", u=U, c=KC)
                for c in range(KC):
                    dve.tensor_tensor(out[:, c], by_unit[:, c, :, :, 0:XHD], wide(shares[:, c], [P, U, 2, XHD]),
                                      ALU.mult).then_inc(out_ready, 1)

            def finish(t):
                dve.wait_ge(result, t + 1)
                dve.tensor_tensor(net.x[:, t, :], net.x[:, t, :], ps[:, PJ, 0:D], ALU.add).then_inc(added, 1)
                dve.wait_ge(added, t + 1)
                own.did(dve.bn_stats(net.stats[:, t, :], net.x[:, t, :]))

            def one(t, s, first, last):
                for u in range(U):
                    shift(t, s, u)
                    if u == 0 and not last:
                        normalise(t + 1, 1 - s)
                    if u == 1 and begun(t, 2):
                        finish(t - 2)
                    if u == 3 and not first:
                        divide(t - 1)
                own.again()

            aggregate(dve, net, aggregated)
            dve.wait_ge(rstd_ready, 1)
            normalise(0, 0)
            dve.tensor_copy(ident_b[:], net.const[:, CONST["ident"]]).then_inc(tables_ready, 1)
            dve.tensor_copy(mask[:], net.const[:, CONST["causal"]].unsqueeze(1)
                            .broadcast_to([P, 4, P])).then_inc(tables_ready, 1)
            dve.wait_ge(rstd_ready, 2)
            pairs(dve, one)
            finish(NB - 2)
            divide(NB - 1)
            finish(NB - 1)


def silu_ffn(nc, net, sem):
    with ExitStack() as ctx:
        def sb(name, shape, dt=F32):
            return ctx.enter_context(nc.sbuf_tensor(name, shape, dt))

        h_tok = sb("ff_h_tok", [P, GB, D])
        h_high, h_low = sb("ff_h_high", [P, KC, GB * P], F32R), sb("ff_h_low", [P, KC, GB * P], F32R)
        gated = sb("ff_gated", [P, 2, BANK])
        high, low = sb("ff_hidden_high", [P, 2, BANK], F32R), sb("ff_hidden_low", [P, 2, BANK], F32R)
        scratch = sb("ff_scratch", [P, NB])
        ps = ctx.enter_context(nc.psum_tensor("ff_psum", [P, 8, BANK], F32))
        DOWN, TURN = 4, 6

        aggregated = sem("ff_aggregated")
        rstd_ready = sem("ff_rstd")
        normed = sem("ff_normed")
        turned = sem("ff_turned")
        h_split = sem("ff_h_split")
        gate_full, up_full = sem("ff_gate_full"), sem("ff_up_full")
        silu_done = sem("ff_silu_done")
        hidden_ready = sem("ff_hidden_ready")
        high_ready = sem("ff_high_ready")
        low_ready = sem("ff_low_ready")
        down_done = sem("ff_down_done")
        added = sem("ff_added")
        stored = sem("ff_stored")
        block = ctx.enter_context(nc.Block("silu_ffn"))

        @block.sync
        def _(sp):
            with sp.Fori(0, NG) as g:
                sp.wait_ge(added, GB * (g + 1))
                sp.dma_start(net.dram["out"].rearrange("(g j) t d -> g t j d", j=GB)[g],
                             net.x.rearrange("p (g j) d -> p g j d", j=GB)[:, g]).then_inc(stored, 16)
            sp.wait_ge(stored, 16 * NG)

        @block.gpsimd
        def _(pool):
            own = Own(pool, net.own_last)
            layer_norm_scale(pool, own, net, scratch, aggregated, rstd_ready, GB)

        @block.tensor
        def _(pe):
            ident = net.const[:, CONST["ident"]]

            def turn(g):
                pe.wait_ge(normed, g + 1)
                need(pe, h_split, 2 * KC * g)
                for c in range(KC):
                    for j in range(GB):
                        mm = pe.transpose(ps[:, TURN + c, j * P:j * P + P], h_tok[:, j, c * P:c * P + P], ident)
                mm.then_inc(turned, 1)

            def gate_up(g, q):
                if q == 0:
                    pe.wait_ge(h_split, 2 * KC * g + KC)
                need(pe, hidden_ready, HC * g + q - 1)
                for m, (hi, lo, full) in enumerate(((net.gate1_high, net.gate1_low, gate_full),
                                                    (net.up1_high, net.up1_low, up_full))):
                    for n, (w, h) in enumerate(((hi, h_high), (lo, h_high), (hi, h_low))):
                        if q == 0 and n == 2:
                            pe.wait_ge(h_split, 2 * KC * (g + 1))
                        for c in range(KC):
                            mm = pe.matmul(ps[:, 2 * (q % 2) + m, :], w[:, c, q * P:q * P + P], h[:, c, :],
                                           start=(n == 0 and c == 0), stop=(n == 2 and c == KC - 1))
                    mm.then_inc(full, 1)

            def down(g, q):
                pe.wait_ge(high_ready, HC * g + q + 1)
                if q == 0:
                    need(pe, added, GB * g)
                for n, (h, w) in enumerate(((high, net.down1_high), (high, net.down1_low),
                                            (low, net.down1_high))):
                    if n == 2:
                        pe.wait_ge(low_ready, HC * g + q + 1)
                    for j in range(GB):
                        mm = pe.matmul(ps[:, DOWN + j // 2, (j % 2) * D:(j % 2) * D + D],
                                       h[:, q % 2, j * P:j * P + P], w[:, q, :],
                                       start=(q == 0 and n == 0 and j % 2 == 0),
                                       stop=(q == HC - 1 and n == 2), skip_group_check=True)
                mm.then_inc(down_done, 1)

            def one(g, first, last):
                for q in range(HC):
                    gate_up(g, q)
                    if q > 0:
                        down(g, q - 1)
                if not last:
                    turn(g + 1)
                down(g, HC - 1)

            pe.wait_ge(net.in_late, 16 * 6)
            turn(0)
            rounds(pe, one)

        @block.scalar
        def _(act):
            def take(g):
                act.wait_ge(turned, g + 1)
                need(act, up_full, HC * g)
                for c in range(KC):
                    act.activation(h_high[:, c, :], ps[:, TURN + c, :], ACT.Copy).then_inc(h_split, 1)

            def one(g, first, last):
                for q in range(HC):
                    act.wait_ge(gate_full, HC * g + q + 1)
                    need(act, low_ready, HC * g + q - 1)
                    act.activation(gated[:, q % 2, :], ps[:, 2 * (q % 2), :], ACT.Silu).then_inc(silu_done, 1)
                    act.wait_ge(hidden_ready, HC * g + q + 1)
                    need(act, down_done, HC * g + q - 1)
                    act.activation(high[:, q % 2, :], gated[:, q % 2, :], ACT.Copy).then_inc(high_ready, 1)
                if not last:
                    take(g + 1)

            take(0)
            rounds(act, one)

        @block.vector
        def _(dve):
            def normalise(g):
                need(dve, turned, g)
                for j in range(GB):
                    b = GB * g + j
                    h = dve.tensor_scalar(h_tok[:, j, :], net.x[:, b, :], net.mean_var[:, b, 0:1],
                                          net.rstd[:, bass.ds(b, 1)], ALU.subtract, ALU.mult)
                h.then_inc(normed, 1)

            def finish(g):
                dve.wait_ge(down_done, HC * (g + 1))
                for j in range(GB):
                    b = GB * g + j
                    dve.tensor_tensor(net.x[:, b, :], net.x[:, b, :],
                                      ps[:, DOWN + j // 2, (j % 2) * D:(j % 2) * D + D], ALU.add).then_inc(added, 1)

            def one(g, first, last):
                dve.wait_ge(h_split, 2 * KC * g + KC)
                need(dve, up_full, HC * g)
                for c in range(KC):
                    dve.tensor_tensor(h_low[:, c, :], ps[:, TURN + c, :], h_high[:, c, :].bitcast(F32),
                                      ALU.subtract).then_inc(h_split, 1)
                for q in range(HC):
                    dve.wait_ge(silu_done, HC * g + q + 1)
                    dve.wait_ge(up_full, HC * g + q + 1)
                    dve.tensor_tensor(gated[:, q % 2, :], gated[:, q % 2, :], ps[:, 2 * (q % 2) + 1, :],
                                      ALU.mult).then_inc(hidden_ready, 1)
                    if q == 0 and not first:
                        finish(g - 1)
                    dve.wait_ge(high_ready, HC * g + q + 1)
                    need(dve, down_done, HC * g + q - 1)
                    dve.tensor_tensor(low[:, q % 2, :], gated[:, q % 2, :], high[:, q % 2, :].bitcast(F32),
                                      ALU.subtract).then_inc(low_ready, 1)
                    if q == 2 and not last:
                        normalise(g + 1)

            aggregate(dve, net, aggregated)
            dve.wait_ge(rstd_ready, 1)
            normalise(0)
            dve.wait_ge(rstd_ready, 2)
            rounds(dve, one)
            finish(NG - 1)


def decoder(nc, dram):
    with ExitStack() as ctx:
        def sb(name, shape, dt=F32):
            return ctx.enter_context(nc.sbuf_tensor(name, shape, dt))

        def placed(name, shape):
            net.places[name] = nc.sbuf_base
            return sb(name, shape)

        def sem(name):
            return ctx.enter_context(nc.semaphore(name))

        net = Net()
        net.dram, net.places = dram, {}
        net.fvec, net.rows, net.const = sb("fvec", [P, KC * len(FVEC)]), sb("rows", [P, ROWS_N]), sb("const", [P, CONST_N])
        net.x, net.ctx = sb("x", [P, NB, D]), sb("ctx", [P, NB, CTX])
        net.stats = sb("stats", [P, NB, 6])
        net.mean_var, net.rstd = sb("mean_var", [P, NB, 2]), sb("rstd", [P, NB])
        net.ones, net.half = sb("ones", [P, P]), sb("minus_half", [P, NB * EXPERTS])
        net.router_w = sb("router_w", [P, KC, EXPERTS])
        net.wq, net.wk = placed("wq", [P, KC, HEADS * DH]), placed("wk", [P, KC, KVH * DH])
        net.wv, net.wo = placed("wv", [P, KC, KVH * DH]), placed("wo", [P, HEADS, D])
        net.in_small, net.in_rwkv, net.in_ctx = sem("in_small"), sem("in_rwkv"), sem("in_ctx")
        net.in_ffn0, net.in_attn1, net.in_late = sem("in_ffn0"), sem("in_attn1"), sem("in_late")
        net.in_x = [sem(f"in_x{g}") for g in range(NG)]
        with ExitStack() as early:
            def early_sb(name, shape):
                net.places[name] = nc.sbuf_base
                return early.enter_context(nc.sbuf_tensor(name, shape, F32))

            net.gate0, net.up0 = early_sb("gate0", [P, KC, HIDDEN]), early_sb("up0", [P, KC, HIDDEN])
            net.egate, net.eup = early_sb("egate", [P, KC, HIDDEN]), early_sb("eup", [P, KC, HIDDEN])
            net.down0, net.edown = early_sb("down0", [P, HC, D]), early_sb("edown", [P, EXPERTS, D])
            with nc.sbuf_tensor("rwkv_w", [P, 4, KC, D], F32) as net.rwkv_w:
                rwkv(nc, net, sem)
            gqa(nc, net, sem)
            experts(nc, net, sem)
        net.xwq, net.xwout = sb("xwq", [P, KC, D]), sb("xwout", [P, KC, D])
        net.xwkv, net.own_last = sb("xwkv", [CTX, 2 * D]), sem("own_last")
        net.gate1, net.up1 = placed("gate1", [P, KC, HIDDEN]), placed("up1", [P, KC, HIDDEN])
        net.down1 = placed("down1", [P, HC, D])
        windowed(nc, net, sem)
        net.gate1_high, net.up1_high = sb("gate1_high", [P, KC, HIDDEN], F32R), sb("up1_high", [P, KC, HIDDEN], F32R)
        net.down1_high = sb("down1_high", [P, HC, D], F32R)
        net.gate1_low, net.up1_low, net.down1_low = (
            in_place(nc, f"{n}_low", net.places[n], w.shape)
            for n, w in (("gate1", net.gate1), ("up1", net.up1), ("down1", net.down1)))
        cross(nc, net, sem)
        silu_ffn(nc, net, sem)


def constants():
    const = np.zeros((P, CONST_N), np.float32)
    p = np.arange(P)
    const[:, CONST["ident"]] = np.eye(P)
    inv_freq = (1.0 / np.float32(THETA) ** (np.arange(0, DH, 2, dtype=np.float32) / np.float32(DH))).astype(np.float32)
    angle = p[:, None].astype(np.float32) * inv_freq[None, :]
    const[:, CONST["cos"]] = np.tile(np.cos(angle.astype(np.float64)), 2)
    const[:, CONST["sin"]] = np.concatenate([-np.sin(angle.astype(np.float64)), np.sin(angle.astype(np.float64))], 1)
    distance = p[:, None] - p[None, :]
    const[:, CONST["window"]] = np.where((distance >= 0) & (distance <= WINDOW), 0.0, FAR)
    const[:, CONST["causal"]] = np.where(distance >= 0, 0.0, FAR)
    const[:, CONST["odd"]] = (p[:, None] // HD) % 2
    const[:, CONST["half"]] = (p[:, None] // XHD) % 2 == np.arange(2)[None, :]
    e = np.arange(EXPERTS)
    const[:, CONST["before"]] = (e[None, :] < e[:, None]).reshape(1, -1)
    return const


def laid_out(inputs):
    a = {n: np.asarray(v) for n, v in inputs.items()}

    def chunks(w):
        return w.reshape(-1, P, w.shape[-1]).transpose(1, 0, 2)

    ctx = a["ctx_512"]
    keys = ctx.reshape(NB, P, KV_HEADS, HD).transpose(0, 3, 2, 1).reshape(NB, 1, HD, KV_HEADS * P)
    return {
        "x": a["x"], "ctx": ctx,
        "ctx_keys": np.broadcast_to(keys, (NB, P // HD, HD, KV_HEADS * P)).reshape(NB, P, -1),
        "ctx_t": ctx.transpose(0, 2, 1),
        "fvec": np.stack([a[n].reshape(KC, P) for n in FVEC]).transpose(2, 0, 1).reshape(P, -1),
        "rows": np.broadcast_to(np.concatenate([a[n] for n in ROWS]), (P, ROWS_N)),
        "const": constants(),
        "rwkv_w": np.stack([chunks(a[f"L0_attn_W{n}"].T) for n in "kvro"], 1),
        "router_w": chunks(a["L0_ffn_router_w"]),
        "gate0": chunks(a["L0_ffn_w_gate"]), "up0": chunks(a["L0_ffn_w_up"]), "down0": chunks(a["L0_ffn_w_down"]),
        "egate": chunks(a["L0_ffn_we_gate"].transpose(1, 0, 2).reshape(D, -1)),
        "eup": chunks(a["L0_ffn_we_up"].transpose(1, 0, 2).reshape(D, -1)),
        "edown": a["L0_ffn_we_down"].transpose(1, 0, 2),
        "wq": chunks(a["L1_attn_Wq"].T), "wk": chunks(a["L1_attn_Wk"].T), "wv": chunks(a["L1_attn_Wv"].T),
        "wo": chunks(a["L1_attn_Wo"].T),
        "xwq": chunks(a["L1_xattn_Wq"].T), "xwkv": a["L1_xattn_Wkv_expand"].T, "xwout": chunks(a["L1_xattn_Wout"].T),
        "gate1": chunks(a["L1_ffn_w_gate"].T), "up1": chunks(a["L1_ffn_w_up"].T), "down1": chunks(a["L1_ffn_w_down"].T),
    }


def kernel(**inputs):
    import concourse.bacc as bacc
    from concourse.bass_utils import run_bass_kernel_spmd

    nc = bacc.Bacc("TRN2", target_bir_lowering=False, num_devices=1)
    arrays, dram = {}, {}
    for name, a in laid_out(inputs).items():
        a = np.ascontiguousarray(a)
        arrays[f"in_{name}_dram"] = a
        dram[name] = nc.dram_tensor(f"in_{name}_dram", a.shape, mybir.dt.from_np(a.dtype), kind="ExternalInput").ap()
    dram["out"] = nc.dram_tensor("out_0_dram", (NB, P, D), F32, kind="ExternalOutput").ap()
    decoder(nc, dram)
    r = run_bass_kernel_spmd(nc, [arrays], core_ids=[0])
    return r.results[0]["out_0_dram"]
```
